# Optimizing a Trainium2 kernel written in Bass

```python
import numpy as np
import jax
import jax.numpy as jnp

def _softmax(x, axis=-1):
    return jax.nn.softmax(x, axis=axis)

def _gelu(x):
    return jax.nn.gelu(x, approximate=True)

def _silu(x):
    return jax.nn.silu(x)

def _sigmoid(x):
    return jax.nn.sigmoid(x)

def _layernorm(x, axis=-1, eps=1e-05):
    m = jnp.mean(x, axis=axis, keepdims=True)
    v = jnp.var(x, axis=axis, keepdims=True)
    return (x - m) / jnp.sqrt(v + eps)

def _scatter_add(tgt, idx, src, axis=0):
    return tgt.at[idx].add(src)

def _segment_sum(src, seg, n):
    return jax.ops.segment_sum(src, seg, n)
kernel_name = 'mk_decoder_preln_d1_seqx_r8_e365d6'

def setup_inputs(seed: int=0):
    np.random.seed(seed)
    _w = jnp.asarray

    def _rec_inputs():
        import jax
        import jax.numpy as jnp
        _rk = jax.random.key(seed)
        x = -0.0005207 + 1.001 * jax.random.normal(jax.random.fold_in(_rk, 1), (8, 128, 512), jnp.float32)
        _lenS = 128 - jax.random.randint(jax.random.fold_in(_rk, 7), (8,), 0, max(1, 128 // 4) + 1, jnp.int32)
        _lenS2 = 128 - jax.random.randint(jax.random.fold_in(_rk, 8), (8,), 0, max(1, 128 // 4) + 1, jnp.int32)
        _ctx_4096P = jax.random.normal(jax.random.fold_in(_rk, 11), (8, 16, 512), jnp.float32)
        _ctx_4096c = jax.random.dirichlet(jax.random.fold_in(_rk, 511), 0.3 * jnp.ones((16,), jnp.float32), (8, 128))
        _ctx_4096t = jnp.einsum('bsk,bkd->bsd', _ctx_4096c, _ctx_4096P)
        _ctx_4096t = _ctx_4096t * jax.lax.rsqrt(jnp.mean(jnp.square(_ctx_4096t)) + 1e-12) * 0.953939
        ctx_4096 = -0.00010331 + 0.999899 * (_ctx_4096t + 0.3 * jax.random.normal(jax.random.fold_in(_rk, 611), (8, 128, 512), jnp.float32))
        return (x, ctx_4096)
    x, ctx_4096 = _rec_inputs()

    def _L0_attn_setup():
        import math
        import jax, jax.numpy as jnp
        import numpy as np
        B, T, E = (2, 256, 512)
        H, HKV = (32, 8)
        DH = E // H
        G = H // HKV
        ROPE_THETA = 500000.0
        ROPE_FACTOR = 32.0
        HI_FREQ_FACTOR = 4.0
        LO_FREQ_FACTOR = 1.0
        ORIG_CTX = 1024

        def _rope_cos_sin(t_len):
            inv_freq = 1.0 / ROPE_THETA ** (jnp.arange(0, DH, 2, dtype=jnp.float32) / DH)
            wavelen = 2.0 * math.pi / inv_freq
            cut_lo = ORIG_CTX / HI_FREQ_FACTOR
            cut_hi = ORIG_CTX / LO_FREQ_FACTOR
            inv_freq = jnp.where(wavelen > cut_hi, inv_freq / ROPE_FACTOR, inv_freq)
            smooth = (ORIG_CTX / wavelen - LO_FREQ_FACTOR) / (HI_FREQ_FACTOR - LO_FREQ_FACTOR)
            smoothed = (1.0 - smooth) * inv_freq / ROPE_FACTOR + smooth * inv_freq
            is_medium = ~(wavelen < cut_hi) & ~(wavelen > cut_lo)
            inv_freq = jnp.where(is_medium, smoothed, inv_freq)
            pos = jnp.arange(t_len, dtype=jnp.float32)
            freqs = pos[:, None] * inv_freq[None, :]
            emb = jnp.concatenate([freqs, freqs], axis=-1)
            return (jnp.cos(emb), jnp.sin(emb))

        def _rotate_half(x):
            x1, x2 = jnp.split(x, 2, axis=-1)
            return jnp.concatenate([-x2, x1], axis=-1)
        key = jax.random.key(seed)
        kx, kq, kk, kv, ko = jax.random.split(key, 5)
        w = lambda k, shape: jax.random.normal(k, shape, jnp.float32) * 0.02
        return {'x': jax.random.normal(kx, (B, T, E), jnp.float32), 'Wq': w(kq, (E, E)), 'Wk': w(kk, (HKV * DH, E)), 'Wv': w(kv, (HKV * DH, E)), 'Wo': w(ko, (E, E))}
    _L0_attn_all = _L0_attn_setup()
    _L0_attn_in = {k: v for k, v in _L0_attn_all.items() if k in ('Wq', 'Wk', 'Wv', 'Wo')}
    del _L0_attn_all

    def _L0_xattn_setup():
        import jax, jax.numpy as jnp
        import numpy as np
        import math
        HIDDEN = 512
        N_HEADS = 32
        HEAD_DIM = 128
        N_KV_HEADS = 4
        N_GROUPS = N_HEADS // N_KV_HEADS
        key = jax.random.key(seed)
        ks = jax.random.split(key, 6)
        B, NL, S = (8, 64, 512)
        latents = jax.random.normal(ks[0], (B, NL, HIDDEN), dtype=jnp.float32)
        context = jax.random.normal(ks[1], (B, S, HIDDEN), dtype=jnp.float32)
        scale = 1.0 / math.sqrt(HIDDEN)
        Wq = jax.random.normal(ks[2], (HIDDEN, N_HEADS * HEAD_DIM), dtype=jnp.float32) * scale
        Wk = jax.random.normal(ks[3], (HIDDEN, N_KV_HEADS * HEAD_DIM), dtype=jnp.float32) * scale
        Wv = jax.random.normal(ks[4], (HIDDEN, N_KV_HEADS * HEAD_DIM), dtype=jnp.float32) * scale
        Wo = jax.random.normal(ks[5], (N_HEADS * HEAD_DIM, HIDDEN), dtype=jnp.float32) * scale
        return {'latents': latents, 'context': context, 'Wq': Wq, 'Wk': Wk, 'Wv': Wv, 'Wo': Wo}
    _L0_xattn_all = _L0_xattn_setup()
    _L0_xattn_in = {k: v for k, v in _L0_xattn_all.items() if k in ('Wq', 'Wk', 'Wv', 'Wo')}
    del _L0_xattn_all

    def _L0_ffn_setup():
        import jax, jax.numpy as jnp
        import numpy as np
        HID, INT, LAT, NE, K = (512, 1024, 256, 8, 2)
        LN_EPS = 1e-05

        def _layernorm(x, gamma, beta):
            mu = jnp.mean(x, axis=-1, keepdims=True)
            var = jnp.var(x, axis=-1, keepdims=True)
            return (x - mu) * jax.lax.rsqrt(var + LN_EPS) * gamma + beta
        key = jax.random.key(seed)
        ks = jax.random.split(key, 8)
        s = lambda d: 1.0 / np.sqrt(d)
        return {'hidden_states': jax.random.normal(ks[0], (4, 256, HID), jnp.float32), 'gate_w': jax.random.normal(ks[1], (HID, NE), jnp.float32) * s(HID), 'up_w': jax.random.normal(ks[2], (HID, INT), jnp.float32) * s(HID), 'down_w': jax.random.normal(ks[3], (INT, HID), jnp.float32) * s(INT), 'fc1_w': jax.random.normal(ks[4], (HID, LAT), jnp.float32) * s(HID), 'fc2_w': jax.random.normal(ks[5], (LAT, HID), jnp.float32) * s(LAT), 'expert_w': jax.random.normal(ks[6], (LAT, LAT), jnp.float32), 'ln_gamma': jnp.ones((HID,), jnp.float32), 'ln_beta': jnp.zeros((HID,), jnp.float32)}
    _L0_ffn_all = _L0_ffn_setup()
    _L0_ffn_in = {k: v for k, v in _L0_ffn_all.items() if k in ('gate_w', 'up_w', 'down_w', 'fc1_w', 'fc2_w', 'expert_w', 'ln_gamma', 'ln_beta')}
    del _L0_ffn_all
    return {'x': x, 'ctx_4096': ctx_4096, 'L0_attn_Wq': _L0_attn_in['Wq'], 'L0_attn_Wk': _L0_attn_in['Wk'], 'L0_attn_Wv': _L0_attn_in['Wv'], 'L0_attn_Wo': _L0_attn_in['Wo'], 'L0_xattn_Wq': _L0_xattn_in['Wq'], 'L0_xattn_Wk': _L0_xattn_in['Wk'], 'L0_xattn_Wv': _L0_xattn_in['Wv'], 'L0_xattn_Wo': _L0_xattn_in['Wo'], 'L0_ffn_gate_w': _L0_ffn_in['gate_w'], 'L0_ffn_up_w': _L0_ffn_in['up_w'], 'L0_ffn_down_w': _L0_ffn_in['down_w'], 'L0_ffn_fc1_w': _L0_ffn_in['fc1_w'], 'L0_ffn_fc2_w': _L0_ffn_in['fc2_w'], 'L0_ffn_expert_w': _L0_ffn_in['expert_w'], 'L0_ffn_ln_gamma': _L0_ffn_in['ln_gamma'], 'L0_ffn_ln_beta': _L0_ffn_in['ln_beta']}

def reference(x, ctx_4096, L0_attn_Wq, L0_attn_Wk, L0_attn_Wv, L0_attn_Wo, L0_xattn_Wq, L0_xattn_Wk, L0_xattn_Wv, L0_xattn_Wo, L0_ffn_gate_w, L0_ffn_up_w, L0_ffn_down_w, L0_ffn_fc1_w, L0_ffn_fc2_w, L0_ffn_expert_w, L0_ffn_ln_gamma, L0_ffn_ln_beta):
    import jax
    import jax.numpy as jnp

    def _L0_attn_ref(x, Wq, Wk, Wv, Wo):
        import math
        import jax, jax.numpy as jnp
        import numpy as np
        B, T, E = (2, 256, 512)
        H, HKV = (32, 8)
        DH = E // H
        G = H // HKV
        ROPE_THETA = 500000.0
        ROPE_FACTOR = 32.0
        HI_FREQ_FACTOR = 4.0
        LO_FREQ_FACTOR = 1.0
        ORIG_CTX = 1024

        def _rope_cos_sin(t_len):
            inv_freq = 1.0 / ROPE_THETA ** (jnp.arange(0, DH, 2, dtype=jnp.float32) / DH)
            wavelen = 2.0 * math.pi / inv_freq
            cut_lo = ORIG_CTX / HI_FREQ_FACTOR
            cut_hi = ORIG_CTX / LO_FREQ_FACTOR
            inv_freq = jnp.where(wavelen > cut_hi, inv_freq / ROPE_FACTOR, inv_freq)
            smooth = (ORIG_CTX / wavelen - LO_FREQ_FACTOR) / (HI_FREQ_FACTOR - LO_FREQ_FACTOR)
            smoothed = (1.0 - smooth) * inv_freq / ROPE_FACTOR + smooth * inv_freq
            is_medium = ~(wavelen < cut_hi) & ~(wavelen > cut_lo)
            inv_freq = jnp.where(is_medium, smoothed, inv_freq)
            pos = jnp.arange(t_len, dtype=jnp.float32)
            freqs = pos[:, None] * inv_freq[None, :]
            emb = jnp.concatenate([freqs, freqs], axis=-1)
            return (jnp.cos(emb), jnp.sin(emb))

        def _rotate_half(x):
            x1, x2 = jnp.split(x, 2, axis=-1)
            return jnp.concatenate([-x2, x1], axis=-1)
        b, t, _ = x.shape
        q = (x @ Wq.T).reshape(b, t, H, DH).transpose(0, 2, 1, 3)
        k = (x @ Wk.T).reshape(b, t, HKV, DH).transpose(0, 2, 1, 3)
        v = (x @ Wv.T).reshape(b, t, HKV, DH).transpose(0, 2, 1, 3)
        cos, sin = _rope_cos_sin(t)
        cos = cos.astype(x.dtype)[None, None]
        sin = sin.astype(x.dtype)[None, None]
        q = q * cos + _rotate_half(q) * sin
        k = k * cos + _rotate_half(k) * sin
        qg = q.reshape(b, HKV, G, t, DH)
        scores = jnp.einsum('bhgtd,bhkd->bhgtk', qg.astype(jnp.float32), k.astype(jnp.float32)) / math.sqrt(DH)
        causal = jnp.tril(jnp.ones((t, t), dtype=bool))
        scores = jnp.where(causal[None, None, None], scores, jnp.finfo(jnp.float32).min)
        attn = jax.nn.softmax(scores, axis=-1).astype(x.dtype)
        ctx = jnp.einsum('bhgtk,bhkd->bhgtd', attn, v)
        out = ctx.reshape(b, H, t, DH).transpose(0, 2, 1, 3).reshape(b, t, E)
        return out @ Wo.T

    def _L0_xattn_ref(latents, context, Wq, Wk, Wv, Wo):
        import jax, jax.numpy as jnp
        import numpy as np
        import math
        HIDDEN = 512
        N_HEADS = 32
        HEAD_DIM = 128
        N_KV_HEADS = 4
        N_GROUPS = N_HEADS // N_KV_HEADS
        b, q_len, _ = latents.shape
        kv_len = q_len + context.shape[1]
        hidden_states = jnp.concatenate([context, latents], axis=1)
        q = (latents @ Wq).reshape(b, q_len, N_KV_HEADS, N_GROUPS, HEAD_DIM)
        k = (hidden_states @ Wk).reshape(b, kv_len, N_KV_HEADS, HEAD_DIM)
        v = (hidden_states @ Wv).reshape(b, kv_len, N_KV_HEADS, HEAD_DIM)
        scale = 1.0 / math.sqrt(HEAD_DIM)
        scores = jnp.einsum('bqhgd,bkhd->bhgqk', q, k) * scale
        attn = jax.nn.softmax(scores.astype(jnp.float32), axis=-1).astype(q.dtype)
        out = jnp.einsum('bhgqk,bkhd->bqhgd', attn, v)
        out = out.reshape(b, q_len, N_HEADS * HEAD_DIM)
        return out @ Wo

    def _L0_ffn_ref(hidden_states, gate_w, up_w, down_w, fc1_w, fc2_w, expert_w, ln_gamma, ln_beta):
        import jax, jax.numpy as jnp
        import numpy as np
        HID, INT, LAT, NE, K = (512, 1024, 256, 8, 2)
        LN_EPS = 1e-05

        def _layernorm(x, gamma, beta):
            mu = jnp.mean(x, axis=-1, keepdims=True)
            var = jnp.var(x, axis=-1, keepdims=True)
            return (x - mu) * jax.lax.rsqrt(var + LN_EPS) * gamma + beta
        logits = jnp.einsum('bsh,he->bse', hidden_states, gate_w)
        routing_weights, selected_experts = jax.lax.top_k(logits, K)
        h = jax.nn.relu(jnp.einsum('bsh,hi->bsi', hidden_states, up_w)) ** 2
        shared_out = jnp.einsum('bsi,ih->bsh', h, down_w)
        x_latent = jnp.einsum('bsh,hl->bsl', hidden_states, fc1_w)
        expert_out = jnp.einsum('bsl,lm->bsm', x_latent, expert_w)
        moe_out = expert_out * jnp.sum(routing_weights, axis=-1, keepdims=True)
        routed_out = jnp.einsum('bsl,lh->bsh', moe_out, fc2_w)
        return _layernorm(shared_out + routed_out, ln_gamma, ln_beta)
    x = x + _L0_attn_ref(_layernorm(x, axis=-1), L0_attn_Wq, L0_attn_Wk, L0_attn_Wv, L0_attn_Wo)
    x = x + _L0_xattn_ref(_layernorm(x, axis=-1), ctx_4096, L0_xattn_Wq, L0_xattn_Wk, L0_xattn_Wv, L0_xattn_Wo)
    x = x + _L0_ffn_ref(_layernorm(x, axis=-1), L0_ffn_gate_w, L0_ffn_up_w, L0_ffn_down_w, L0_ffn_fc1_w, L0_ffn_fc2_w, L0_ffn_expert_w, L0_ffn_ln_gamma, L0_ffn_ln_beta)
    return x

_drawn_inputs = setup_inputs


def setup_inputs(seed=0):
    import zlib

    import numpy as np

    out = dict(_drawn_inputs(seed))
    spreads = {'L0_ffn_ln_gamma': (1.0, 0.2), 'L0_ffn_ln_beta': (0.0, 0.1)}
    factors = {'L0_attn_Wq': 6.91, 'L0_attn_Wk': 5.791}
    for name, (base, spread) in spreads.items():
        noise = np.random.default_rng([zlib.crc32(name.encode()), seed]).standard_normal(out[name].shape)
        drawn = base * np.exp(spread * noise) if base else spread * noise
        out[name] = jnp.asarray(drawn.astype(out[name].dtype))
    for name, factor in factors.items():
        out[name] = (out[name] * factor).astype(out[name].dtype)
    return out
```

```python
from contextlib import ExitStack

import numpy as np

import concourse.bass as bass
from concourse import mybir

F32 = mybir.dt.float32
F32R = mybir.dt.float32r
ALU = mybir.AluOpType
ACT = mybir.ActivationFunctionType
AX = mybir.AxisListType

P = 128
NB = 8
D = 512
KC = D // P
EPS = 1e-5

SH, SKV, SD = 32, 8, 16
SG = SH // SKV
S_SCALE = 1.0 / float(np.sqrt(SD))
MASKED = -float(2.0 ** 126)

XH, XKV, XD = 32, 4, 128
XG = XH // XKV
KEYS = 2 * P
X_SCALE = 1.0 / float(np.sqrt(XD))
DUOS = NB * XG // 2
PB = XG // 2

INT, LAT, NE = 1024, 256, 8
IC, LC = INT // P, LAT // P

KB = 1024


def decoder_layer(nc, x, ctx, s_wq, s_wk, s_wv, s_wo, x_wq, x_wk, x_wv, x_wo, gate_w, up_w, down_w,
                  fc1_w, fc2_w, expert_w, gamma, beta, rope, out):
    with ExitStack() as stack:
        def sem(name):
            return stack.enter_context(nc.semaphore(name))

        at, cursor = {}, 16512
        for region, size in (("X", 16 * KB), ("XT", 32 * KB), ("WQ", 32 * KB), ("WO", 32 * KB),
                             ("Q", 32 * KB), ("O", 16 * KB), ("KV", 12 * KB), ("P", 8 * KB),
                             ("PT", 8 * KB), ("ST", 8 * KB), ("F", 9 * KB + 512), ("C", 2 * KB)):
            at[region] = cursor
            cursor += size

        def sb(name, region, kb, shape, dt=F32):
            return nc.alloc_sbuf_tensor_at(name, [P, *shape], dt, offset=at[region] + int(kb * KB))

        x_res = sb("x_res", "X", 0, [NB, D])
        ident = sb("ident", "C", 0, [P])
        ident_r = sb("ident_r", "C", 0.5, [P], F32R)
        rope_t = sb("rope_t", "C", 1, [2 * SD])
        stats = sb("stats", "C", 1.125, [6])
        mv = sb("mv", "C", 1.25, [2])
        rstd = sb("rstd", "C", 1.375, [1])
        half = sb("half", "C", 1.4375, [1])
        var_eps = sb("var_eps", "C", 1.5, [1])
        bd_mask = sb("bd_mask", "C", 1.53125, [SG])
        top8 = sb("top8", "C", 1.5625, [2, NE])
        route = sb("route", "C", 1.6875, [2])
        mv1 = sb("mv1", "C", 1.71875, [NB, 2])
        rstd1 = sb("rstd1", "C", 1.8125, [NB])
        stats1 = sb("stats1", "C", 1.875, [6])

        XTh = sb("XTh", "XT", 0, [KC, NB * P], F32R)
        XTl = sb("XTl", "XT", 16, [KC, NB * P], F32R)

        SQh = sb("SQh", "WO", 0, [KC, D], F32R)
        SQl = sb("SQl", "WO", 8, [KC, D], F32R)
        SOh = sb("SOh", "WO", 16, [SG, D], F32R)
        SOl = sb("SOl", "WO", 24, [SG, D], F32R)
        XKh = sb("XKh", "Q", 0, [KC, D], F32R)
        XKl = sb("XKl", "Q", 8, [KC, D], F32R)
        XVh = sb("XVh", "Q", 16, [KC, D], F32R)
        XVl = sb("XVl", "Q", 24, [KC, D], F32R)
        SKVh = sb("SKVh", "KV", 0, [KC, 2 * P], F32R)
        SKVl = sb("SKVl", "KV", 4, [KC, 2 * P], F32R)
        xnTh = sb("xnTh", "KV", 8, [KC, P], F32R)
        xnTl = sb("xnTl", "KV", 10, [KC, P], F32R)
        KVst = sb("KVst", "O", 0, [XKV, 1024], F32R)
        Kbdh = sb("Kbdh", "WQ", 0, [KC, D], F32R)
        QTh = sb("QTh", "WQ", 8, [KC, P], F32R)
        KTh = sb("KTh", "WQ", 10, [KC, P], F32R)
        HTh = sb("HTh", "WQ", 12, [KC, KEYS], F32R)
        Kbdl = sb("Kbdl", "WQ", 16, [KC, D], F32R)
        QTl = sb("QTl", "WQ", 24, [KC, P], F32R)
        KTl = sb("KTl", "WQ", 26, [KC, P], F32R)
        HTl = sb("HTl", "WQ", 28, [KC, KEYS], F32R)
        OTh, OTl = QTh, QTl
        Pa = sb("Pa", "P", 0, [3, D])
        cx = sb("cx", "P", 6, [D])
        PTah = sb("PTah", "PT", 0, [2, D], F32R)
        PTal = sb("PTal", "PT", 4, [2, D], F32R)
        xn = sb("xn", "ST", 0, [D])
        xn2 = sb("xn2", "ST", 2, [D])
        qr = sb("qr", "ST", 4, [D])
        kr = sb("kr", "PT", 0, [D])
        mask_r = sb("mask_r", "ST", 6.5, [P], F32R)
        a_max = sb("a_max", "ST", 7, [SH])
        a_nb = sb("a_nb", "ST", 7.125, [SH])
        a_sum = sb("a_sum", "ST", 7.25, [SH])
        a_rec = sb("a_rec", "ST", 7.375, [SH])
        mask_f = sb("mask_f", "ST", 7.5, [P])
        VBW = P + SD
        Vbdh = sb("Vbdh", "F", 0, [SKV * VBW], F32R)
        Vbdl = sb("Vbdl", "F", 4.5, [SKV * VBW], F32R)
        tq1, tq2, tk = Pa[:, 0, :], Pa[:, 1, :], Pa[:, 2, :]
        rawQ = sb("rawQ", "O", 0, [KC, D])
        rawO = sb("rawO", "O", 8, [KC, D])
        rawOg = sb("rawOg", "XT", 0, [KC, D])
        rawKV = sb("rawKV", "P", 0, [2, D])
        rawXK = sb("rawXK", "WQ", 0, [KC, D])
        rawXV = sb("rawXV", "WQ", 16, [KC, D])

        WQh = sb("WQh", "WQ", 0, [XG, KC, P], F32R)
        WQl = sb("WQl", "WQ", 16, [XG, KC, P], F32R)
        WOh = sb("WOh", "WO", 0, [XG, D], F32R)
        WOl = sb("WOl", "WO", 16, [XG, D], F32R)
        Qh = sb("Qh", "Q", 0, [2, XG, KEYS], F32R)
        Ql = sb("Ql", "Q", 16, [2, XG, KEYS], F32R)
        Oh = sb("Oh", "O", 0, [2, XG, P], F32R)
        Ol = sb("Ol", "O", 8, [2, XG, P], F32R)
        KV = sb("KV", "KV", 0, [3, 1024], F32R)
        Pb = sb("Pb", "P", 0, [4, 2, KEYS])
        PTh = sb("PTh", "PT", 0, [2, D], F32R)
        PTl = sb("PTl", "PT", 4, [2, D], F32R)
        raw = sb("raw", "ST", 0, [4, D])
        b_max = sb("b_max", "F", 8, [4, 2])
        b_nb = sb("b_nb", "F", 8.0625, [4, 2])
        b_sum = sb("b_sum", "F", 8.125, [4, 2])
        b_rec = sb("b_rec", "F", 8.1875, [4, 2])

        UPh = sb("UPh", "WQ", 0, [KC, INT], F32R)
        UPl = sb("UPl", "WQ", 16, [KC, INT], F32R)
        DNh = sb("DNh", "XT", 0, [IC, D], F32R)
        DNl = sb("DNl", "XT", 16, [IC, D], F32R)
        F1h = sb("F1h", "Q", 0, [KC, LAT], F32R)
        F2h = sb("F2h", "Q", 4, [LC, D], F32R)
        HBh = sb("HBh", "Q", 8, [IC, KEYS], F32R)
        F1l = sb("F1l", "Q", 16, [KC, LAT], F32R)
        F2l = sb("F2l", "Q", 20, [LC, D], F32R)
        HBl = sb("HBl", "Q", 24, [IC, KEYS], F32R)
        EXh = sb("EXh", "KV", 8, [LC, LAT], F32R)
        EXl = sb("EXl", "KV", 10, [LC, LAT], F32R)
        GTh = sb("GTh", "F", 0, [KC, P], F32R)
        GTl = sb("GTl", "F", 2, [KC, P], F32R)
        gam = sb("gam", "F", 4, [D])
        bet = sb("bet", "F", 6, [D])
        X3h = sb("X3h", "WO", 0, [KC, KEYS], F32R)
        X3l = sb("X3l", "WO", 4, [KC, KEYS], F32R)
        xn3 = sb("xn3", "WO", 8, [2, D])
        ysh = sb("ysh", "WO", 12, [2, D])
        yy = sb("yy", "WO", 16, [2, D])
        yo = sb("yo", "WO", 20, [2, D])
        xb = sb("xb", "WO", 24, [2, D])
        lgT = sb("lgT", "WO", 28, [KEYS])
        logits = sb("logits", "WO", 29.25, [2, NE])
        gate_raw = sb("gate_raw", "WO", 29, [KC, NE])
        hr = sb("hr", "O", 0, [2, D])
        hq = sb("hq", "O", 4, [2, D])
        LTh = sb("LTh", "O", 8, [LC, KEYS], F32R)
        LTl = sb("LTl", "O", 10, [LC, KEYS], F32R)
        ETh = sb("ETh", "O", 12, [LC, KEYS], F32R)
        ETl = sb("ETl", "O", 14, [LC, KEYS], F32R)

        kv_scratch = nc.dram_tensor("kv_scratch", (XKV, NB, P, 1024), F32, kind="Internal").ap()

        bank = [stack.enter_context(nc.psum_tensor(f"bank{i}", [P, 512], F32)) for i in range(8)]

        def f32(ap):
            return ap.bitcast(F32)

        def split3(pe, dst, lh, ll, rh, rl, start, stop):
            pe.matmul(dst, lh, rh, start=start, stop=False)
            pe.matmul(dst, lh, rl, start=False, stop=False)
            return pe.matmul(dst, ll, rh, start=False, stop=stop)

        ld_x, ld_w, ld_rope, ld_cx, st_kv, st_xt = (sem(n) for n in (
            "ld_x", "ld_w", "ld_rope", "ld_cx", "st_kv", "st_xt"))
        g_const, g_rstd, g_kbd, g_norm = (sem(n) for n in ("g_const", "g_rstd", "g_kbd", "g_norm"))
        pe_w, pe_xn, pe_ht, pe_qkv, pe_kvp, pe_qk, pe_s, pe_pt, pe_pv, pe_wo = (sem(n) for n in (
            "pe_w", "pe_xn", "pe_ht", "pe_qkv", "pe_kvp", "pe_qk", "pe_s", "pe_pt", "pe_pv", "pe_wo"))
        a_w, a_xn, a_ht, a_v, a_kvp, a_qk, a_exp, a_pt, a_o = (sem(n) for n in (
            "a_w", "a_xn", "a_ht", "a_v", "a_kvp", "a_qk", "a_exp", "a_pt", "a_o"))
        a_wog = sem("a_wog")
        v_c, v_w, v_st, v_xn, v_xnl, v_htl, v_rt, v_qr, v_vl, v_kvl, v_qkl, v_kbd, v_mx, v_nb, \
            v_rec, v_ptl, v_ol, v_x2, v_st2, v_xn2 = (sem(n) for n in (
                "v_c", "v_w", "v_st", "v_xn", "v_xnl", "v_htl", "v_rt", "v_qr", "v_vl", "v_kvl",
                "v_qkl", "v_kbd", "v_mx", "v_nb", "v_rec", "v_ptl", "v_ol", "v_x2", "v_st2", "v_xn2"))
        b_ld = [sem(f"b_ld{i}") for i in range(4)]
        b_kv = [sem(f"b_kv{i}") for i in range(3)]
        b_pe_q, b_pe_s, b_pe_pt, b_pe_pv, b_pe_wo = (sem(n) for n in (
            "b_pe_q", "b_pe_s", "b_pe_pt", "b_pe_pv", "b_pe_wo"))
        b_a_w, b_a_q, b_a_exp, b_a_pt, b_a_o = (sem(n) for n in (
            "b_a_w", "b_a_q", "b_a_exp", "b_a_pt", "b_a_o"))
        b_v_mx, b_v_nb, b_v_rec, b_v_pt, b_v_q, b_v_o, b_v_x = (sem(n) for n in (
            "b_v_mx", "b_v_nb", "b_v_rec", "b_v_pt", "b_v_q", "b_v_o", "b_v_x"))
        b_g_w, b_g_norm = sem("b_g_w"), sem("b_g_norm")
        c_ld, c_out = sem("c_ld"), [sem("c_out0"), sem("c_out1")]
        c_pe_x, c_pe_g, c_pe_gt, c_pe_h, c_pe_l, c_pe_e, c_pe_y = (sem(n) for n in (
            "c_pe_x", "c_pe_g", "c_pe_gt", "c_pe_h", "c_pe_l", "c_pe_e", "c_pe_y"))
        c_a_x, c_a_g, c_a_hr, c_a_h, c_a_l, c_a_y = (sem(n) for n in (
            "c_a_x", "c_a_g", "c_a_hr", "c_a_h", "c_a_l", "c_a_y"))
        c_v_g0, c_v_st, c_v_xn, c_v_x, c_v_h2, c_v_h, c_v_l, c_v_r, c_v_y, c_v_n = (
            sem(n) for n in ("c_v_g0", "c_v_st", "c_v_xn", "c_v_x", "c_v_h2", "c_v_h", "c_v_l",
                             "c_v_r", "c_v_y", "c_v_n"))
        c_g_r, c_g_xb = sem("c_g_r"), sem("c_g_xb")

        W0 = XG
        WPG = 2 * XG
        ffn_chunks = (
            [(up_w[kc * P:(kc + 1) * P, n * D:(n + 1) * D], UPh[:, kc, n * D:(n + 1) * D],
              UPl[:, kc, n * D:(n + 1) * D]) for kc in range(KC) for n in range(INT // D)]
            + [(down_w[c * P:(c + 1) * P, :], DNh[:, c, :], DNl[:, c, :]) for c in range(IC)]
            + [(fc1_w[c * 2 * P:(c + 1) * 2 * P, :].rearrange("(k p) n -> p k n", p=P),
                F1h[:, 2 * c:2 * c + 2, :], F1l[:, 2 * c:2 * c + 2, :]) for c in range(KC // 2)]
            + [(fc2_w[c * P:(c + 1) * P, :], F2h[:, c, :], F2l[:, c, :]) for c in range(LC)]
            + [(expert_w.rearrange("(k p) n -> p k n", p=P), EXh[:, :, :], EXl[:, :, :])])
        NF = len(ffn_chunks)

        def wq_src(g, h):
            return x_wq.rearrange("(k p) (h n) -> h p k n", p=P, n=XD)[XG * g + h]

        def wo_src(g, h):
            return x_wo.rearrange("(h p) n -> h p n", p=XD)[XG * g + h]

        def chunk_steps(last):
            steps = [(h // 2, "wo", h) for h in range(XG)]
            if not last:
                steps += [(17 + h, "wq", h) for h in range(XG)]
            else:
                steps += [(17 + i, "ffn", i) for i in range(8)]
                steps += [(25 + (i - 8) // 2, "ffn", i) for i in range(8, NF)]
            return steps

        def raw_view(slot, dst):
            v = raw[:, slot, :]
            if len(dst.shape) == 3:
                v = v.rearrange("p (k n) -> p k n", k=dst.shape[1])
            return v

        def targets(kind, i):
            if kind == "wo":
                return WOh[:, i, :], WOl[:, i, :]
            if kind == "wq":
                return WQh[:, i, :, :], WQl[:, i, :, :]
            return ffn_chunks[i][1:]

        block = stack.enter_context(nc.Block())

        @block.sync
        def _(sp):
            sp.dma_start(x_res[:], x.rearrange("b t d -> t b d")).then_inc(ld_x, 16)
            sp.dma_start(rawQ[:], s_wq.rearrange("(m p) n -> p m n", p=P)).then_inc(ld_w, 16)
            sp.dma_start(rawKV[:, 0, :], s_wk).then_inc(ld_w, 16)
            sp.dma_start(rawKV[:, 1, :], s_wv).then_inc(ld_w, 16)
            sp.dma_start(rawO[:], s_wo.rearrange("(m p) n -> p m n", p=P)).then_inc(ld_w, 16)
            sp.dma_start(rawXK[:], x_wk.rearrange("(k p) n -> p k n", p=P)).then_inc(ld_w, 16)
            sp.dma_start(rawXV[:], x_wv.rearrange("(k p) n -> p k n", p=P)).then_inc(ld_w, 16)
            sp.dma_start(rope_t[:], rope).then_inc(ld_rope, 16)
            sp.dma_start(cx[:], ctx[0]).then_inc(ld_cx, 16)

            def keep(b):
                sp.wait_ge(v_htl, 2 * b + 2)
                for src, dst in ((HTh, XTh), (HTl, XTl)):
                    sp.dma_start(f32(dst[:].rearrange("p k (b n) -> p b k n", b=NB)[:, b]),
                                 f32(src[:, :, P:KEYS])).then_inc(st_xt, 16)

            def store_kv(b):
                sp.wait_ge(a_kvp, 4 * b + 4)
                sp.wait_ge(v_kvl, 4 * b + 4)
                sp.dma_start(kv_scratch[:, b].rearrange("g p n -> p g n"), f32(KVst[:])).then_inc(st_kv, 16)

            with sp.Fori(0, NB - 1) as b:
                keep(b)
                sp.wait_ge(pe_ht, 2 * b + 2)
                sp.dma_start(cx[:], ctx[b + 1]).then_inc(ld_cx, 16)
                store_kv(b)
            keep(NB - 1)
            sp.wait_ge(pe_ht, 2 * NB)
            for h in range(XG):
                if h >= 4:
                    sp.wait_ge(b_g_w, h - 3)
                sp.dma_start(raw_view(h % 4, WQh[:, h, :, :]), wq_src(0, h)).then_inc(b_ld[h % 4], 16)
            store_kv(NB - 1)
            sp.wait_ge(st_kv, 16 * NB)
            sp.wait_ge(pe_qkv, 2 * NB)
            for b in range(3):
                sp.dma_start(f32(KV[:, b, :]), kv_scratch[0, b]).then_inc(b_kv[b], 16)

            def group(g, last):
                kv_loads = [(4 * (b - 3) + 4, g, b) for b in range(3, NB)]
                if not last:
                    kv_loads += [(24, g + 1, 2), (28, g + 1, 0), (32, g + 1, 1)]
                w_loads = [(max(step - 2, 0), kind, i) for step, kind, i in chunk_steps(last)]
                for k in range(DUOS):
                    for n, (step, kind, i) in enumerate(w_loads):
                        if step == k:
                            sp.wait_ge(b_g_w, W0 + WPG * g + n - 3)
                            dst = targets(kind, i)[0]
                            src = (wo_src(g, i) if kind == "wo" else wq_src(g + 1, i) if kind == "wq"
                                   else ffn_chunks[i][0])
                            sp.dma_start(raw_view(n % 4, dst), src).then_inc(b_ld[n % 4], 16)
                    for done, gg, b in kv_loads:
                        if done == k + 1:
                            n = NB * gg + b if last else sp.snap(NB * gg + b)
                            sp.wait_ge(b_pe_pv, DUOS * g + done)
                            sp.dma_start(f32(KV[:, b % 3, :]), kv_scratch.rearrange("g b p n -> (g b) p n")[n]
                                         ).then_inc(b_kv[b % 3], 16)

            with sp.Fori(0, XKV - 1) as g:
                group(g, False)
            group(XKV - 1, True)
            sp.wait_ge(b_pe_wo, PB * NB * XKV)
            sp.dma_start(gate_raw[:], gate_w.rearrange("(k p) n -> p k n", p=P)).then_inc(c_ld, 16)
            sp.dma_start(gam[:], gamma.partition_broadcast(P)).then_inc(c_ld, 16)
            sp.dma_start(bet[:], beta.partition_broadcast(P)).then_inc(c_ld, 16)
            with sp.Fori(0, NB // 2) as c:
                for t in range(2):
                    tile = sp.snap(2 * c + t)
                    sp.wait_ge(c_v_n, 6 * c + 3 * t + 3)
                    sp.dma_start(out[tile], yo[:, t, :]).then_inc(c_out[t], 16)
            sp.wait_ge(c_out[0], 16 * (NB // 2))
            sp.wait_ge(c_out[1], 16 * (NB // 2))

        @block.gpsimd
        def _(gp):
            gp.memset(ident[:], 0.0).then_inc(g_const, 1)
            gp.memset(mask_f[:], 0.0).then_inc(g_const, 1)
            gp.memset(bd_mask[:], 0.0).then_inc(g_const, 1)
            gp.memset(half[:], -0.5).then_inc(g_const, 1)
            gp.wait_ge(g_const, 4)
            gp.affine_select(out=ident[:], in_=ident[:], compare_op=ALU.not_equal, fill=1.0, base=0,
                             pattern=[[-1, P]], channel_multiplier=1).then_inc(g_const, 1)
            gp.affine_select(out=mask_f[:], in_=mask_f[:], compare_op=ALU.is_ge, fill=MASKED, base=0,
                             pattern=[[-1, P]], channel_multiplier=1).then_inc(g_const, 1)
            n = 6
            for base in range(2):
                for r in range(SD):
                    gp.wait_ge(g_const, n)
                    gp.affine_select(out=bd_mask[:], in_=bd_mask[:], compare_op=ALU.not_equal, fill=1.0,
                                     base=-(64 * base + r), pattern=[[-SD, SG]],
                                     channel_multiplier=1).then_inc(g_const, 1)
                    n += 1
            gp.wait_ge(v_st, 3)
            gp.tensor_tensor(rstd1[:], rstd1[:], half[:].to_broadcast([P, NB]), ALU.pow).then_inc(g_rstd, 1)

            def batch(b):
                for m in range(KC):
                    gp.wait_ge(a_qk, 2 * b + 2)
                    src = f32(KTh[:, m, :]).unsqueeze(1).to_broadcast([P, SG, P])
                    gp.tensor_tensor(Kbdh[:, m, :].rearrange("p (c k) -> p c k", c=SG), src,
                                     bd_mask[:].unsqueeze(2).to_broadcast([P, SG, P]), ALU.mult).then_inc(g_kbd, 1)
                for j in range(SKV):
                    gp.wait_ge(v_rec, SKV * b + j + 1)
                    pj = Pa[:, j % 3, :].rearrange("p (c k) -> p c k", c=SG)
                    gp.tensor_tensor(pj, pj, a_rec[:, SG * j:SG * j + SG].unsqueeze(2).to_broadcast([P, SG, P]),
                                     ALU.mult).then_inc(g_norm, 1)
                gp.wait_ge(v_st2, b + 1)
                gp.tensor_tensor(rstd[:], var_eps[:], half[:], ALU.pow).then_inc(g_rstd, 1)

            with gp.Fori(0, NB) as b:
                batch(b)

            def lo_part(slot, count, dst, hi):
                gp.wait_ge(b_a_w, count)
                gp.tensor_tensor(dst, raw_view(slot, dst), f32(hi), ALU.subtract).then_inc(b_g_w, 1)

            def norm(g, k):
                gp.wait_ge(b_v_rec, DUOS * g + k + 1)
                pk = Pb[:, k % 4, :, :]
                gp.tensor_tensor(pk, pk, b_rec[:, k % 4, :].unsqueeze(2).to_broadcast([P, 2, KEYS]),
                                 ALU.mult).then_inc(b_g_norm, 1)

            for h in range(XG):
                lo_part(h % 4, h + 1, WQl[:, h, :, :], WQh[:, h, :, :])
            norm(0, 0)
            norm(0, 1)

            def group(g, last):
                chunks = chunk_steps(last)
                for k in range(DUOS):
                    if k + 2 < DUOS:
                        norm(g, k + 2)
                    elif not last:
                        norm(g + 1, k + 2 - DUOS)
                    for n, (step, kind, i) in enumerate(chunks):
                        if step == k:
                            hi, lo = targets(kind, i)
                            lo_part(n % 4, W0 + WPG * g + n + 1, lo, hi)

            with gp.Fori(0, XKV - 1) as g:
                group(g, False)
            group(XKV - 1, True)

            with gp.Fori(0, NB // 2) as c:
                for t in range(2):
                    gp.wait_ge(c_v_st, 4 * c + t + 1)
                    gp.tensor_tensor(rstd[:], var_eps[:], half[:], ALU.pow).then_inc(c_g_r, 1)
                for t in range(2):
                    gp.wait_ge(c_ld, 48)
                    gp.wait_ge(c_v_n, 6 * c)
                    gp.tensor_tensor(xb[:, t, :], x_res[:, 2 * c + t, :], bet[:], ALU.add).then_inc(c_g_xb, 1)
                for t in range(2):
                    gp.wait_ge(c_v_st, 4 * c + 2 + t + 1)
                    gp.tensor_tensor(rstd[:], var_eps[:], half[:], ALU.pow).then_inc(c_g_r, 1)

        @block.tensor
        def _(pe):
            pe.wait_ge(g_const, 6)
            pe.wait_ge(ld_w, 16 * 6)
            for n in range(10):
                bk = bank[n % 8]
                if n >= 8:
                    pe.wait_ge(v_w, n - 7)
                for m in range(KC):
                    if n < 4:
                        src = rawQ[:, m, n * P:(n + 1) * P]
                    elif n < 6:
                        kc = 2 * (n - 4) + m // 2
                        src = rawKV[:, m % 2, kc * P:(kc + 1) * P]
                    else:
                        if m == 0:
                            pe.wait_ge(a_wog, KC)
                        src = rawOg[:, m, (n - 6) * P:(n - 5) * P]
                    op = pe.transpose(bk[:, m * P:(m + 1) * P], src, ident[:])
                op.then_inc(pe_w, 1)
            pe.wait_ge(v_w, 12)
            pe.wait_ge(v_c, 2)

            def turn_latents(b):
                pe.wait_ge(v_xn2, b + 1)
                pe.wait_ge(v_ol, b + 1)
                for kc in range(KC):
                    op = pe.transpose(bank[7][:, kc * P:(kc + 1) * P], xn2[:, kc * P:(kc + 1) * P], ident[:])
                op.then_inc(pe_ht, 1)
                pe.wait_ge(ld_cx, 16 * b + 16)
                pe.wait_ge(a_exp, SKV * b + SKV)
                for kc in range(KC):
                    op = pe.transpose(bank[4][:, kc * P:(kc + 1) * P], cx[:, kc * P:(kc + 1) * P], ident[:])
                op.then_inc(pe_ht, 1)

            def keys_values(b):
                pe.wait_ge(v_ptl, SKV * b + SKV)
                pe.wait_ge(v_htl, 2 * b + 2)
                for n in range(2):
                    for gg in range(2):
                        g = 2 * n + gg
                        dst = bank[5 + n][:, gg * KEYS:(gg + 1) * KEYS]
                        for kc in range(KC):
                            op = split3(pe, dst, XKh[:, kc, g * XD:(g + 1) * XD], XKl[:, kc, g * XD:(g + 1) * XD],
                                        HTh[:, kc, :], HTl[:, kc, :], kc == 0, kc == KC - 1)
                    op.then_inc(pe_kvp, 1)
                for t in range(2):
                    pe.wait_ge(v_kvl, 4 * b + t + 1)
                    for kc in range(KC):
                        op = split3(pe, bank[5 + t][:], HTh[:, kc, t * P:(t + 1) * P], HTl[:, kc, t * P:(t + 1) * P],
                                    XVh[:, kc, :], XVl[:, kc, :], kc == 0, kc == KC - 1)
                    op.then_inc(pe_kvp, 1)

            def batch(b, first):
                pe.wait_ge(v_xn, b + 1)
                if not first:
                    pe.wait_ge(v_vl, b)
                for kc in range(KC):
                    op = pe.transpose(bank[0][:, kc * P:(kc + 1) * P], xn[:, kc * P:(kc + 1) * P], ident[:])
                op.then_inc(pe_xn, 1)
                if not first:
                    turn_latents(b - 1)
                    pe.wait_ge(v_x2, b)
                pe.wait_ge(v_xnl, b + 1)
                for kc in range(KC):
                    op = split3(pe, bank[1][:], xnTh[:, kc, :], xnTl[:, kc, :], SQh[:, kc, :], SQl[:, kc, :],
                                kc == 0, kc == KC - 1)
                op.then_inc(pe_qkv, 1)
                for kc in range(KC):
                    op = split3(pe, bank[0][:, 0:2 * P], xnTh[:, kc, :], xnTl[:, kc, :], SKVh[:, kc, :],
                                SKVl[:, kc, :], kc == 0, kc == KC - 1)
                op.then_inc(pe_qkv, 1)
                if not first:
                    keys_values(b - 1)
                pe.wait_ge(v_qr, 2 * b + 2)
                for m in range(KC):
                    op = pe.transpose(bank[2][:, m * P:(m + 1) * P], qr[:, m * P:(m + 1) * P], ident[:])
                op.then_inc(pe_qk, 1)
                for m in range(KC):
                    op = pe.transpose(bank[3][:, m * P:(m + 1) * P], kr[:, m * P:(m + 1) * P], ident[:])
                op.then_inc(pe_qk, 1)

                def scores(j):
                    bk = bank[2 + j % 3]
                    m, r = j // 2, 64 * (j % 2)
                    if j >= 3:
                        pe.wait_ge(a_exp, SKV * b + j - 2)
                    elif j < 2:
                        pe.wait_ge(v_qkl, 2 * b + 2)
                    pe.wait_ge(g_kbd, KC * b + m + 1)
                    pe.wait_ge(v_kbd, KC * b + m + 1)
                    pe.matmul(bk[:].rearrange("p (c k) -> p c k", c=SG), ident_r[:],
                              mask_r[:].unsqueeze(1).to_broadcast([P, SG, P]), start=True, stop=False)
                    rows = slice(r, r + 64)
                    split3(pe, bk[:], QTh[rows, m, :], QTl[rows, m, :], Kbdh[rows, m, :], Kbdl[rows, m, :],
                           False, True).then_inc(pe_s, 1)

                def turn(j):
                    pe.wait_ge(g_norm, SKV * b + j + 1)
                    if j >= 2:
                        pe.wait_ge(v_ptl, SKV * b + j - 1)
                    elif not first:
                        pe.wait_ge(v_kvl, 4 * b - 1 + j)
                    for c in range(SG):
                        op = pe.transpose(bank[5 + j % 2][:, c * P:(c + 1) * P],
                                          Pa[:, j % 3, c * P:(c + 1) * P], ident[:])
                    op.then_inc(pe_pt, 1)

                def values(j):
                    pe.wait_ge(v_ptl, SKV * b + j + 1)
                    if j == 0:
                        pe.wait_ge(v_vl, b + 1)
                        pe.wait_ge(a_v, b + 1)
                        if not first:
                            pe.wait_ge(v_htl, 2 * b)
                    op = split3(pe, bank[7][:], Vbdh[:, j * P:(j + 1) * P], Vbdl[:, j * P:(j + 1) * P],
                                PTah[:, j % 2, :], PTal[:, j % 2, :], j == 0, j == SKV - 1)
                    if j == SKV - 1:
                        op.then_inc(pe_pv, 1)

                scores(0)
                scores(1)
                scores(2)
                for j in range(SKV):
                    turn(j)
                    if j + 3 < SKV:
                        scores(j + 3)
                    if j >= 1:
                        values(j - 1)
                values(SKV - 1)
                pe.wait_ge(v_ol, b + 1)
                for g in range(SG):
                    op = split3(pe, bank[1][:], OTh[:, g, :], OTl[:, g, :], SOh[:, g, :], SOl[:, g, :],
                                g == 0, g == SG - 1)
                op.then_inc(pe_wo, 1)

            batch(0, True)
            with pe.Fori(1, NB) as b:
                batch(b, False)
            turn_latents(NB - 1)
            keys_values(NB - 1)

            def queries(g_count, head, pair):
                pe.wait_ge(b_g_w, g_count)
                for kc in range(KC):
                    op = split3(pe, bank[6][:, (head % 2) * KEYS:(head % 2 + 1) * KEYS],
                                WQh[:, head, kc, :], WQl[:, head, kc, :],
                                XTh[:, kc, pair * KEYS:(pair + 1) * KEYS], XTl[:, kc, pair * KEYS:(pair + 1) * KEYS],
                                kc == 0, kc == KC - 1)
                op.then_inc(b_pe_q, 1)

            def scores_b(g, k):
                b, i = k // PB, k % PB
                slot = b % 3
                if i == 0:
                    pe.wait_ge(b_kv[slot], 16 * ((3 if slot < 2 else 2) * g + b // 3 + 1))
                if b % 2 == 0:
                    pe.wait_ge(b_v_q, 4 + 16 * g + 4 * (b // 2) - 4 + i + 1)
                for h in range(2):
                    head = 2 * i + h
                    op = split3(pe, bank[k % 3][:, h * KEYS:(h + 1) * KEYS],
                                Qh[:, (b // 2) % 2, head, (b % 2) * P:(b % 2 + 1) * P],
                                Ql[:, (b // 2) % 2, head, (b % 2) * P:(b % 2 + 1) * P],
                                KV[:, slot, 0:KEYS], KV[:, slot, KEYS:2 * KEYS], True, True)
                op.then_inc(b_pe_s, 1)

            def out_piece(g, b, i):
                pe.wait_ge(b_v_o, DUOS * g + PB * b + i + 1)
                pe.wait_ge(b_g_w, W0 + WPG * g + 2 * i + 2)
                if i == 0:
                    pe.wait_ge(b_v_x, NB * g + b)
                for h in range(2):
                    head = 2 * i + h
                    op = split3(pe, bank[7][:], Oh[:, b % 2, head, :], Ol[:, b % 2, head, :], WOh[:, head, :],
                                WOl[:, head, :], head == 0, head == XG - 1)
                op.then_inc(b_pe_wo, 1)

            pe.wait_ge(st_xt, 32 * NB)
            pe.wait_ge(v_kvl, 4 * NB)
            for h in range(XG):
                if h % 2 == 0 and h:
                    pe.wait_ge(b_v_q, h // 2)
                queries(h + 1, h, 0)
            scores_b(0, 0)
            scores_b(0, 1)

            def group(g, last):
                for k in range(DUOS):
                    if k + 2 < DUOS or not last:
                        if k + 2 < DUOS:
                            pe.wait_ge(b_a_exp, DUOS * g + k)
                            scores_b(g, k + 2)
                        else:
                            pe.wait_ge(b_a_exp, DUOS * g + k + 1)
                            scores_b(g + 1, k + 2 - DUOS)
                    pe.wait_ge(b_g_norm, DUOS * g + k + 1)
                    pe.wait_ge(b_v_pt, DUOS * g + max(k - 1, 0))
                    for c in range(2):
                        for h in range(2):
                            op = pe.transpose(bank[3 + k % 2][:, c * KEYS + h * P:c * KEYS + (h + 1) * P],
                                              Pb[:, k % 4, h, c * P:(c + 1) * P], ident[:])
                    op.then_inc(b_pe_pt, 1)
                    if k >= PB:
                        out_piece(g, k // PB - 1, k % PB)
                    if k < DUOS - XG or not last:
                        if k % 2 == 0:
                            pe.wait_ge(b_v_q, 4 + 16 * g + k // 2)
                        if k < DUOS - XG:
                            queries(W0 + WPG * g, k % XG, k // XG + 1)
                        else:
                            queries(W0 + WPG * g + XG + k % XG + 1, k % XG, 0)
                    pe.wait_ge(b_v_pt, DUOS * g + k + 1)
                    pe.wait_ge(b_v_o, DUOS * g + k)
                    slot = (k // PB) % 3
                    for c in range(2):
                        vh = KV[:, slot, 2 * KEYS + c * P:2 * KEYS + (c + 1) * P]
                        vl = KV[:, slot, 3 * KEYS + c * P:3 * KEYS + (c + 1) * P]
                        op = split3(pe, bank[5][:, 0:KEYS], vh, vl, PTh[:, k % 2, c * KEYS:(c + 1) * KEYS],
                                    PTl[:, k % 2, c * KEYS:(c + 1) * KEYS], c == 0, c == 1)
                    op.then_inc(b_pe_pv, 1)
                for i in range(PB):
                    out_piece(g, NB - 1, i)

            with pe.Fori(0, XKV - 1) as g:
                group(g, False)
            group(XKV - 1, True)

            pe.wait_ge(b_g_w, W0 + WPG * (XKV - 1) + XG + NF)
            pe.wait_ge(c_v_g0, 3)
            with pe.Fori(0, NB // 2) as c:
                for t in range(2):
                    pe.wait_ge(c_v_xn, 2 * c + t + 1)
                    for kc in range(KC):
                        op = pe.transpose(bank[t][:, kc * P:(kc + 1) * P], xn3[:, t, kc * P:(kc + 1) * P], ident[:])
                    op.then_inc(c_pe_x, 1)
                pe.wait_ge(c_v_x, 2 * c + 2)
                for kc in range(KC):
                    op = split3(pe, bank[0][:, 0:KEYS], GTh[:, kc, :], GTl[:, kc, :], X3h[:, kc, :], X3l[:, kc, :],
                                kc == 0, kc == KC - 1)
                op.then_inc(c_pe_g, 1)
                for m in range(LC):
                    for kc in range(KC):
                        op = split3(pe, bank[1][:, m * KEYS:(m + 1) * KEYS], F1h[:, kc, m * P:(m + 1) * P],
                                    F1l[:, kc, m * P:(m + 1) * P], X3h[:, kc, :], X3l[:, kc, :], kc == 0, kc == KC - 1)
                op.then_inc(c_pe_l, 1)
                for n in range(IC // 2):
                    pe.wait_ge(c_v_h, 4 * c)
                    for mm in range(2):
                        m = 2 * n + mm
                        for kc in range(KC):
                            op = split3(pe, bank[2 + n][:, mm * KEYS:(mm + 1) * KEYS], UPh[:, kc, m * P:(m + 1) * P],
                                        UPl[:, kc, m * P:(m + 1) * P], X3h[:, kc, :], X3l[:, kc, :],
                                        kc == 0, kc == KC - 1)
                    op.then_inc(c_pe_h, 1)
                    if n == 0:
                        pe.wait_ge(c_a_g, c + 2)
                        for t in range(2):
                            op = pe.transpose(bank[0][:, KEYS + t * P:KEYS + (t + 1) * P],
                                              lgT[:, t * P:(t + 1) * P], ident[:])
                        op.then_inc(c_pe_gt, 1)
                    if n == 1:
                        pe.wait_ge(c_v_l, 2 * c + 1)
                        for m in range(LC):
                            for kc in range(LC):
                                op = split3(pe, bank[1][:, m * KEYS:(m + 1) * KEYS], EXh[:, kc, m * P:(m + 1) * P],
                                            EXl[:, kc, m * P:(m + 1) * P], LTh[:, kc, :], LTl[:, kc, :],
                                            kc == 0, kc == LC - 1)
                        op.then_inc(c_pe_e, 1)
                pe.wait_ge(c_v_l, 2 * c + 2)
                pe.wait_ge(c_v_r, c + 1)
                for t in range(2):
                    for kc in range(LC):
                        op = split3(pe, bank[t][:], ETh[:, kc, t * P:(t + 1) * P], ETl[:, kc, t * P:(t + 1) * P],
                                    F2h[:, kc, :], F2l[:, kc, :], kc == 0, kc == LC - 1)
                    op.then_inc(c_pe_y, 1)
                for t in range(2):
                    for m in range(IC):
                        if t == 0 and m % 2 == 0:
                            pe.wait_ge(c_v_h, 4 * c + m // 2 + 1)
                        op = split3(pe, bank[6 + t][:], HBh[:, m, t * P:(t + 1) * P], HBl[:, m, t * P:(t + 1) * P],
                                    DNh[:, m, :], DNl[:, m, :], m == 0, m == IC - 1)
                    op.then_inc(c_pe_y, 1)

        @block.scalar
        def _(act):
            def hi(dst, src):
                return act.activation(dst, src, ACT.Copy)

            act.wait_ge(ld_w, 16 * 6)
            for m in range(KC):
                act.activation(rawOg[:, m, :].rearrange("p (g j d) -> p g j d", g=SG, j=SKV),
                               rawO[:, m, :].rearrange("p (j g d) -> p g j d", j=SKV, g=SG),
                               ACT.Copy).then_inc(a_wog, 1)
            for n in range(10):
                act.wait_ge(pe_w, n + 1)
                if n < 4:
                    dst = SQh[:, n, :]
                elif n < 6:
                    dst = SKVh[:, 2 * (n - 4):2 * (n - 4) + 2, :].rearrange("p k n -> p (k n)")
                else:
                    dst = SOh[:, n - 6, :]
                hi(dst, bank[n % 8][:]).then_inc(a_w, 1)
            hi(XKh[:], rawXK[:]).then_inc(a_w, 1)
            hi(XVh[:], rawXV[:]).then_inc(a_w, 1)

            def latents(b):
                for t in range(2):
                    act.wait_ge(pe_ht, 2 * b + t + 1)
                    src = bank[7 if t == 0 else 4][:].rearrange("p (k n) -> p k n", k=KC)
                    hi(HTh[:, :, (1 - t) * P:(2 - t) * P], src).then_inc(a_ht, 1)

            def keys_values(b, first):
                if not first:
                    act.wait_ge(st_kv, 16 * b)
                for n in range(2):
                    act.wait_ge(pe_kvp, 4 * b + n + 1)
                    hi(KVst[:, 2 * n:2 * n + 2, 0:KEYS],
                       bank[5 + n][:].rearrange("p (g n) -> p g n", g=2)).then_inc(a_kvp, 1)
                for t in range(2):
                    act.wait_ge(pe_kvp, 4 * b + t + 3)
                    hi(KVst[:, :, 2 * KEYS + t * P:2 * KEYS + (t + 1) * P],
                       bank[5 + t][:].rearrange("p (g n) -> p g n", g=XKV)).then_inc(a_kvp, 1)

            def batch(b, first):
                act.wait_ge(pe_xn, b + 1)
                hi(xnTh[:], bank[0][:].rearrange("p (k n) -> p k n", k=KC)).then_inc(a_xn, 1)
                if not first:
                    act.wait_ge(st_xt, 32 * (b - 1))
                    latents(b - 1)
                act.wait_ge(pe_qkv, 2 * b + 2)
                act.wait_ge(v_c, 4)
                hi(Vbdh[:].rearrange("p (j c) -> p j c", c=VBW)[:, :, 0:SD],
                   bank[0][:, P:2 * P].rearrange("p (j d) -> p j d", j=SKV)).then_inc(a_v, 1)
                if not first:
                    keys_values(b - 1, False)
                act.wait_ge(pe_qk, 2 * b + 1)
                hi(QTh[:], bank[2][:].rearrange("p (k n) -> p k n", k=KC)).then_inc(a_qk, 1)
                act.wait_ge(pe_qk, 2 * b + 2)
                hi(KTh[:], bank[3][:].rearrange("p (k n) -> p k n", k=KC)).then_inc(a_qk, 1)

                def probs(j):
                    act.wait_ge(v_nb, SKV * b + j + 1)
                    if j >= 3:
                        act.wait_ge(pe_pt, SKV * b + j - 2)
                    for c in range(SG):
                        h = SG * j + c
                        op = act.activation(Pa[:, j % 3, c * P:(c + 1) * P], bank[2 + j % 3][:, c * P:(c + 1) * P],
                                            ACT.Exp, bias=a_nb[:, h:h + 1], scale=S_SCALE, accum_out=a_sum[:, h:h + 1])
                    op.then_inc(a_exp, 1)

                probs(0)
                probs(1)
                for j in range(SKV):
                    if j + 2 < SKV:
                        probs(j + 2)
                    act.wait_ge(pe_pt, SKV * b + j + 1)
                    hi(PTah[:, j % 2, :], bank[5 + j % 2][:]).then_inc(a_pt, 1)
                act.wait_ge(pe_pv, b + 1)
                hi(OTh[:], bank[7][:].rearrange("p (k n) -> p k n", k=KC)).then_inc(a_o, 1)

            batch(0, True)
            with act.Fori(1, NB) as b:
                batch(b, False)
            act.wait_ge(st_xt, 32 * (NB - 1))
            latents(NB - 1)
            keys_values(NB - 1, False)

            def weight(slot, loads, hi_dst):
                act.wait_ge(b_ld[slot], 16 * loads)
                hi(hi_dst, raw_view(slot, hi_dst)).then_inc(b_a_w, 1)

            def probs_b(g, k):
                act.wait_ge(b_v_nb, DUOS * g + k + 1)
                for h in range(2):
                    op = act.activation(Pb[:, k % 4, h, :], bank[k % 3][:, h * KEYS:(h + 1) * KEYS], ACT.Exp,
                                        bias=b_nb[:, k % 4, h:h + 1], scale=X_SCALE,
                                        accum_out=b_sum[:, k % 4, h:h + 1])
                op.then_inc(b_a_exp, 1)

            def queries(count, fill, parity):
                act.wait_ge(b_pe_q, 2 * count)
                hi(Qh[:, parity, 2 * fill:2 * fill + 2, :],
                   bank[6][:].rearrange("p (h n) -> p h n", h=2)).then_inc(b_a_q, 1)

            act.wait_ge(pe_kvp, 4 * NB)
            act.wait_ge(st_xt, 32 * NB)
            for h in range(XG):
                weight(h % 4, h // 4 + 1, WQh[:, h, :, :])
            for f in range(4):
                queries(f + 1, f, 0)
            probs_b(0, 0)
            probs_b(0, 1)

            def group(g, last):
                chunks = chunk_steps(last)
                for k in range(DUOS):
                    act.wait_ge(b_pe_pt, DUOS * g + k + 1)
                    hi(PTh[:, k % 2, :], bank[3 + k % 2][:]).then_inc(b_a_pt, 1)
                    if k + 2 < DUOS:
                        probs_b(g, k + 2)
                    elif not last:
                        probs_b(g + 1, k + 2 - DUOS)
                    for n, (step, kind, i) in enumerate(chunks):
                        if step == k:
                            if kind == "wo":
                                act.wait_ge(b_pe_wo, PB * NB * g)
                            elif kind == "wq" or i < 8:
                                act.wait_ge(b_pe_q, XG + DUOS * g + 17 + i)
                            elif i < 16 or i < NF - 1:
                                act.wait_ge(b_pe_q, XG + DUOS * g + 24)
                            else:
                                act.wait_ge(b_pe_pv, DUOS * g + 24)
                            weight(n % 4, 2 + 4 * g + n // 4 + 1, targets(kind, i)[0])
                    if k % 2 == 1 and (k < DUOS - XG or not last):
                        queries(4 + 16 * g + k // 2 + 1, (k % XG) // 2, (k // XG + 1) % 2)
                    act.wait_ge(b_pe_pv, DUOS * g + k + 1)
                    b, i = k // PB, k % PB
                    hi(Oh[:, b % 2, 2 * i:2 * i + 2, :],
                       bank[5][:, 0:KEYS].rearrange("p (h n) -> p h n", h=2)).then_inc(b_a_o, 1)

            with act.Fori(0, XKV - 1) as g:
                group(g, False)
            group(XKV - 1, True)

            act.wait_ge(c_ld, 48)
            act.wait_ge(c_v_g0, 2)
            hi(GTh[:, :, 0:NE], gate_raw[:]).then_inc(c_a_g, 1)
            with act.Fori(0, NB // 2) as c:
                for t in range(2):
                    act.wait_ge(c_pe_x, 2 * c + t + 1)
                    hi(X3h[:, :, t * P:(t + 1) * P],
                       bank[t][:].rearrange("p (k n) -> p k n", k=KC)).then_inc(c_a_x, 1)
                act.wait_ge(c_pe_g, c + 1)
                hi(lgT[:], bank[0][:, 0:KEYS]).then_inc(c_a_g, 1)
                act.wait_ge(c_pe_l, c + 1)
                hi(LTh[:].rearrange("p m n -> p (m n)"), bank[1][:]).then_inc(c_a_l, 1)
                for n in range(IC // 2):
                    act.wait_ge(c_pe_h, 4 * c + n + 1)
                    act.activation(hr[:, n % 2, :], bank[2 + n][:], ACT.Relu).then_inc(c_a_hr, 1)
                    if n == 2:
                        act.wait_ge(c_pe_e, c + 1)
                        hi(ETh[:].rearrange("p m n -> p (m n)"), bank[1][:]).then_inc(c_a_l, 1)
                    act.wait_ge(c_v_h2, 4 * c + n + 1)
                    hi(HBh[:, 2 * n:2 * n + 2, :].rearrange("p m n -> p (m n)"), hq[:, n % 2, :]).then_inc(c_a_h, 1)
                for t in range(2):
                    act.wait_ge(c_pe_y, 4 * c + 3 + t)
                    hi(ysh[:, t, :], bank[6 + t][:]).then_inc(c_a_y, 1)

        @block.vector
        def _(dve):
            def lo(dst, src, hi_part):
                return dve.tensor_tensor(dst, src, f32(hi_part), ALU.subtract)

            dve.memset(f32(Vbdh[:]), 0.0).then_inc(v_c, 1)
            dve.memset(f32(Vbdl[:]), 0.0).then_inc(v_c, 1)
            dve.wait_ge(g_const, 6)
            dve.tensor_copy(ident_r[:], ident[:]).then_inc(v_c, 1)
            dve.tensor_copy(mask_r[:], mask_f[:]).then_inc(v_c, 1)
            dve.wait_ge(ld_x, 16)
            n = 0
            for b in range(NB):
                dve.bn_stats(stats1[:], x_res[:, b, :]).then_inc(v_rt, 1)
                dve.wait_ge(v_rt, 2 * b + 1)
                dve.bn_aggr(mv1[:, b, :], stats1[:]).then_inc(v_rt, 1)
                dve.wait_ge(v_rt, 2 * b + 2)
            dve.tensor_scalar(rstd1[:], mv1[:, :, 1], EPS, None, ALU.add).then_inc(v_st, 3)
            RT0 = 2 * NB
            for n in range(10):
                dve.wait_ge(a_w, n + 1)
                if n < 4:
                    dst, h = SQl[:, n, :], SQh[:, n, :]
                elif n < 6:
                    dst = SKVl[:, 2 * (n - 4):2 * (n - 4) + 2, :].rearrange("p k n -> p (k n)")
                    h = SKVh[:, 2 * (n - 4):2 * (n - 4) + 2, :].rearrange("p k n -> p (k n)")
                else:
                    dst, h = SOl[:, n - 6, :], SOh[:, n - 6, :]
                lo(dst, bank[n % 8][:], h).then_inc(v_w, 1)
            dve.wait_ge(a_w, 11)
            lo(XKl[:], rawXK[:], XKh[:]).then_inc(v_w, 1)
            dve.wait_ge(a_w, 12)
            lo(XVl[:], rawXV[:], XVh[:]).then_inc(v_w, 1)

            def latents(b):
                for t in range(2):
                    dve.wait_ge(a_ht, 2 * b + t + 1)
                    src = bank[7 if t == 0 else 4][:].rearrange("p (k n) -> p k n", k=KC)
                    cols = slice((1 - t) * P, (2 - t) * P)
                    lo(HTl[:, :, cols], src, HTh[:, :, cols]).then_inc(v_htl, 1)

            def keys_values(b):
                for n in range(2):
                    dve.wait_ge(a_kvp, 4 * b + n + 1)
                    lo(KVst[:, 2 * n:2 * n + 2, KEYS:2 * KEYS], bank[5 + n][:].rearrange("p (g n) -> p g n", g=2),
                       KVst[:, 2 * n:2 * n + 2, 0:KEYS]).then_inc(v_kvl, 1)
                for t in range(2):
                    dve.wait_ge(a_kvp, 4 * b + t + 3)
                    lo(KVst[:, :, 3 * KEYS + t * P:3 * KEYS + (t + 1) * P],
                       bank[5 + t][:].rearrange("p (g n) -> p g n", g=XKV),
                       KVst[:, :, 2 * KEYS + t * P:2 * KEYS + (t + 1) * P]).then_inc(v_kvl, 1)

            def norm_stats(src, sem_st):
                dve.drain()
                dve.bn_stats(stats[:], src)
                dve.drain()
                dve.bn_aggr(mv[:], stats[:])
                dve.drain()
                dve.tensor_scalar(var_eps[:], mv[:, 1:2], EPS, None, ALU.add).then_inc(sem_st, 1)

            dve.wait_ge(g_rstd, 1)
            dve.wait_ge(ld_rope, 16)
            cosf, sinf = rope_t[:, 0:SD], rope_t[:, SD:2 * SD]
            HD = SD // 2

            def batch(b, first):
                if not first:
                    dve.wait_ge(pe_xn, b)
                dve.tensor_scalar(xn[:], x_res[:, b, :], mv1[:, b, 0:1], rstd1[:, bass.ds(b, 1)], ALU.subtract,
                                  ALU.mult).then_inc(v_xn, 1)
                dve.wait_ge(a_xn, b + 1)
                lo(xnTl[:], bank[0][:].rearrange("p (k n) -> p k n", k=KC), xnTh[:]).then_inc(v_xnl, 1)
                if not first:
                    latents(b - 1)
                if not first:
                    dve.wait_ge(pe_pt, SKV * b)
                base = RT0 + 6 * b
                for n, (src, t1, t2, nh) in enumerate(((bank[1][:], tq1, tq2, SH),
                                                       (bank[0][:, 0:P], tk[:, 0:P], tk[:, P:2 * P], SKV))):
                    if n == 0:
                        dve.wait_ge(pe_qkv, 2 * b + 1)
                    else:
                        dve.wait_ge(a_v, b + 1)
                    s3 = src.rearrange("p (h d) -> p h d", d=SD)
                    a3 = t1.rearrange("p (h d) -> p h d", d=SD)
                    b3 = t2.rearrange("p (h d) -> p h d", d=SD)
                    dve.tensor_tensor(a3, s3, cosf.unsqueeze(1).to_broadcast([P, nh, SD]), ALU.mult).then_inc(v_rt, 1)
                    dve.tensor_tensor(b3[:, :, 0:HD], s3[:, :, HD:SD],
                                      sinf[:, 0:HD].unsqueeze(1).to_broadcast([P, nh, HD]), ALU.mult).then_inc(v_rt, 1)
                    dve.tensor_tensor(b3[:, :, HD:SD], s3[:, :, 0:HD],
                                      sinf[:, HD:SD].unsqueeze(1).to_broadcast([P, nh, HD]), ALU.mult).then_inc(v_rt, 1)
                vv = [t[:].rearrange("p (j c) -> p j c", c=VBW)[:, :, 0:SD] for t in (Vbdl, Vbdh)]
                lo(vv[0], bank[0][:, P:2 * P].rearrange("p (j d) -> p j d", j=SKV), vv[1]).then_inc(v_vl, 1)
                dve.wait_ge(v_rt, base + 3)
                if not first:
                    dve.wait_ge(pe_qk, 2 * b)
                dve.tensor_tensor(qr[:], tq1, tq2, ALU.add).then_inc(v_qr, 1)
                dve.wait_ge(v_rt, base + 6)
                if not first:
                    dve.wait_ge(pe_pv, b)
                k1, k2 = (tk[:, n * P:(n + 1) * P].rearrange("p (j d) -> p j d", d=SD).unsqueeze(2)
                          .to_broadcast([P, SKV, SG, SD]) for n in range(2))
                dve.tensor_tensor(kr[:].rearrange("p (j g d) -> p j g d", j=SKV, g=SG), k1, k2,
                                  ALU.add).then_inc(v_qr, 1)
                if not first:
                    keys_values(b - 1)
                dve.wait_ge(a_qk, 2 * b + 1)
                lo(QTl[:], bank[2][:].rearrange("p (k n) -> p k n", k=KC), QTh[:]).then_inc(v_qkl, 1)
                dve.wait_ge(a_qk, 2 * b + 2)
                lo(KTl[:], bank[3][:].rearrange("p (k n) -> p k n", k=KC), KTh[:]).then_inc(v_qkl, 1)
                dve.wait_ge(v_qkl, 2 * b + 2)
                if first:
                    dve.wait_ge(g_const, 6 + 2 * SD)
                for m in range(KC):
                    dve.tensor_tensor(Kbdl[:, m, :].rearrange("p (c k) -> p c k", c=SG),
                                      f32(KTl[:, m, :]).unsqueeze(1).to_broadcast([P, SG, P]),
                                      bd_mask[:].unsqueeze(2).to_broadcast([P, SG, P]), ALU.mult).then_inc(v_kbd, 1)

                def maxima(j):
                    dve.wait_ge(pe_s, SKV * b + j + 1)
                    hs = slice(SG * j, SG * j + SG)
                    dve.tensor_reduce(a_max[:, hs], bank[2 + j % 3][:].rearrange("p (c k) -> p c k", c=SG), AX.X,
                                      ALU.max).then_inc(v_mx, 1)
                    dve.wait_ge(v_mx, SKV * b + j + 1)
                    dve.tensor_scalar(a_nb[:, hs], a_max[:, hs], -S_SCALE, None, ALU.mult).then_inc(v_nb, 1)

                maxima(0)
                maxima(1)
                maxima(2)
                for j in range(SKV):
                    dve.wait_ge(a_exp, SKV * b + j + 1)
                    hs = slice(SG * j, SG * j + SG)
                    dve.reciprocal(a_rec[:, hs], a_sum[:, hs]).then_inc(v_rec, 1)
                    if j + 3 < SKV:
                        maxima(j + 3)
                    dve.wait_ge(a_pt, SKV * b + j + 1)
                    lo(PTal[:, j % 2, :], bank[5 + j % 2][:], PTah[:, j % 2, :]).then_inc(v_ptl, 1)
                dve.wait_ge(a_o, b + 1)
                lo(OTl[:], bank[7][:].rearrange("p (k n) -> p k n", k=KC), OTh[:]).then_inc(v_ol, 1)
                dve.wait_ge(pe_wo, b + 1)
                dve.tensor_tensor(x_res[:, b, :], x_res[:, b, :], bank[1][:], ALU.add).then_inc(v_x2, 1)
                norm_stats(x_res[:, b, :], v_st2)
                dve.wait_ge(g_rstd, b + 2)
                if not first:
                    dve.wait_ge(pe_ht, 2 * b)
                dve.tensor_scalar(xn2[:], x_res[:, b, :], mv[:, 0:1], rstd[:], ALU.subtract,
                                  ALU.mult).then_inc(v_xn2, 1)

            batch(0, True)
            with dve.Fori(1, NB) as b:
                batch(b, False)
            latents(NB - 1)
            keys_values(NB - 1)

            def maxima_b(g, k):
                dve.wait_ge(b_pe_s, DUOS * g + k + 1)
                dve.tensor_reduce(b_max[:, k % 4, :], bank[k % 3][:].rearrange("p (h k) -> p h k", h=2), AX.X,
                                  ALU.max).then_inc(b_v_mx, 1)
                dve.wait_ge(b_v_mx, DUOS * g + k + 1)
                dve.tensor_scalar(b_nb[:, k % 4, :], b_max[:, k % 4, :], -X_SCALE, None, ALU.mult).then_inc(b_v_nb, 1)

            def reciprocals(g, k):
                dve.wait_ge(b_a_exp, DUOS * g + k + 1)
                dve.reciprocal(b_rec[:, k % 4, :], b_sum[:, k % 4, :]).then_inc(b_v_rec, 1)

            def queries(count, fill, parity):
                dve.wait_ge(b_a_q, count)
                lo(Ql[:, parity, 2 * fill:2 * fill + 2, :], bank[6][:].rearrange("p (h n) -> p h n", h=2),
                   Qh[:, parity, 2 * fill:2 * fill + 2, :]).then_inc(b_v_q, 1)

            def residual(g, b):
                dve.wait_ge(b_pe_wo, PB * NB * g + PB * b + PB)
                dve.tensor_tensor(x_res[:, b, :], x_res[:, b, :], bank[7][:], ALU.add).then_inc(b_v_x, 1)

            for f in range(4):
                queries(f + 1, f, 0)
            for k in range(2):
                maxima_b(0, k)
            for k in range(2):
                reciprocals(0, k)

            def group(g, last):
                for k in range(DUOS):
                    gg, kk = (g, k + 2) if k + 2 < DUOS else (g + 1, k + 2 - DUOS)
                    ahead = k + 2 < DUOS or not last
                    if ahead:
                        maxima_b(gg, kk)
                    dve.wait_ge(b_a_pt, DUOS * g + k + 1)
                    lo(PTl[:, k % 2, :], bank[3 + k % 2][:], PTh[:, k % 2, :]).then_inc(b_v_pt, 1)
                    if ahead:
                        reciprocals(gg, kk)
                    if k >= PB and k % PB == PB - 1:
                        residual(g, k // PB - 1)
                    if k % 2 == 1 and (k < DUOS - XG or not last):
                        queries(4 + 16 * g + k // 2 + 1, (k % XG) // 2, (k // XG + 1) % 2)
                    dve.wait_ge(b_a_o, DUOS * g + k + 1)
                    b, i = k // PB, k % PB
                    lo(Ol[:, b % 2, 2 * i:2 * i + 2, :], bank[5][:, 0:KEYS].rearrange("p (h n) -> p h n", h=2),
                       Oh[:, b % 2, 2 * i:2 * i + 2, :]).then_inc(b_v_o, 1)
                residual(g, NB - 1)

            with dve.Fori(0, XKV - 1) as g:
                group(g, False)
            group(XKV - 1, True)

            dve.memset(f32(GTh[:]), 0.0).then_inc(c_v_g0, 1)
            dve.memset(f32(GTl[:]), 0.0).then_inc(c_v_g0, 1)
            dve.wait_ge(c_a_g, 1)
            dve.wait_ge(c_v_g0, 2)
            lo(GTl[:, :, 0:NE], gate_raw[:], GTh[:, :, 0:NE]).then_inc(c_v_g0, 1)
            dve.wait_ge(b_v_x, NB * XKV)
            with dve.Fori(0, NB // 2) as c:
                for t in range(2):
                    norm_stats(x_res[:, 2 * c + t, :], c_v_st)
                    dve.wait_ge(c_g_r, 4 * c + t + 1)
                    dve.tensor_scalar(xn3[:, t, :], x_res[:, 2 * c + t, :], mv[:, 0:1], rstd[:], ALU.subtract,
                                      ALU.mult).then_inc(c_v_xn, 1)
                for t in range(2):
                    dve.wait_ge(c_a_x, 2 * c + t + 1)
                    lo(X3l[:, :, t * P:(t + 1) * P], bank[t][:].rearrange("p (k n) -> p k n", k=KC),
                       X3h[:, :, t * P:(t + 1) * P]).then_inc(c_v_x, 1)
                dve.wait_ge(c_a_l, 2 * c + 1)
                lo(LTl[:].rearrange("p m n -> p (m n)"), bank[1][:],
                   LTh[:].rearrange("p m n -> p (m n)")).then_inc(c_v_l, 1)
                for n in range(IC // 2):
                    dve.wait_ge(c_a_hr, 4 * c + n + 1)
                    dve.scalar_tensor_tensor(out=hq[:, n % 2, :], in0=bank[2 + n][:], scalar=0.0, in1=hr[:, n % 2, :],
                                             op0=ALU.max, op1=ALU.mult).then_inc(c_v_h2, 1)
                    if n == 2:
                        dve.wait_ge(c_a_l, 2 * c + 2)
                        lo(ETl[:].rearrange("p m n -> p (m n)"), bank[1][:],
                           ETh[:].rearrange("p m n -> p (m n)")).then_inc(c_v_l, 1)
                    dve.wait_ge(c_a_h, 4 * c + n + 1)
                    lo(HBl[:, 2 * n:2 * n + 2, :].rearrange("p m n -> p (m n)"), hq[:, n % 2, :],
                       HBh[:, 2 * n:2 * n + 2, :].rearrange("p m n -> p (m n)")).then_inc(c_v_h, 1)
                    if n == 1:
                        dve.wait_ge(c_pe_gt, c + 1)
                        dve.tensor_copy(logits[:], bank[0][:, KEYS:2 * KEYS].rearrange(
                            "p (t n) -> p t n", t=2)[:, :, 0:NE])
                        dve.drain()
                        for t in range(2):
                            dve.max(top8[:, t, :], logits[:, t, :])
                        dve.drain()
                        dve.tensor_tensor(route[:], top8[:, :, 0], top8[:, :, 1], ALU.add).then_inc(c_v_r, 1)
                for t in range(2):
                    dve.wait_ge(c_a_y, 2 * c + t + 1)
                    dve.wait_ge(c_v_r, c + 1)
                    dve.scalar_tensor_tensor(out=yy[:, t, :], in0=bank[t][:], scalar=route[:, t:t + 1],
                                             in1=ysh[:, t, :], op0=ALU.mult, op1=ALU.add).then_inc(c_v_y, 1)
                    norm_stats(yy[:, t, :], c_v_st)
                    dve.wait_ge(c_g_r, 4 * c + 2 + t + 1)
                    dve.scalar_tensor_tensor(out=yy[:, t, :], in0=yy[:, t, :], scalar=mv[:, 0:1], in1=gam[:],
                                             op0=ALU.subtract, op1=ALU.mult).then_inc(c_v_n, 1)
                    dve.wait_ge(c_v_n, 6 * c + 3 * t + 1)
                    dve.wait_ge(c_g_xb, 2 * c + t + 1)
                    dve.wait_ge(c_out[t], 16 * c)
                    dve.scalar_tensor_tensor(out=yo[:, t, :], in0=yy[:, t, :], scalar=rstd[:], in1=xb[:, t, :],
                                             op0=ALU.mult, op1=ALU.add).then_inc(c_v_n, 2)


def rope_tables():
    f = np.float32
    inv = (f(1.0) / np.power(f(500000.0), np.arange(0, SD, 2, dtype=np.float32) / f(SD))).astype(f)
    wavelen = (f(2.0 * np.pi) / inv).astype(f)
    lo, hi, factor, ctx = f(1.0), f(4.0), f(32.0), f(1024)
    freq = np.where(wavelen > ctx / lo, inv / factor, inv).astype(f)
    smooth = ((ctx / wavelen - lo) / (hi - lo)).astype(f)
    smoothed = ((f(1.0) - smooth) * freq / factor + smooth * freq).astype(f)
    medium = ~(wavelen < ctx / lo) & ~(wavelen > ctx / hi)
    freq = np.where(medium, smoothed, freq).astype(f)
    ang = (np.arange(P, dtype=np.float32)[:, None] * freq[None, :]).astype(f)
    cos, sin = np.cos(ang), np.sin(ang)
    return np.concatenate([cos, cos, -sin, sin], axis=1).astype(f)


_INS = ["x", "ctx_4096", "L0_attn_Wq", "L0_attn_Wk", "L0_attn_Wv", "L0_attn_Wo", "L0_xattn_Wq", "L0_xattn_Wk",
        "L0_xattn_Wv", "L0_xattn_Wo", "L0_ffn_gate_w", "L0_ffn_up_w", "L0_ffn_down_w", "L0_ffn_fc1_w",
        "L0_ffn_fc2_w", "L0_ffn_expert_w", "L0_ffn_ln_gamma", "L0_ffn_ln_beta"]


def kernel(**inputs):
    import numpy as _np
    import concourse.bacc as _bacc
    from concourse import mybir as _mybir
    from concourse.bass_utils import run_bass_kernel_spmd as _run

    nc = _bacc.Bacc("TRN2", target_bir_lowering=False, num_devices=1)
    arrays, args = {}, []
    for name in _INS:
        a = _np.ascontiguousarray(inputs[name])
        arrays[f"in_{name}_dram"] = a
        args.append(nc.dram_tensor(f"in_{name}_dram", a.shape, _mybir.dt.from_np(a.dtype), kind="ExternalInput").ap())
    table = rope_tables()
    arrays["rope_dram"] = table
    args.append(nc.dram_tensor("rope_dram", table.shape, _mybir.dt.from_np(table.dtype), kind="ExternalInput").ap())
    args.append(nc.dram_tensor("out_0_dram", (NB, P, D), F32, kind="ExternalOutput").ap())
    decoder_layer(nc, *args)
    r = _run(nc, [arrays], core_ids=[0])
    return r.results[0]["out_0_dram"]
```

```python
from contextlib import ExitStack

import numpy as np

import concourse.bass as bass
from concourse import mybir

F32 = mybir.dt.float32
F32R = mybir.dt.float32r
ALU = mybir.AluOpType
ACT = mybir.ActivationFunctionType
AX = mybir.AxisListType

P = 128
NB = 8
D = 512
KC = D // P
EPS = 1e-5

SH, SKV, SD = 32, 8, 16
SG = SH // SKV
S_SCALE = 1.0 / float(np.sqrt(SD))
MASKED = -float(2.0 ** 126)

XH, XKV, XD = 32, 4, 128
XG = XH // XKV
KEYS = 2 * P
X_SCALE = 1.0 / float(np.sqrt(XD))
DUOS = NB * XG // 2
PB = XG // 2

INT, LAT, NE = 1024, 256, 8
IC, LC = INT // P, LAT // P

KB = 1024


def decoder_layer(nc, x, ctx, s_wq, s_wk, s_wv, s_wo, x_wq, x_wk, x_wv, x_wo, gate_w, up_w, down_w,
                  fc1_w, fc2_w, expert_w, gamma, beta, rope, out):
    with ExitStack() as stack:
        def sem(name):
            return stack.enter_context(nc.semaphore(name))

        at, cursor = {}, 16512
        for region, size in (("X", 16 * KB), ("XT", 32 * KB), ("WQ", 32 * KB), ("WO", 32 * KB),
                             ("Q", 32 * KB), ("O", 16 * KB), ("KV", 12 * KB), ("P", 8 * KB),
                             ("PT", 8 * KB), ("ST", 8 * KB), ("F", 9 * KB + 512), ("C", 2 * KB)):
            at[region] = cursor
            cursor += size

        def sb(name, region, kb, shape, dt=F32):
            return nc.alloc_sbuf_tensor_at(name, [P, *shape], dt, offset=at[region] + int(kb * KB))

        def f32(ap):
            return ap.bitcast(F32)

        x_res = sb("x_res", "X", 0, [NB, D])
        ident = sb("ident", "C", 0, [P])
        ident_r = sb("ident_r", "C", 0.5, [P], F32R)
        rope_t = sb("rope_t", "C", 1, [2 * SD])
        stats = sb("stats", "C", 1.125, [6])
        mv = sb("mv", "C", 1.25, [2])
        rstd = sb("rstd", "C", 1.375, [1])
        half = sb("half", "C", 1.4375, [1])
        var_eps = sb("var_eps", "C", 1.5, [1])
        bd_mask = sb("bd_mask", "C", 1.53125, [SG])
        top8 = sb("top8", "C", 1.5625, [2, NE])
        route = sb("route", "C", 1.6875, [2])
        mv1 = sb("mv1", "C", 1.71875, [NB, 2])
        rstd1 = sb("rstd1", "C", 1.8125, [NB])
        stats1 = sb("stats1", "C", 1.875, [6])

        XTh = sb("XTh", "XT", 0, [KC, NB * P], F32R)
        XTl = sb("XTl", "XT", 16, [KC, NB * P], F32R)

        SQh = sb("SQh", "WO", 0, [KC, D], F32R)
        SQl = sb("SQl", "WO", 8, [KC, D], F32R)
        SOh = sb("SOh", "WO", 16, [SG, D], F32R)
        SOl = sb("SOl", "WO", 24, [SG, D], F32R)
        XKh = sb("XKh", "Q", 0, [KC, D], F32R)
        XKl = sb("XKl", "Q", 8, [KC, D], F32R)
        XVh = sb("XVh", "Q", 16, [KC, D], F32R)
        XVl = sb("XVl", "Q", 24, [KC, D], F32R)
        SKVh = sb("SKVh", "KV", 0, [KC, 2 * P], F32R)
        SKVl = sb("SKVl", "KV", 4, [KC, 2 * P], F32R)
        xnTh = sb("xnTh", "KV", 8, [KC, P], F32R)
        xnTl = sb("xnTl", "KV", 10, [KC, P], F32R)
        KVst = sb("KVst", "O", 0, [XKV, 1024], F32R)
        Kbdh = sb("Kbdh", "WQ", 0, [KC, D], F32R)
        QTh = sb("QTh", "WQ", 8, [KC, P], F32R)
        KTh = sb("KTh", "WQ", 10, [KC, P], F32R)
        HTh = sb("HTh", "WQ", 12, [KC, KEYS], F32R)
        Kbdl = sb("Kbdl", "WQ", 16, [KC, D], F32R)
        QTl = sb("QTl", "WQ", 24, [KC, P], F32R)
        KTl = sb("KTl", "WQ", 26, [KC, P], F32R)
        HTl = sb("HTl", "WQ", 28, [KC, KEYS], F32R)
        Pa = sb("Pa", "P", 0, [3, D])
        cx = sb("cx", "P", 6, [D])
        PTah = sb("PTah", "PT", 0, [2, D], F32R)
        PTal = sb("PTal", "PT", 4, [2, D], F32R)
        xn = sb("xn", "ST", 0, [D])
        xn2 = sb("xn2", "ST", 2, [D])
        kr = sb("kr", "ST", 4, [D])
        mask_r = sb("mask_r", "ST", 6.5, [P], F32R)
        a_max = sb("a_max", "ST", 7, [SH])
        a_nb = sb("a_nb", "ST", 7.125, [SH])
        a_sum = sb("a_sum", "ST", 7.25, [SH])
        a_rec = sb("a_rec", "ST", 7.375, [SH])
        mask_f = sb("mask_f", "ST", 7.5, [P])
        VBW = P + SD
        Vbdh = sb("Vbdh", "F", 0, [SKV * VBW], F32R)
        Vbdl = sb("Vbdl", "F", 4.5, [SKV * VBW], F32R)
        OTh, OTl = PTah[:, 0, :], PTal[:, 0, :]

        temp_h = sb("temp_h", "XT", 0, [KC, NB * P])
        temp_l = sb("temp_l", "XT", 16, [KC, NB * P])
        last2, last1 = slice((NB - 2) * P, (NB - 1) * P), slice((NB - 1) * P, NB * P)
        rope_q1, rope_q2, q_rot = temp_h[:, :, last1], temp_l[:, :, last1], temp_l[:, :, last2]
        rope_k1, rope_k2 = temp_h[:, 0, last2], temp_h[:, 1, last2]
        q_first = sb("q_first", "PT", 0, [KC, P])
        rawQ = sb("rawQ", "O", 0, [KC, D])
        rawO = sb("rawO", "O", 8, [KC, D])
        rawOg = sb("rawOg", "XT", 0, [KC, D])
        rawKV = sb("rawKV", "P", 0, [2, D])
        rawXK = sb("rawXK", "XT", 8, [KC, D])
        rawXV = sb("rawXV", "XT", 16, [KC, D])

        WQh = sb("WQh", "WQ", 0, [XG, KC, P], F32R)
        WQl = sb("WQl", "WQ", 16, [XG, KC, P], F32R)
        WOh = sb("WOh", "WO", 0, [XG, D], F32R)
        WOl = sb("WOl", "WO", 16, [XG, D], F32R)
        Qh = sb("Qh", "Q", 0, [2, XG, KEYS], F32R)
        Ql = sb("Ql", "Q", 16, [2, XG, KEYS], F32R)
        Oh = sb("Oh", "O", 0, [2, XG, P], F32R)
        Ol = sb("Ol", "O", 8, [2, XG, P], F32R)
        KV = sb("KV", "KV", 0, [3, 1024], F32R)
        Pb = sb("Pb", "P", 0, [4, 2, KEYS])
        PTh = sb("PTh", "PT", 0, [2, D], F32R)
        PTl = sb("PTl", "PT", 4, [2, D], F32R)
        raw = sb("raw", "ST", 0, [4, D])
        b_max = sb("b_max", "F", 8, [4, 2])
        b_nb = sb("b_nb", "F", 8.0625, [4, 2])
        b_sum = sb("b_sum", "F", 8.125, [4, 2])
        b_rec = sb("b_rec", "F", 8.1875, [4, 2])

        UPh = sb("UPh", "WQ", 0, [KC, INT], F32R)
        UPl = sb("UPl", "WQ", 16, [KC, INT], F32R)
        DNh = sb("DNh", "XT", 0, [IC, D], F32R)
        DNl = sb("DNl", "XT", 16, [IC, D], F32R)
        F1h = sb("F1h", "Q", 0, [KC, LAT], F32R)
        F2h = sb("F2h", "Q", 4, [LC, D], F32R)
        HBh = sb("HBh", "Q", 8, [IC, KEYS], F32R)
        F1l = sb("F1l", "Q", 16, [KC, LAT], F32R)
        F2l = sb("F2l", "Q", 20, [LC, D], F32R)
        HBl = sb("HBl", "Q", 24, [IC, KEYS], F32R)
        EXh = sb("EXh", "KV", 8, [LC, LAT], F32R)
        EXl = sb("EXl", "KV", 10, [LC, LAT], F32R)
        xn3 = sb("xn3", "F", 0, [2, D])
        GTh = sb("GTh", "F", 4, [KC, P], F32R)
        GTl = sb("GTl", "F", 6, [KC, P], F32R)
        gate_raw = sb("gate_raw", "F", 8.5, [KC, NE])
        X3h = sb("X3h", "KV", 0, [KC, KEYS], F32R)
        X3l = sb("X3l", "KV", 4, [KC, KEYS], F32R)
        gam = sb("gam", "WO", 0, [D])
        bet = sb("bet", "WO", 2, [D])
        ysh = sb("ysh", "WO", 12, [2, D])
        yy = sb("yy", "WO", 16, [2, D])
        yo = sb("yo", "WO", 20, [2, D])
        xb = sb("xb", "WO", 24, [2, D])
        lgT = sb("lgT", "WO", 28, [KEYS])
        logits = sb("logits", "WO", 29.25, [2, NE])
        hr = sb("hr", "O", 0, [2, D])
        hq = sb("hq", "O", 4, [2, D])
        LTh = sb("LTh", "O", 8, [LC, KEYS], F32R)
        LTl = sb("LTl", "O", 10, [LC, KEYS], F32R)
        ETh = sb("ETh", "O", 12, [LC, KEYS], F32R)
        ETl = sb("ETl", "O", 14, [LC, KEYS], F32R)

        kv_scratch = nc.dram_tensor("kv_scratch", (XKV, NB, P, 1024), F32, kind="Internal").ap()

        bank = [stack.enter_context(nc.psum_tensor(f"bank{i}", [P, 512], F32)) for i in range(8)]

        def split3(pe, dst, lh, ll, rh, rl, start, stop):
            pe.matmul(dst, lh, rh, start=start, stop=False)
            pe.matmul(dst, lh, rl, start=False, stop=False)
            return pe.matmul(dst, ll, rh, start=False, stop=stop)

        ld_x0, ld_x, ld_q, ld_kv, ld_o, ld_xk, ld_xv, ld_rope, ld_cx, st_kv, st_xt = (sem(n) for n in (
            "ld_x0", "ld_x", "ld_q", "ld_kv", "ld_o", "ld_xk", "ld_xv", "ld_rope", "ld_cx", "st_kv", "st_xt"))
        g_const, g_rstd, g_kbd, g_norm = (sem(n) for n in ("g_const", "g_rstd", "g_kbd", "g_norm"))
        pe_w, pe_xn, pe_ht, pe_qkv, pe_kvp, pe_qk, pe_s, pe_pt, pe_pv, pe_wo = (sem(n) for n in (
            "pe_w", "pe_xn", "pe_ht", "pe_qkv", "pe_kvp", "pe_qk", "pe_s", "pe_pt", "pe_pv", "pe_wo"))
        a_w, a_xn, a_ht, a_v, a_kvp, a_qk, a_exp, a_pt, a_o = (sem(n) for n in (
            "a_w", "a_xn", "a_ht", "a_v", "a_kvp", "a_qk", "a_exp", "a_pt", "a_o"))
        a_wog = sem("a_wog")
        v_c, v_w, v_st, v_xn, v_xnl, v_htl, v_rt, v_qr, v_vl, v_kvl, v_qkl, v_kbd, v_mx, v_nb, \
            v_rec, v_ptl, v_ol, v_x2, v_st2, v_xn2 = (sem(n) for n in (
                "v_c", "v_w", "v_st", "v_xn", "v_xnl", "v_htl", "v_rt", "v_qr", "v_vl", "v_kvl",
                "v_qkl", "v_kbd", "v_mx", "v_nb", "v_rec", "v_ptl", "v_ol", "v_x2", "v_st2", "v_xn2"))
        b_ld = [sem(f"b_ld{i}") for i in range(4)]
        b_kv = [sem(f"b_kv{i}") for i in range(3)]
        b_pe_q, b_pe_s, b_pe_pt, b_pe_pv, b_pe_wo = (sem(n) for n in (
            "b_pe_q", "b_pe_s", "b_pe_pt", "b_pe_pv", "b_pe_wo"))
        b_a_w, b_a_q, b_a_exp, b_a_pt, b_a_o = (sem(n) for n in (
            "b_a_w", "b_a_q", "b_a_exp", "b_a_pt", "b_a_o"))
        b_v_mx, b_v_nb, b_v_rec, b_v_pt, b_v_q, b_v_o, b_v_x = (sem(n) for n in (
            "b_v_mx", "b_v_nb", "b_v_rec", "b_v_pt", "b_v_q", "b_v_o", "b_v_x"))
        b_g_w, b_g_norm = sem("b_g_w"), sem("b_g_norm")
        ld_gate, c_ld, c_out = sem("ld_gate"), sem("c_ld"), [sem("c_out0"), sem("c_out1")]
        c_pe_x, c_pe_g, c_pe_gt, c_pe_h, c_pe_l, c_pe_e, c_pe_y = (sem(n) for n in (
            "c_pe_x", "c_pe_g", "c_pe_gt", "c_pe_h", "c_pe_l", "c_pe_e", "c_pe_y"))
        c_a_x, c_a_g, c_a_hr, c_a_h, c_a_l, c_a_y = (sem(n) for n in (
            "c_a_x", "c_a_g", "c_a_hr", "c_a_h", "c_a_l", "c_a_y"))
        c_v_g0, c_v_st, c_v_xn, c_v_x, c_v_h2, c_v_h, c_v_l, c_v_r, c_v_y, c_v_n = (
            sem(n) for n in ("c_v_g0", "c_v_st", "c_v_xn", "c_v_x", "c_v_h2", "c_v_h", "c_v_l",
                             "c_v_r", "c_v_y", "c_v_n"))
        c_g_r, c_g_xb = sem("c_g_r"), sem("c_g_xb")

        W0 = XG
        WPG = 2 * XG
        ffn_chunks = (
            [(up_w[kc * P:(kc + 1) * P, n * D:(n + 1) * D], UPh[:, kc, n * D:(n + 1) * D],
              UPl[:, kc, n * D:(n + 1) * D]) for kc in range(KC) for n in range(INT // D)]
            + [(down_w[c * P:(c + 1) * P, :], DNh[:, c, :], DNl[:, c, :]) for c in range(IC)]
            + [(fc1_w[c * 2 * P:(c + 1) * 2 * P, :].rearrange("(k p) n -> p k n", p=P),
                F1h[:, 2 * c:2 * c + 2, :], F1l[:, 2 * c:2 * c + 2, :]) for c in range(KC // 2)]
            + [(fc2_w[c * P:(c + 1) * P, :], F2h[:, c, :], F2l[:, c, :]) for c in range(LC)]
            + [(expert_w.rearrange("(k p) n -> p k n", p=P), EXh[:, :, :], EXl[:, :, :])])
        NF = len(ffn_chunks)

        def wq_src(g, h):
            return x_wq.rearrange("(k p) (h n) -> h p k n", p=P, n=XD)[XG * g + h]

        def wo_src(g, h):
            return x_wo.rearrange("(h p) n -> h p n", p=XD)[XG * g + h]

        def chunk_steps(last):
            steps = [(h // 2, "wo", h) for h in range(XG)]
            if not last:
                steps += [(17 + h, "wq", h) for h in range(XG)]
            else:
                steps += [(17 + i, "ffn", i) for i in range(8)]
                steps += [(25 + (i - 8) // 2, "ffn", i) for i in range(8, NF)]
            return steps

        def raw_view(slot, dst):
            v = raw[:, slot, :]
            if len(dst.shape) == 3:
                v = v.rearrange("p (k n) -> p k n", k=dst.shape[1])
            return v

        def targets(kind, i):
            if kind == "wo":
                return WOh[:, i, :], WOl[:, i, :]
            if kind == "wq":
                return WQh[:, i, :, :], WQl[:, i, :, :]
            return ffn_chunks[i][1:]

        WBANK = (2, 3, 4, 5, 6, 7, 2, 3, 4, 5)

        LN3_STEPS = (22, 24)
        VBANK = (5, 1)

        block = stack.enter_context(nc.Block())

        @block.sync
        def _(sp):
            sp.dma_start(x_res[:, 0, :], x[0]).then_inc(ld_x0, 16)
            sp.dma_start(rawQ[:], s_wq.rearrange("(m p) n -> p m n", p=P)).then_inc(ld_q, 16)
            sp.dma_start(rawKV[:, 0, :], s_wk).then_inc(ld_kv, 16)
            sp.dma_start(rawKV[:, 1, :], s_wv).then_inc(ld_kv, 16)
            sp.dma_start(rope_t[:], rope).then_inc(ld_rope, 16)
            sp.dma_start(rawO[:], s_wo.rearrange("(m p) n -> p m n", p=P)).then_inc(ld_o, 16)
            sp.dma_start(rawXK[:], x_wk.rearrange("(k p) n -> p k n", p=P)).then_inc(ld_xk, 16)
            sp.dma_start(rawXV[:], x_wv.rearrange("(k p) n -> p k n", p=P)).then_inc(ld_xv, 16)
            sp.dma_start(x_res[:, 1:, :], x[1:].rearrange("b t d -> t b d")).then_inc(ld_x, 16)
            sp.dma_start(cx[:], ctx[0]).then_inc(ld_cx, 16)
            sp.sem_inc(st_xt, 32)
            sp.sem_inc(st_kv, 16)

            def keep(b):
                sp.wait_ge(v_htl, 2 * b + 2)
                for src, dst in ((HTh, XTh), (HTl, XTl)):
                    sp.dma_start(f32(dst[:].rearrange("p k (b n) -> p b k n", b=NB)[:, b]),
                                 f32(src[:, :, P:KEYS])).then_inc(st_xt, 16)

            def store_kv(b):
                sp.wait_ge(v_kvl, 4 * b + 8)
                sp.dma_start(kv_scratch[:, b].rearrange("g p n -> p g n"), f32(KVst[:])).then_inc(st_kv, 16)

            with sp.Fori(0, NB - 1) as b:
                next_ctx = sp.snap(b + 1)
                sp.wait_ge(pe_ht, 2 * b + 1)
                sp.dma_start(cx[:], ctx[next_ctx]).then_inc(ld_cx, 16)
                keep(b)
                store_kv(b)
            keep(NB - 1)
            sp.wait_ge(pe_ht, 2 * NB)
            for h in range(XG):
                if h >= 4:
                    sp.wait_ge(b_g_w, h - 3)
                sp.dma_start(raw_view(h % 4, WQh[:, h, :, :]), wq_src(0, h)).then_inc(b_ld[h % 4], 16)
            sp.wait_ge(pe_pv, NB)
            sp.dma_start(gate_raw[:], gate_w.rearrange("(k p) n -> p k n", p=P)).then_inc(ld_gate, 16)
            store_kv(NB - 1)
            sp.wait_ge(st_kv, 16 * NB + 16)
            sp.wait_ge(pe_qkv, 2 * NB)
            for b in range(3):
                sp.dma_start(f32(KV[:, b, :]), kv_scratch[0, b]).then_inc(b_kv[b], 16)

            def group(g, last):
                kv_loads = [(4 * (b - 3) + 4, g, b) for b in range(3, NB)]
                if not last:
                    kv_loads += [(24, g + 1, 2), (28, g + 1, 0), (32, g + 1, 1)]
                w_loads = [(max(step - 2, 0), kind, i) for step, kind, i in chunk_steps(last)]
                for k in range(DUOS):
                    for n, (step, kind, i) in enumerate(w_loads):
                        if step == k:
                            sp.wait_ge(b_g_w, W0 + WPG * g + n - 3)
                            dst = targets(kind, i)[0]
                            src = (wo_src(g, i) if kind == "wo" else wq_src(g + 1, i) if kind == "wq"
                                   else ffn_chunks[i][0])
                            sp.dma_start(raw_view(n % 4, dst), src).then_inc(b_ld[n % 4], 16)
                    for done, gg, b in kv_loads:
                        if done == k + 1:
                            n = NB * gg + b if last else sp.snap(NB * gg + b)
                            sp.wait_ge(b_pe_pv, DUOS * g + done)
                            sp.dma_start(f32(KV[:, b % 3, :]), kv_scratch.rearrange("g b p n -> (g b) p n")[n]
                                         ).then_inc(b_kv[b % 3], 16)

            with sp.Fori(0, XKV - 1) as g:
                group(g, False)
            group(XKV - 1, True)
            sp.wait_ge(b_pe_wo, PB * NB * XKV + 1)
            sp.dma_start(gam[:], gamma.partition_broadcast(P)).then_inc(c_ld, 16)
            sp.dma_start(bet[:], beta.partition_broadcast(P)).then_inc(c_ld, 16)
            sp.sem_inc(c_out[0], 16)
            sp.sem_inc(c_out[1], 16)
            with sp.Fori(0, NB // 2) as c:
                for t in range(2):
                    tile = sp.snap(2 * c + t)
                    sp.wait_ge(c_v_n, 6 * c + 3 * t + 9)
                    sp.dma_start(out[tile], yo[:, t, :]).then_inc(c_out[t], 16)
            sp.wait_ge(c_out[0], 16 * (NB // 2) + 16)
            sp.wait_ge(c_out[1], 16 * (NB // 2) + 16)

        @block.gpsimd
        def _(gp):
            gp.memset(ident[:], 0.0).then_inc(g_const, 1)
            gp.memset(mask_f[:], 0.0).then_inc(g_const, 1)
            gp.memset(bd_mask[:], 0.0).then_inc(g_const, 1)
            gp.memset(half[:], -0.5).then_inc(g_const, 1)
            gp.wait_ge(g_const, 4)
            gp.affine_select(out=ident[:], in_=ident[:], compare_op=ALU.not_equal, fill=1.0, base=0,
                             pattern=[[-1, P]], channel_multiplier=1).then_inc(g_const, 1)
            gp.affine_select(out=mask_f[:], in_=mask_f[:], compare_op=ALU.is_ge, fill=MASKED, base=0,
                             pattern=[[-1, P]], channel_multiplier=1).then_inc(g_const, 1)
            n = 6
            for base in range(2):
                for r in range(SD):
                    gp.wait_ge(g_const, n)
                    gp.affine_select(out=bd_mask[:], in_=bd_mask[:], compare_op=ALU.not_equal, fill=1.0,
                                     base=-(64 * base + r), pattern=[[-SD, SG]],
                                     channel_multiplier=1).then_inc(g_const, 1)
                    n += 1
            gp.wait_ge(v_st, 1)
            gp.tensor_tensor(rstd1[:, 0:1], rstd1[:, 0:1], half[:], ALU.pow).then_inc(g_rstd, 1)

            def diagonal_keys(b):
                for m in range(KC):
                    gp.wait_ge(a_qk, 2 * b + 2)
                    src = f32(KTh[:, m, :]).unsqueeze(1).to_broadcast([P, SG, P])
                    gp.tensor_tensor(Kbdh[:, m, :].rearrange("p (c k) -> p c k", c=SG), src,
                                     bd_mask[:].unsqueeze(2).to_broadcast([P, SG, P]), ALU.mult).then_inc(g_kbd, 1)

            def batch(b, last):
                for j in range(SKV):
                    gp.wait_ge(v_rec, SKV * b + j + 1)
                    pj = Pa[:, j % 3, :].rearrange("p (c k) -> p c k", c=SG)
                    gp.tensor_tensor(pj, pj, a_rec[:, SG * j:SG * j + SG].unsqueeze(2).to_broadcast([P, SG, P]),
                                     ALU.mult).then_inc(g_norm, 1)
                gp.wait_ge(v_st2, b + 1)
                gp.tensor_tensor(rstd[:], var_eps[:], half[:], ALU.pow).then_inc(g_rstd, 1)
                if not last:
                    diagonal_keys(b + 1)

            diagonal_keys(0)
            gp.wait_ge(v_st, 2)
            gp.tensor_tensor(rstd1[:, 1:NB], rstd1[:, 1:NB], half[:].to_broadcast([P, NB - 1]),
                             ALU.pow).then_inc(g_rstd, 1)
            with gp.Fori(0, NB - 1) as b:
                batch(b, False)
            batch(NB - 1, True)

            def lo_part(slot, count, dst, hi):
                gp.wait_ge(b_a_w, count)
                gp.tensor_tensor(dst, raw_view(slot, dst), f32(hi), ALU.subtract).then_inc(b_g_w, 1)

            def norm(g, k):
                gp.wait_ge(b_v_rec, DUOS * g + k + 1)
                pk = Pb[:, k % 4, :, :]
                gp.tensor_tensor(pk, pk, b_rec[:, k % 4, :].unsqueeze(2).to_broadcast([P, 2, KEYS]),
                                 ALU.mult).then_inc(b_g_norm, 1)

            def inv_std(n):
                gp.wait_ge(c_v_st, n)
                gp.tensor_tensor(rstd[:], var_eps[:], half[:], ALU.pow).then_inc(c_g_r, 1)

            for h in range(XG):
                lo_part(h % 4, h + 1, WQl[:, h, :, :], WQh[:, h, :, :])
            norm(0, 0)
            norm(0, 1)

            def group(g, last):
                chunks = chunk_steps(last)
                for k in range(DUOS):
                    if k + 2 < DUOS:
                        norm(g, k + 2)
                    elif not last:
                        norm(g + 1, k + 2 - DUOS)
                    if last and k in LN3_STEPS:
                        inv_std(LN3_STEPS.index(k) + 1)
                    for n, (step, kind, i) in enumerate(chunks):
                        if step == k:
                            hi, lo = targets(kind, i)
                            lo_part(n % 4, W0 + WPG * g + n + 1, lo, hi)

            with gp.Fori(0, XKV - 1) as g:
                group(g, False)
            group(XKV - 1, True)

            def pair(c, last):
                for t in range(2):
                    gp.wait_ge(c_ld, 32)
                    gp.wait_ge(c_v_n, 6 * c + 6)
                    gp.tensor_tensor(xb[:, t, :], x_res[:, 2 * c + t, :], bet[:], ALU.add).then_inc(c_g_xb, 1)
                for t in range(2 if last else 4):
                    inv_std(4 * c + t + 3)

            with gp.Fori(0, NB // 2 - 1) as c:
                pair(c, False)
            pair(NB // 2 - 1, True)

        @block.tensor
        def _(pe):
            def turn_weights(n):
                for m in range(KC):
                    if n < 4:
                        src = rawQ[:, m, n * P:(n + 1) * P]
                    elif n < 6:
                        kc = 2 * (n - 4) + m // 2
                        src = rawKV[:, m % 2, kc * P:(kc + 1) * P]
                    else:
                        src = rawOg[:, m, (n - 6) * P:(n - 5) * P]
                    op = pe.transpose(bank[WBANK[n]][:, m * P:(m + 1) * P], src, ident[:])
                op.then_inc(pe_w, 1)

            def turn_xn(b):
                pe.wait_ge(v_xn, b + 1)
                for kc in range(KC):
                    op = pe.transpose(bank[0][:, kc * P:(kc + 1) * P], xn[:, kc * P:(kc + 1) * P], ident[:])
                op.then_inc(pe_xn, 1)

            def q_product(kcs):
                for kc in kcs:
                    op = split3(pe, bank[1][:], xnTh[:, kc, :], xnTl[:, kc, :], SQh[:, kc, :], SQl[:, kc, :],
                                kc == 0, kc == KC - 1)
                if KC - 1 in kcs:
                    op.then_inc(pe_qkv, 1)

            def kv_product():
                for kc in range(KC):
                    op = split3(pe, bank[0][:, 0:2 * P], xnTh[:, kc, :], xnTl[:, kc, :], SKVh[:, kc, :],
                                SKVl[:, kc, :], kc == 0, kc == KC - 1)
                op.then_inc(pe_qkv, 1)

            def turn_qk(b, q):
                pe.wait_ge(v_qr, 2 * b + 2)
                for m in range(KC):
                    op = pe.transpose(bank[2][:, m * P:(m + 1) * P], q[:, m, :], ident[:])
                op.then_inc(pe_qk, 1)
                for m in range(KC):
                    op = pe.transpose(bank[3][:, m * P:(m + 1) * P], kr[:, m * P:(m + 1) * P], ident[:])
                op.then_inc(pe_qk, 1)

            def turn_context(b):
                pe.wait_ge(ld_cx, 16 * b + 16)
                for kc in range(KC):
                    op = pe.transpose(bank[1][:, kc * P:(kc + 1) * P], cx[:, kc * P:(kc + 1) * P], ident[:])
                op.then_inc(pe_ht, 1)

            def cross_values(t):
                for kc in range(KC):
                    op = split3(pe, bank[VBANK[t]][:], HTh[:, kc, t * P:(t + 1) * P], HTl[:, kc, t * P:(t + 1) * P],
                                XVh[:, kc, :], XVl[:, kc, :], kc == 0, kc == KC - 1)
                op.then_inc(pe_kvp, 1)

            def cross_keys(n):
                for gg in range(2):
                    g = 2 * n + gg
                    dst = bank[6 + n][:, gg * KEYS:(gg + 1) * KEYS]
                    for kc in range(KC):
                        op = split3(pe, dst, XKh[:, kc, g * XD:(g + 1) * XD], XKl[:, kc, g * XD:(g + 1) * XD],
                                    HTh[:, kc, :], HTl[:, kc, :], kc == 0, kc == KC - 1)
                op.then_inc(pe_kvp, 1)

            def scores(b, j):
                bk = bank[2 + j % 3]
                m, r = j // 2, 64 * (j % 2)
                if j >= 3:
                    pe.wait_ge(a_exp, SKV * b + j - 2)
                elif j < 2:
                    pe.wait_ge(v_qkl, 2 * b + 2)
                pe.wait_ge(g_kbd, KC * b + m + 1)
                pe.wait_ge(v_kbd, KC * b + m + 1)
                pe.matmul(bk[:].rearrange("p (c k) -> p c k", c=SG), ident_r[:],
                          mask_r[:].unsqueeze(1).to_broadcast([P, SG, P]), start=True, stop=False)
                rows = slice(r, r + 64)
                split3(pe, bk[:], QTh[rows, m, :], QTl[rows, m, :], Kbdh[rows, m, :], Kbdl[rows, m, :],
                       False, True).then_inc(pe_s, 1)

            def batch(b, last):
                def turn(j):
                    pe.wait_ge(g_norm, SKV * b + j + 1)
                    if j >= 2:
                        pe.wait_ge(v_ptl, SKV * b + j - 1)
                    elif j == 0:
                        pe.wait_ge(v_kvl, 4 * b + 3)
                    for c in range(SG):
                        op = pe.transpose(bank[5 + j % 2][:, c * P:(c + 1) * P],
                                          Pa[:, j % 3, c * P:(c + 1) * P], ident[:])
                    op.then_inc(pe_pt, 1)

                def values(j):
                    pe.wait_ge(v_ptl, SKV * b + j + 1)
                    if j == 0:
                        pe.wait_ge(v_vl, b + 1)
                        pe.wait_ge(a_v, b + 1)
                    op = split3(pe, bank[7][:], Vbdh[:, j * P:(j + 1) * P], Vbdl[:, j * P:(j + 1) * P],
                                PTah[:, j % 2, :], PTal[:, j % 2, :], j == 0, j == SKV - 1)
                    if j == SKV - 1:
                        op.then_inc(pe_pv, 1)

                for j in range(SKV):
                    turn(j)
                    if j + 3 < SKV:
                        scores(b, j + 3)
                    if j >= 1:
                        values(j - 1)
                    if j == 1:
                        pe.wait_ge(v_kvl, 4 * b + 4)
                        turn_context(b)
                    if last:
                        continue
                    if j == 1:
                        pe.wait_ge(v_vl, b + 1)
                        turn_xn(b + 1)
                    elif j == 3:
                        pe.wait_ge(v_xnl, b + 2)
                        pe.wait_ge(v_htl, 2 * b + 1)
                        q_product((0, 1))
                    elif j == 4:
                        q_product((2, 3))
                    elif j == 5:
                        kv_product()
                values(SKV - 1)
                if not last:
                    pe.wait_ge(a_exp, SKV * b + SKV)
                    turn_qk(b + 1, q_rot)
                pe.wait_ge(v_ol, b + 1)
                for g in range(SG):
                    op = split3(pe, bank[7][:], OTh[:, g * P:(g + 1) * P], OTl[:, g * P:(g + 1) * P], SOh[:, g, :],
                                SOl[:, g, :], g == 0, g == SG - 1)
                op.then_inc(pe_wo, 1)
                if last:
                    pe.wait_ge(v_htl, 2 * b + 1)
                cross_values(0)
                pe.wait_ge(v_xn2, b + 1)
                pe.wait_ge(a_exp, SKV * b + SKV)
                for kc in range(KC):
                    op = pe.transpose(bank[4][:, kc * P:(kc + 1) * P], xn2[:, kc * P:(kc + 1) * P], ident[:])
                op.then_inc(pe_ht, 1)
                pe.wait_ge(v_htl, 2 * b + 2)
                cross_keys(0)
                cross_keys(1)
                if not last:
                    for j in range(3):
                        scores(b + 1, j)
                cross_values(1)

            pe.wait_ge(g_const, 6)
            pe.wait_ge(ld_q, 16)
            for n in range(4):
                turn_weights(n)
            pe.wait_ge(ld_kv, 32)
            for n in range(4, 6):
                turn_weights(n)
            turn_xn(0)
            pe.wait_ge(v_w, 6)
            pe.wait_ge(v_xnl, 1)
            q_product(range(KC))
            kv_product()
            pe.wait_ge(a_wog, KC)
            for n in range(6, 10):
                turn_weights(n)
            pe.wait_ge(v_w, 10)
            turn_qk(0, q_first)
            pe.wait_ge(v_w, 12)
            pe.wait_ge(v_c, 4)
            for j in range(3):
                scores(0, j)
            with pe.Fori(0, NB - 1) as b:
                batch(b, False)
            batch(NB - 1, True)

            def queries(g_count, head, pair):
                pe.wait_ge(b_g_w, g_count)
                for kc in range(KC):
                    op = split3(pe, bank[6][:, (head % 2) * KEYS:(head % 2 + 1) * KEYS],
                                WQh[:, head, kc, :], WQl[:, head, kc, :],
                                XTh[:, kc, pair * KEYS:(pair + 1) * KEYS], XTl[:, kc, pair * KEYS:(pair + 1) * KEYS],
                                kc == 0, kc == KC - 1)
                op.then_inc(b_pe_q, 1)

            def scores_b(g, k):
                b, i = k // PB, k % PB
                slot = b % 3
                if i == 0:
                    pe.wait_ge(b_kv[slot], 16 * ((3 if slot < 2 else 2) * g + b // 3 + 1))
                if b % 2 == 0:
                    pe.wait_ge(b_v_q, 4 + 16 * g + 4 * (b // 2) - 4 + i + 1)
                for h in range(2):
                    head = 2 * i + h
                    op = split3(pe, bank[k % 3][:, h * KEYS:(h + 1) * KEYS],
                                Qh[:, (b // 2) % 2, head, (b % 2) * P:(b % 2 + 1) * P],
                                Ql[:, (b // 2) % 2, head, (b % 2) * P:(b % 2 + 1) * P],
                                KV[:, slot, 0:KEYS], KV[:, slot, KEYS:2 * KEYS], True, True)
                op.then_inc(b_pe_s, 1)

            def out_piece(g, b, i):
                pe.wait_ge(b_v_o, DUOS * g + PB * b + i + 2)
                pe.wait_ge(b_g_w, W0 + WPG * g + 2 * i + 2)
                if i == 0:
                    pe.wait_ge(b_v_x, NB * g + b + 1)
                for h in range(2):
                    head = 2 * i + h
                    op = split3(pe, bank[7][:], Oh[:, b % 2, head, :], Ol[:, b % 2, head, :], WOh[:, head, :],
                                WOl[:, head, :], head == 0, head == XG - 1)
                op.then_inc(b_pe_wo, 1)

            def turn_x3(c):
                for t in range(2):
                    pe.wait_ge(c_v_xn, 2 * c + t + 1)
                    for kc in range(KC):
                        op = pe.transpose(bank[2 + t][:, kc * P:(kc + 1) * P], xn3[:, t, kc * P:(kc + 1) * P],
                                          ident[:])
                    op.then_inc(c_pe_x, 1)

            pe.sem_inc(b_pe_wo, 1)
            pe.wait_ge(st_xt, 32 * NB + 32)
            pe.wait_ge(v_kvl, 4 * NB + 4)
            for h in range(XG):
                if h % 2 == 0 and h:
                    pe.wait_ge(b_v_q, h // 2)
                queries(h + 1, h, 0)
            scores_b(0, 0)
            scores_b(0, 1)

            def group(g, last):
                for k in range(DUOS):
                    if k + 2 < DUOS or not last:
                        if k + 2 < DUOS:
                            pe.wait_ge(b_a_exp, DUOS * g + max(k, 1))
                            scores_b(g, k + 2)
                        else:
                            pe.wait_ge(b_a_exp, DUOS * g + k + 1)
                            scores_b(g + 1, k + 2 - DUOS)
                    pe.wait_ge(b_g_norm, DUOS * g + k + 1)
                    pe.wait_ge(b_v_pt, DUOS * g + k + 1)
                    for c in range(2):
                        for h in range(2):
                            op = pe.transpose(bank[3 + k % 2][:, c * KEYS + h * P:c * KEYS + (h + 1) * P],
                                              Pb[:, k % 4, h, c * P:(c + 1) * P], ident[:])
                    op.then_inc(b_pe_pt, 1)
                    if k >= PB:
                        out_piece(g, k // PB - 1, k % PB)
                    if k < DUOS - XG or not last:
                        if k % 2 == 0:
                            pe.wait_ge(b_v_q, 4 + 16 * g + k // 2)
                        if k < DUOS - XG:
                            queries(W0 + WPG * g, k % XG, k // XG + 1)
                        else:
                            queries(W0 + WPG * g + XG + k % XG + 1, k % XG, 0)
                    pe.wait_ge(b_v_pt, DUOS * g + k + 3)
                    pe.wait_ge(b_v_o, DUOS * g + k + 1)
                    slot = (k // PB) % 3
                    for c in range(2):
                        vh = KV[:, slot, 2 * KEYS + c * P:2 * KEYS + (c + 1) * P]
                        vl = KV[:, slot, 3 * KEYS + c * P:3 * KEYS + (c + 1) * P]
                        op = split3(pe, bank[5][:, 0:KEYS], vh, vl, PTh[:, k % 2, c * KEYS:(c + 1) * KEYS],
                                    PTl[:, k % 2, c * KEYS:(c + 1) * KEYS], c == 0, c == 1)
                    op.then_inc(b_pe_pv, 1)
                if last:
                    turn_x3(0)
                for i in range(PB):
                    out_piece(g, NB - 1, i)

            with pe.Fori(0, XKV - 1) as g:
                group(g, False)
            group(XKV - 1, True)

            pe.wait_ge(b_g_w, W0 + WPG * (XKV - 1) + XG + NF)
            pe.wait_ge(c_v_g0, 3)

            def pair(c, last):
                pe.wait_ge(c_v_x, 2 * c + 2)
                pe.wait_ge(c_v_y, 2 * c + 1)
                for kc in range(KC):
                    op = split3(pe, bank[0][:, 0:KEYS], GTh[:, kc, :], GTl[:, kc, :], X3h[:, kc, :], X3l[:, kc, :],
                                kc == 0, kc == KC - 1)
                op.then_inc(c_pe_g, 1)
                pe.wait_ge(c_v_y, 2 * c + 2)
                for m in range(LC):
                    for kc in range(KC):
                        op = split3(pe, bank[1][:, m * KEYS:(m + 1) * KEYS], F1h[:, kc, m * P:(m + 1) * P],
                                    F1l[:, kc, m * P:(m + 1) * P], X3h[:, kc, :], X3l[:, kc, :], kc == 0, kc == KC - 1)
                op.then_inc(c_pe_l, 1)
                for n in range(IC // 2):
                    for mm in range(2):
                        m = 2 * n + mm
                        for kc in range(KC):
                            op = split3(pe, bank[2 + n][:, mm * KEYS:(mm + 1) * KEYS], UPh[:, kc, m * P:(m + 1) * P],
                                        UPl[:, kc, m * P:(m + 1) * P], X3h[:, kc, :], X3l[:, kc, :],
                                        kc == 0, kc == KC - 1)
                    op.then_inc(c_pe_h, 1)
                    if n == 0:
                        pe.wait_ge(c_a_g, c + 2)
                        for t in range(2):
                            op = pe.transpose(bank[0][:, KEYS + t * P:KEYS + (t + 1) * P],
                                              lgT[:, t * P:(t + 1) * P], ident[:])
                        op.then_inc(c_pe_gt, 1)
                    if n == 1:
                        pe.wait_ge(c_v_l, 2 * c + 1)
                        for m in range(LC):
                            for kc in range(LC):
                                op = split3(pe, bank[1][:, m * KEYS:(m + 1) * KEYS], EXh[:, kc, m * P:(m + 1) * P],
                                            EXl[:, kc, m * P:(m + 1) * P], LTh[:, kc, :], LTl[:, kc, :],
                                            kc == 0, kc == LC - 1)
                        op.then_inc(c_pe_e, 1)
                pe.wait_ge(c_v_l, 2 * c + 2)
                pe.wait_ge(c_v_r, c + 1)
                for t in range(2):
                    for kc in range(LC):
                        op = split3(pe, bank[t][:], ETh[:, kc, t * P:(t + 1) * P], ETl[:, kc, t * P:(t + 1) * P],
                                    F2h[:, kc, :], F2l[:, kc, :], kc == 0, kc == LC - 1)
                    op.then_inc(c_pe_y, 1)
                if not last:
                    pe.wait_ge(c_v_h, 4 * c + 2)
                    turn_x3(c + 1)
                pe.wait_ge(b_v_x, NB * XKV + 1)
                for t in range(2):
                    for m in range(IC):
                        if t == 0 and m % 2 == 0:
                            pe.wait_ge(c_v_h, 4 * c + m // 2 + 1)
                        op = split3(pe, bank[6 + t][:], HBh[:, m, t * P:(t + 1) * P], HBl[:, m, t * P:(t + 1) * P],
                                    DNh[:, m, :], DNl[:, m, :], m == 0, m == IC - 1)
                    op.then_inc(c_pe_y, 1)

            with pe.Fori(0, NB // 2 - 1) as c:
                pair(c, False)
            pair(NB // 2 - 1, True)

        @block.scalar
        def _(act):
            def hi(dst, src):
                return act.activation(dst, src, ACT.Copy)

            def weight_a(n):
                act.wait_ge(pe_w, n + 1)
                if n < 4:
                    dst = SQh[:, n, :]
                elif n < 6:
                    dst = SKVh[:, 2 * (n - 4):2 * (n - 4) + 2, :].rearrange("p k n -> p (k n)")
                else:
                    dst = SOh[:, n - 6, :]
                hi(dst, bank[WBANK[n]][:]).then_inc(a_w, 1)

            def xn_hi(b):
                act.wait_ge(pe_xn, b + 1)
                hi(xnTh[:], bank[0][:].rearrange("p (k n) -> p k n", k=KC)).then_inc(a_xn, 1)

            def values_hi(b):
                act.wait_ge(pe_qkv, 2 * b + 2)
                hi(Vbdh[:].rearrange("p (j c) -> p j c", c=VBW)[:, :, 0:SD],
                   bank[0][:, P:2 * P].rearrange("p (j d) -> p j d", j=SKV)).then_inc(a_v, 1)

            def qk_hi(b):
                act.wait_ge(pe_qk, 2 * b + 1)
                hi(QTh[:], bank[2][:].rearrange("p (k n) -> p k n", k=KC)).then_inc(a_qk, 1)
                act.wait_ge(pe_qk, 2 * b + 2)
                hi(KTh[:], bank[3][:].rearrange("p (k n) -> p k n", k=KC)).then_inc(a_qk, 1)

            def context_hi(b):
                act.wait_ge(pe_ht, 2 * b + 1)
                hi(HTh[:, :, 0:P], bank[1][:].rearrange("p (k n) -> p k n", k=KC)).then_inc(a_ht, 1)

            def latents_hi(b):
                act.wait_ge(pe_ht, 2 * b + 2)
                act.wait_ge(st_xt, 32 * b + 32)
                hi(HTh[:, :, P:KEYS], bank[4][:].rearrange("p (k n) -> p k n", k=KC)).then_inc(a_ht, 1)

            def cross_values_hi(b, t):
                act.wait_ge(pe_kvp, 4 * b + 3 * t + 1)
                hi(KVst[:, :, 2 * KEYS + t * P:2 * KEYS + (t + 1) * P],
                   bank[VBANK[t]][:].rearrange("p (g n) -> p g n", g=XKV)).then_inc(a_kvp, 1)

            def cross_keys_hi(b, n):
                act.wait_ge(pe_kvp, 4 * b + n + 2)
                hi(KVst[:, 2 * n:2 * n + 2, 0:KEYS],
                   bank[6 + n][:].rearrange("p (g n) -> p g n", g=2)).then_inc(a_kvp, 1)

            def probs(b, j):
                act.wait_ge(v_nb, SKV * b + j + 1)
                if j >= 3:
                    act.wait_ge(pe_pt, SKV * b + j - 2)
                for c in range(SG):
                    h = SG * j + c
                    op = act.activation(Pa[:, j % 3, c * P:(c + 1) * P], bank[2 + j % 3][:, c * P:(c + 1) * P],
                                        ACT.Exp, bias=a_nb[:, h:h + 1], scale=S_SCALE, accum_out=a_sum[:, h:h + 1])
                op.then_inc(a_exp, 1)

            def batch(b, last):
                for j in range(SKV):
                    if j + 2 < SKV:
                        probs(b, j + 2)
                    act.wait_ge(pe_pt, SKV * b + j + 1)
                    hi(PTah[:, j % 2, :], bank[5 + j % 2][:]).then_inc(a_pt, 1)
                    if j == 1:
                        context_hi(b)
                    if j == 2 and not last:
                        xn_hi(b + 1)
                act.wait_ge(pe_pv, b + 1)
                hi(OTh, bank[7][:]).then_inc(a_o, 1)
                if not last:
                    qk_hi(b + 1)
                    values_hi(b + 1)
                act.wait_ge(st_kv, 16 * b + 16)
                cross_values_hi(b, 0)
                latents_hi(b)
                cross_keys_hi(b, 0)
                cross_keys_hi(b, 1)
                if not last:
                    probs(b + 1, 0)
                    probs(b + 1, 1)
                cross_values_hi(b, 1)

            for n in range(6):
                weight_a(n)
            xn_hi(0)
            act.wait_ge(ld_o, 16)
            for m in range(KC):
                act.activation(rawOg[:, m, :].rearrange("p (g j d) -> p g j d", g=SG, j=SKV),
                               rawO[:, m, :].rearrange("p (j g d) -> p g j d", j=SKV, g=SG),
                               ACT.Copy).then_inc(a_wog, 1)
            for n in range(6, 10):
                weight_a(n)
            act.wait_ge(ld_xk, 16)
            hi(XKh[:], rawXK[:]).then_inc(a_w, 1)
            qk_hi(0)
            act.wait_ge(v_c, 2)
            values_hi(0)
            act.wait_ge(ld_xv, 16)
            hi(XVh[:], rawXV[:]).then_inc(a_w, 1)
            probs(0, 0)
            probs(0, 1)
            with act.Fori(0, NB - 1) as b:
                batch(b, False)
            batch(NB - 1, True)

            def weight(slot, loads, hi_dst):
                act.wait_ge(b_ld[slot], 16 * loads)
                hi(hi_dst, raw_view(slot, hi_dst)).then_inc(b_a_w, 1)

            def probs_b(g, k):
                act.wait_ge(b_v_nb, DUOS * g + k + 1)
                for h in range(2):
                    op = act.activation(Pb[:, k % 4, h, :], bank[k % 3][:, h * KEYS:(h + 1) * KEYS], ACT.Exp,
                                        bias=b_nb[:, k % 4, h:h + 1], scale=X_SCALE,
                                        accum_out=b_sum[:, k % 4, h:h + 1])
                op.then_inc(b_a_exp, 1)

            def queries(count, fill, parity):
                act.wait_ge(b_pe_q, 2 * count)
                hi(Qh[:, parity, 2 * fill:2 * fill + 2, :],
                   bank[6][:].rearrange("p (h n) -> p h n", h=2)).then_inc(b_a_q, 1)

            act.wait_ge(pe_kvp, 4 * NB)
            act.wait_ge(st_xt, 32 * NB + 32)
            for h in range(XG):
                weight(h % 4, h // 4 + 1, WQh[:, h, :, :])
            for f in range(4):
                queries(f + 1, f, 0)
            probs_b(0, 0)
            probs_b(0, 1)
            act.wait_ge(ld_gate, 16)
            act.wait_ge(c_v_g0, 2)
            hi(GTh[:, :, 0:NE], gate_raw[:]).then_inc(c_a_g, 1)

            def group(g, last):
                chunks = chunk_steps(last)
                for k in range(DUOS):
                    act.wait_ge(b_pe_pt, DUOS * g + k + 1)
                    hi(PTh[:, k % 2, :], bank[3 + k % 2][:]).then_inc(b_a_pt, 1)
                    if k + 2 < DUOS:
                        probs_b(g, k + 2)
                    elif not last:
                        probs_b(g + 1, k + 2 - DUOS)
                    for n, (step, kind, i) in enumerate(chunks):
                        if step == k:
                            if kind == "wo":
                                act.wait_ge(b_pe_wo, PB * NB * g + 1)
                            elif kind == "wq" or i < 8:
                                act.wait_ge(b_pe_q, XG + DUOS * g + 17 + i)
                            elif i < 16 or i < NF - 1:
                                act.wait_ge(b_pe_q, XG + DUOS * g + 24)
                            else:
                                act.wait_ge(b_pe_pv, DUOS * g + 24)
                            weight(n % 4, 2 + 4 * g + n // 4 + 1, targets(kind, i)[0])
                    if k % 2 == 1 and (k < DUOS - XG or not last):
                        queries(4 + 16 * g + k // 2 + 1, (k % XG) // 2, (k // XG + 1) % 2)
                    act.wait_ge(b_pe_pv, DUOS * g + k + 1)
                    b, i = k // PB, k % PB
                    hi(Oh[:, b % 2, 2 * i:2 * i + 2, :],
                       bank[5][:, 0:KEYS].rearrange("p (h n) -> p h n", h=2)).then_inc(b_a_o, 1)

            with act.Fori(0, XKV - 1) as g:
                group(g, False)
            group(XKV - 1, True)

            def x3_hi(c):
                for t in range(2):
                    act.wait_ge(c_pe_x, 2 * c + t + 1)
                    hi(X3h[:, :, t * P:(t + 1) * P],
                       bank[2 + t][:].rearrange("p (k n) -> p k n", k=KC)).then_inc(c_a_x, 1)

            def pair(c, last):
                act.wait_ge(c_pe_g, c + 1)
                hi(lgT[:], bank[0][:, 0:KEYS]).then_inc(c_a_g, 1)
                act.wait_ge(c_pe_l, c + 1)
                hi(LTh[:].rearrange("p m n -> p (m n)"), bank[1][:]).then_inc(c_a_l, 1)
                for n in range(IC // 2):
                    act.wait_ge(c_pe_h, 4 * c + n + 1)
                    act.activation(hr[:, n % 2, :], bank[2 + n][:], ACT.Relu).then_inc(c_a_hr, 1)
                    if n == 2:
                        act.wait_ge(c_pe_e, c + 1)
                        hi(ETh[:].rearrange("p m n -> p (m n)"), bank[1][:]).then_inc(c_a_l, 1)
                    act.wait_ge(c_v_h2, 4 * c + n + 1)
                    hi(HBh[:, 2 * n:2 * n + 2, :].rearrange("p m n -> p (m n)"), hq[:, n % 2, :]).then_inc(c_a_h, 1)
                if not last:
                    x3_hi(c + 1)
                for t in range(2):
                    act.wait_ge(c_pe_y, 4 * c + 3 + t)
                    hi(ysh[:, t, :], bank[6 + t][:]).then_inc(c_a_y, 1)

            x3_hi(0)
            with act.Fori(0, NB // 2 - 1) as c:
                pair(c, False)
            pair(NB // 2 - 1, True)

        @block.vector
        def _(dve):
            def lo(dst, src, hi_part):
                return dve.tensor_tensor(dst, src, f32(hi_part), ALU.subtract)

            dve.memset(f32(Vbdh[:]), 0.0).then_inc(v_c, 1)
            dve.memset(f32(Vbdl[:]), 0.0).then_inc(v_c, 1)
            dve.wait_ge(g_const, 6)
            dve.tensor_copy(ident_r[:], ident[:]).then_inc(v_c, 1)
            dve.tensor_copy(mask_r[:], mask_f[:]).then_inc(v_c, 1)

            def ln1_stats(b):
                dve.bn_stats(stats1[:], x_res[:, b, :])
                dve.drain()
                dve.bn_aggr(mv1[:, b, :], stats1[:])
                dve.drain()

            def weight_a(n):
                dve.wait_ge(a_w, n + 1)
                if n < 4:
                    dst, h = SQl[:, n, :], SQh[:, n, :]
                elif n < 6:
                    dst = SKVl[:, 2 * (n - 4):2 * (n - 4) + 2, :].rearrange("p k n -> p (k n)")
                    h = SKVh[:, 2 * (n - 4):2 * (n - 4) + 2, :].rearrange("p k n -> p (k n)")
                else:
                    dst, h = SOl[:, n - 6, :], SOh[:, n - 6, :]
                lo(dst, bank[WBANK[n]][:], h).then_inc(v_w, 1)

            def norm_stats(src, sem_st):
                dve.drain()
                dve.bn_stats(stats[:], src)
                dve.drain()
                dve.bn_aggr(mv[:], stats[:])
                dve.drain()
                dve.tensor_scalar(var_eps[:], mv[:, 1:2], EPS, None, ALU.add).then_inc(sem_st, 1)

            cosf, sinf = rope_t[:, 0:SD], rope_t[:, SD:2 * SD]
            HD = SD // 2

            def ln1(b):
                dve.tensor_scalar(xn[:], x_res[:, b, :], mv1[:, b, 0:1], rstd1[:, bass.ds(b, 1)], ALU.subtract,
                                  ALU.mult).then_inc(v_xn, 1)

            def ln1_lo(b):
                dve.wait_ge(a_xn, b + 1)
                lo(xnTl[:], bank[0][:].rearrange("p (k n) -> p k n", k=KC), xnTh[:]).then_inc(v_xnl, 1)

            def rotate(src, t1, t2, m, nh):
                s4, a4, b4 = (t.rearrange("p (m h d) -> p m h d", m=m, d=SD) if len(t.shape) == 2 else
                              t.rearrange("p m (h d) -> p m h d", d=SD) for t in (src, t1, t2))
                cos4 = cosf.unsqueeze(1).unsqueeze(1).to_broadcast([P, m, nh, SD])
                sin4 = [sinf[:, n * HD:(n + 1) * HD].unsqueeze(1).unsqueeze(1).to_broadcast([P, m, nh, HD])
                        for n in range(2)]
                dve.tensor_tensor(a4, s4, cos4, ALU.mult).then_inc(v_rt, 1)
                dve.tensor_tensor(b4[:, :, :, 0:HD], s4[:, :, :, HD:SD], sin4[0], ALU.mult).then_inc(v_rt, 1)
                dve.tensor_tensor(b4[:, :, :, HD:SD], s4[:, :, :, 0:HD], sin4[1], ALU.mult).then_inc(v_rt, 1)

            def rope_q(b, t1, t2, q):
                dve.wait_ge(pe_qkv, 2 * b + 1)
                rotate(bank[1][:], t1, t2, KC, SH // KC)
                dve.wait_ge(v_rt, 6 * b + 3)
                dve.tensor_tensor(q, t1, t2, ALU.add).then_inc(v_qr, 1)

            def rope_k(b, t1, t2):
                dve.wait_ge(pe_qkv, 2 * b + 2)
                rotate(bank[0][:, 0:P], t1, t2, 1, SKV)
                dve.wait_ge(v_rt, 6 * b + 6)
                k1, k2 = (t.rearrange("p (j d) -> p j d", d=SD).unsqueeze(2).to_broadcast([P, SKV, SG, SD])
                          for t in (t1, t2))
                dve.tensor_tensor(kr[:].rearrange("p (j g d) -> p j g d", j=SKV, g=SG), k1, k2,
                                  ALU.add).then_inc(v_qr, 1)

            def values_lo(b):
                dve.wait_ge(a_v, b + 1)
                vv = [t[:].rearrange("p (j c) -> p j c", c=VBW)[:, :, 0:SD] for t in (Vbdl, Vbdh)]
                lo(vv[0], bank[0][:, P:2 * P].rearrange("p (j d) -> p j d", j=SKV), vv[1]).then_inc(v_vl, 1)

            def qk_lo(b):
                dve.wait_ge(a_qk, 2 * b + 1)
                lo(QTl[:], bank[2][:].rearrange("p (k n) -> p k n", k=KC), QTh[:]).then_inc(v_qkl, 1)
                dve.wait_ge(a_qk, 2 * b + 2)
                lo(KTl[:], bank[3][:].rearrange("p (k n) -> p k n", k=KC), KTh[:]).then_inc(v_qkl, 1)

            def diagonal_keys(b):
                dve.wait_ge(v_qkl, 2 * b + 2)
                for m in range(KC):
                    dve.tensor_tensor(Kbdl[:, m, :].rearrange("p (c k) -> p c k", c=SG),
                                      f32(KTl[:, m, :]).unsqueeze(1).to_broadcast([P, SG, P]),
                                      bd_mask[:].unsqueeze(2).to_broadcast([P, SG, P]), ALU.mult).then_inc(v_kbd, 1)

            def latents(b, t):
                dve.wait_ge(a_ht, 2 * b + t + 1)
                src = bank[4 if t else 1][:].rearrange("p (k n) -> p k n", k=KC)
                cols = slice(t * P, (t + 1) * P)
                lo(HTl[:, :, cols], src, HTh[:, :, cols]).then_inc(v_htl, 1)

            def cross_values_lo(b, t):
                dve.wait_ge(a_kvp, 4 * b + 3 * t + 1)
                lo(KVst[:, :, 3 * KEYS + t * P:3 * KEYS + (t + 1) * P],
                   bank[VBANK[t]][:].rearrange("p (g n) -> p g n", g=XKV),
                   KVst[:, :, 2 * KEYS + t * P:2 * KEYS + (t + 1) * P]).then_inc(v_kvl, 1)

            def cross_keys_lo(b, n):
                dve.wait_ge(a_kvp, 4 * b + n + 2)
                lo(KVst[:, 2 * n:2 * n + 2, KEYS:2 * KEYS], bank[6 + n][:].rearrange("p (g n) -> p g n", g=2),
                   KVst[:, 2 * n:2 * n + 2, 0:KEYS]).then_inc(v_kvl, 1)

            def maxima(b, j):
                dve.wait_ge(pe_s, SKV * b + j + 1)
                hs = slice(SG * j, SG * j + SG)
                dve.tensor_reduce(a_max[:, hs], bank[2 + j % 3][:].rearrange("p (c k) -> p c k", c=SG), AX.X,
                                  ALU.max).then_inc(v_mx, 1)
                dve.wait_ge(v_mx, SKV * b + j + 1)
                dve.tensor_scalar(a_nb[:, hs], a_max[:, hs], -S_SCALE, None, ALU.mult).then_inc(v_nb, 1)

            def reciprocals_a(b, j):
                dve.wait_ge(a_exp, SKV * b + j + 1)
                hs = slice(SG * j, SG * j + SG)
                dve.reciprocal(a_rec[:, hs], a_sum[:, hs]).then_inc(v_rec, 1)

            def batch(b, last):
                if not last:
                    ln1(b + 1)
                reciprocals_a(b, 1)
                for j in range(SKV):
                    if j + 3 < SKV:
                        maxima(b, j + 3)
                    dve.wait_ge(a_pt, SKV * b + j + 1)
                    lo(PTal[:, j % 2, :], bank[5 + j % 2][:], PTah[:, j % 2, :]).then_inc(v_ptl, 1)
                    if j + 2 < SKV:
                        reciprocals_a(b, j + 2)
                    if j == 1:
                        latents(b, 0)
                    if last:
                        continue
                    if j == 2:
                        ln1_lo(b + 1)
                    if j == 5:
                        rope_q(b + 1, rope_q1, rope_q2, q_rot)
                    if j == 6:
                        rope_k(b + 1, rope_k1, rope_k2)
                dve.wait_ge(a_o, b + 1)
                lo(OTl, bank[7][:], OTh).then_inc(v_ol, 1)
                if not last:
                    qk_lo(b + 1)
                dve.wait_ge(pe_wo, b + 1)
                dve.tensor_tensor(x_res[:, b, :], x_res[:, b, :], bank[7][:], ALU.add).then_inc(v_x2, 1)
                norm_stats(x_res[:, b, :], v_st2)
                dve.wait_ge(g_rstd, b + 3)
                dve.tensor_scalar(xn2[:], x_res[:, b, :], mv[:, 0:1], rstd[:], ALU.subtract,
                                  ALU.mult).then_inc(v_xn2, 1)
                cross_values_lo(b, 0)
                latents(b, 1)
                if not last:
                    diagonal_keys(b + 1)
                cross_keys_lo(b, 0)
                cross_keys_lo(b, 1)
                if not last:
                    values_lo(b + 1)
                    maxima(b + 1, 0)
                    maxima(b + 1, 1)
                    maxima(b + 1, 2)
                    reciprocals_a(b + 1, 0)
                cross_values_lo(b, 1)

            dve.wait_ge(ld_x0, 16)
            ln1_stats(0)
            dve.tensor_scalar(rstd1[:, 0:1], mv1[:, 0:1, 1], EPS, None, ALU.add).then_inc(v_st, 1)
            dve.wait_ge(g_rstd, 1)
            ln1(0)
            for n in range(6):
                weight_a(n)
            ln1_lo(0)
            dve.wait_ge(ld_rope, 16)
            rope_q(0, Pa[:, 0, :], Pa[:, 1, :], q_first[:].rearrange("p m n -> p (m n)"))
            rope_k(0, Pa[:, 2, 0:P], Pa[:, 2, P:2 * P])
            for n in range(6, 10):
                weight_a(n)
            qk_lo(0)
            values_lo(0)
            dve.wait_ge(g_const, 6 + 2 * SD)
            diagonal_keys(0)
            dve.wait_ge(a_w, 11)
            lo(XKl[:], rawXK[:], XKh[:]).then_inc(v_w, 1)
            dve.wait_ge(a_w, 12)
            lo(XVl[:], rawXV[:], XVh[:]).then_inc(v_w, 1)
            dve.wait_ge(ld_x, 16)
            for b in range(1, NB):
                ln1_stats(b)
            dve.tensor_scalar(rstd1[:, 1:NB], mv1[:, 1:NB, 1], EPS, None, ALU.add).then_inc(v_st, 1)
            dve.wait_ge(g_rstd, 2)
            dve.sem_inc(v_kvl, 4)
            maxima(0, 0)
            maxima(0, 1)
            maxima(0, 2)
            reciprocals_a(0, 0)
            with dve.Fori(0, NB - 1) as b:
                batch(b, False)
            batch(NB - 1, True)

            def maxima_b(g, k):
                dve.wait_ge(b_pe_s, DUOS * g + k + 1)
                dve.tensor_reduce(b_max[:, k % 4, :], bank[k % 3][:].rearrange("p (h k) -> p h k", h=2), AX.X,
                                  ALU.max).then_inc(b_v_mx, 1)
                dve.wait_ge(b_v_mx, DUOS * g + k + 1)
                dve.tensor_scalar(b_nb[:, k % 4, :], b_max[:, k % 4, :], -X_SCALE, None, ALU.mult).then_inc(b_v_nb, 1)

            def reciprocals(g, k):
                dve.wait_ge(b_a_exp, DUOS * g + k + 1)
                dve.reciprocal(b_rec[:, k % 4, :], b_sum[:, k % 4, :]).then_inc(b_v_rec, 1)

            def queries(count, fill, parity):
                dve.wait_ge(b_a_q, count)
                lo(Ql[:, parity, 2 * fill:2 * fill + 2, :], bank[6][:].rearrange("p (h n) -> p h n", h=2),
                   Qh[:, parity, 2 * fill:2 * fill + 2, :]).then_inc(b_v_q, 1)

            def residual(g, b):
                dve.wait_ge(b_pe_wo, PB * NB * g + PB * b + PB + 1)
                dve.tensor_tensor(x_res[:, b, :], x_res[:, b, :], bank[7][:], ALU.add).then_inc(b_v_x, 1)

            dve.memset(f32(GTh[:]), 0.0).then_inc(c_v_g0, 1)
            dve.memset(f32(GTl[:]), 0.0).then_inc(c_v_g0, 1)
            dve.wait_ge(c_v_g0, 2)
            dve.sem_inc(b_v_pt, 2)
            dve.sem_inc(b_v_o, 1)
            dve.sem_inc(b_v_x, 1)

            def ln3(c, t, n):
                dve.wait_ge(c_g_r, n)
                dve.tensor_scalar(xn3[:, t, :], x_res[:, 2 * c + t, :], mv[:, 0:1], rstd[:], ALU.subtract,
                                  ALU.mult).then_inc(c_v_xn, 1)

            def x3_lo(c):
                for t in range(2):
                    dve.wait_ge(c_a_x, 2 * c + t + 1)
                    lo(X3l[:, :, t * P:(t + 1) * P], bank[2 + t][:].rearrange("p (k n) -> p k n", k=KC),
                       X3h[:, :, t * P:(t + 1) * P]).then_inc(c_v_x, 1)

            for f in range(4):
                queries(f + 1, f, 0)
            for k in range(2):
                maxima_b(0, k)
            for k in range(2):
                reciprocals(0, k)
            dve.wait_ge(c_a_g, 1)
            lo(GTl[:, :, 0:NE], gate_raw[:], GTh[:, :, 0:NE]).then_inc(c_v_g0, 1)

            def group(g, last):
                for k in range(DUOS):
                    gg, kk = (g, k + 2) if k + 2 < DUOS else (g + 1, k + 2 - DUOS)
                    ahead = k + 2 < DUOS or not last
                    if ahead:
                        maxima_b(gg, kk)
                    dve.wait_ge(b_a_pt, DUOS * g + k + 1)
                    lo(PTl[:, k % 2, :], bank[3 + k % 2][:], PTh[:, k % 2, :]).then_inc(b_v_pt, 1)
                    if ahead:
                        reciprocals(gg, kk)
                    if k >= PB and k % PB == PB - 1:
                        residual(g, k // PB - 1)
                    if k % 2 == 1 and (k < DUOS - XG or not last):
                        queries(4 + 16 * g + k // 2 + 1, (k % XG) // 2, (k // XG + 1) % 2)
                    dve.wait_ge(b_a_o, DUOS * g + k + 1)
                    b, i = k // PB, k % PB
                    lo(Ol[:, b % 2, 2 * i:2 * i + 2, :], bank[5][:, 0:KEYS].rearrange("p (h n) -> p h n", h=2),
                       Oh[:, b % 2, 2 * i:2 * i + 2, :]).then_inc(b_v_o, 1)
                    if last:
                        if k - 2 in LN3_STEPS:
                            ln3(0, LN3_STEPS.index(k - 2), LN3_STEPS.index(k - 2) + 1)
                        if k in LN3_STEPS:
                            norm_stats(x_res[:, LN3_STEPS.index(k), :], c_v_st)
                if last:
                    x3_lo(0)
                residual(g, NB - 1)

            with dve.Fori(0, XKV - 1) as g:
                group(g, False)
            group(XKV - 1, True)

            def pair(c, last):
                dve.wait_ge(c_a_l, 2 * c + 1)
                lo(LTl[:].rearrange("p m n -> p (m n)"), bank[1][:],
                   LTh[:].rearrange("p m n -> p (m n)")).then_inc(c_v_l, 1)
                for n in range(IC // 2):
                    dve.wait_ge(c_a_hr, 4 * c + n + 1)
                    dve.scalar_tensor_tensor(out=hq[:, n % 2, :], in0=bank[2 + n][:], scalar=0.0, in1=hr[:, n % 2, :],
                                             op0=ALU.max, op1=ALU.mult).then_inc(c_v_h2, 1)
                    if n == 2:
                        dve.wait_ge(c_a_l, 2 * c + 2)
                        lo(ETl[:].rearrange("p m n -> p (m n)"), bank[1][:],
                           ETh[:].rearrange("p m n -> p (m n)")).then_inc(c_v_l, 1)
                    dve.wait_ge(c_a_h, 4 * c + n + 1)
                    lo(HBl[:, 2 * n:2 * n + 2, :].rearrange("p m n -> p (m n)"), hq[:, n % 2, :],
                       HBh[:, 2 * n:2 * n + 2, :].rearrange("p m n -> p (m n)")).then_inc(c_v_h, 1)
                    if n == 1:
                        dve.wait_ge(c_pe_gt, c + 1)
                        dve.tensor_copy(logits[:], bank[0][:, KEYS:2 * KEYS].rearrange(
                            "p (t n) -> p t n", t=2)[:, :, 0:NE])
                        dve.drain()
                        for t in range(2):
                            dve.max(top8[:, t, :], logits[:, t, :])
                        dve.drain()
                        dve.tensor_tensor(route[:], top8[:, :, 0], top8[:, :, 1], ALU.add).then_inc(c_v_r, 1)
                    if not last and n in (0, 2):
                        norm_stats(x_res[:, 2 * c + 2 + n // 2, :], c_v_st)
                        ln3(c + 1, n // 2, 4 * c + 3 + n // 2)
                if not last:
                    x3_lo(c + 1)
                for t in range(2):
                    dve.wait_ge(c_a_y, 2 * c + t + 1)
                    dve.wait_ge(c_v_r, c + 1)
                    dve.scalar_tensor_tensor(out=yy[:, t, :], in0=bank[t][:], scalar=route[:, t:t + 1],
                                             in1=ysh[:, t, :], op0=ALU.mult, op1=ALU.add).then_inc(c_v_y, 1)
                    norm_stats(yy[:, t, :], c_v_st)
                    dve.wait_ge(c_g_r, 4 * c + t + (3 if last else 5))
                    dve.scalar_tensor_tensor(out=yy[:, t, :], in0=yy[:, t, :], scalar=mv[:, 0:1], in1=gam[:],
                                             op0=ALU.subtract, op1=ALU.mult).then_inc(c_v_n, 1)
                    dve.wait_ge(c_v_n, 6 * c + 3 * t + 7)
                    dve.wait_ge(c_g_xb, 2 * c + t + 1)
                    dve.wait_ge(c_out[t], 16 * c + 16)
                    dve.scalar_tensor_tensor(out=yo[:, t, :], in0=yy[:, t, :], scalar=rstd[:], in1=xb[:, t, :],
                                             op0=ALU.mult, op1=ALU.add).then_inc(c_v_n, 2)

            dve.sem_inc(c_v_y, 2)
            dve.sem_inc(c_v_n, 6)
            with dve.Fori(0, NB // 2 - 1) as c:
                pair(c, False)
            pair(NB // 2 - 1, True)


def rope_tables():
    f = np.float32
    inv = (f(1.0) / np.power(f(500000.0), np.arange(0, SD, 2, dtype=np.float32) / f(SD))).astype(f)
    wavelen = (f(2.0 * np.pi) / inv).astype(f)
    lo, hi, factor, ctx = f(1.0), f(4.0), f(32.0), f(1024)
    freq = np.where(wavelen > ctx / lo, inv / factor, inv).astype(f)
    smooth = ((ctx / wavelen - lo) / (hi - lo)).astype(f)
    smoothed = ((f(1.0) - smooth) * freq / factor + smooth * freq).astype(f)
    medium = ~(wavelen < ctx / lo) & ~(wavelen > ctx / hi)
    freq = np.where(medium, smoothed, freq).astype(f)
    ang = (np.arange(P, dtype=np.float32)[:, None] * freq[None, :]).astype(f)
    cos, sin = np.cos(ang), np.sin(ang)
    return np.concatenate([cos, cos, -sin, sin], axis=1).astype(f)


_INS = ["x", "ctx_4096", "L0_attn_Wq", "L0_attn_Wk", "L0_attn_Wv", "L0_attn_Wo", "L0_xattn_Wq", "L0_xattn_Wk",
        "L0_xattn_Wv", "L0_xattn_Wo", "L0_ffn_gate_w", "L0_ffn_up_w", "L0_ffn_down_w", "L0_ffn_fc1_w",
        "L0_ffn_fc2_w", "L0_ffn_expert_w", "L0_ffn_ln_gamma", "L0_ffn_ln_beta"]


def kernel(**inputs):
    import numpy as _np
    import concourse.bacc as _bacc
    from concourse import mybir as _mybir
    from concourse.bass_utils import run_bass_kernel_spmd as _run

    nc = _bacc.Bacc("TRN2", target_bir_lowering=False, num_devices=1)
    arrays, args = {}, []
    for name in _INS:
        a = _np.ascontiguousarray(inputs[name])
        arrays[f"in_{name}_dram"] = a
        args.append(nc.dram_tensor(f"in_{name}_dram", a.shape, _mybir.dt.from_np(a.dtype), kind="ExternalInput").ap())
    table = rope_tables()
    arrays["rope_dram"] = table
    args.append(nc.dram_tensor("rope_dram", table.shape, _mybir.dt.from_np(table.dtype), kind="ExternalInput").ap())
    args.append(nc.dram_tensor("out_0_dram", (NB, P, D), F32, kind="ExternalOutput").ap())
    decoder_layer(nc, *args)
    r = _run(nc, [arrays], core_ids=[0])
    return r.results[0]["out_0_dram"]
```

```python
from contextlib import ExitStack

import numpy as np

import concourse.bass as bass
from concourse import mybir

F32 = mybir.dt.float32
F32R = mybir.dt.float32r
ALU = mybir.AluOpType
ACT = mybir.ActivationFunctionType
AX = mybir.AxisListType

P = 128
NB = 8
D = 512
KC = D // P
EPS = 1e-5

SH, SKV, SD = 32, 8, 16
SG = SH // SKV
S_SCALE = 1.0 / float(np.sqrt(SD))
MASKED = -float(2.0 ** 126)

XH, XKV, XD = 32, 4, 128
XG = XH // XKV
KEYS = 2 * P
X_SCALE = 1.0 / float(np.sqrt(XD))
DUOS = NB * XG // 2
PB = XG // 2

INT, LAT, NE = 1024, 256, 8
IC, LC = INT // P, LAT // P

KB = 1024


def decoder_layer(nc, x, ctx, s_wq, s_wk, s_wv, s_wo, x_wq, x_wk, x_wv, x_wo, gate_w, up_w, down_w,
                  fc1_w, fc2_w, expert_w, gamma, beta, rope, out):
    with ExitStack() as stack:
        def sem(name):
            return stack.enter_context(nc.semaphore(name))

        at, cursor = {}, 16512
        for region, size in (("X", 16 * KB), ("XT", 32 * KB), ("WQ", 32 * KB), ("WO", 32 * KB),
                             ("Q", 32 * KB), ("O", 16 * KB), ("KV", 12 * KB), ("P", 8 * KB),
                             ("PT", 8 * KB), ("ST", 8 * KB), ("F", 9 * KB + 512), ("C", 2 * KB)):
            at[region] = cursor
            cursor += size

        def sb(name, region, kb, shape, dt=F32):
            return nc.alloc_sbuf_tensor_at(name, [P, *shape], dt, offset=at[region] + int(kb * KB))

        def f32(ap):
            return ap.bitcast(F32)

        x_res = sb("x_res", "X", 0, [NB, D])
        ident = sb("ident", "C", 0, [P])
        ident_r = sb("ident_r", "C", 0.5, [P], F32R)
        rope_t = sb("rope_t", "C", 1, [2 * SD])
        stats = sb("stats", "C", 1.125, [6])
        mv = sb("mv", "C", 1.25, [2])
        rstd = sb("rstd", "C", 1.375, [1])
        half = sb("half", "C", 1.4375, [1])
        var_eps = sb("var_eps", "C", 1.5, [1])
        bd_mask = sb("bd_mask", "C", 1.53125, [SG])
        top8 = sb("top8", "C", 1.5625, [2, NE])
        route = sb("route", "C", 1.6875, [2])
        mv1 = sb("mv1", "C", 1.71875, [2])
        rstd1 = sb("rstd1", "C", 1.8125, [1])
        var1 = sb("var1", "C", 1.84375, [1])
        stats1 = sb("stats1", "C", 1.875, [6])

        XTh = sb("XTh", "XT", 0, [KC, NB * P], F32R)
        XTl = sb("XTl", "XT", 16, [KC, NB * P], F32R)

        SQh = sb("SQh", "WO", 0, [KC, D], F32R)
        SQl = sb("SQl", "WO", 8, [KC, D], F32R)
        SOh = sb("SOh", "WO", 16, [SG, D], F32R)
        SOl = sb("SOl", "WO", 24, [SG, D], F32R)
        XKh = sb("XKh", "Q", 0, [KC, D], F32R)
        XKl = sb("XKl", "Q", 8, [KC, D], F32R)
        XVh = sb("XVh", "Q", 16, [KC, D], F32R)
        XVl = sb("XVl", "Q", 24, [KC, D], F32R)
        SKVh = sb("SKVh", "KV", 0, [KC, 2 * P], F32R)
        SKVl = sb("SKVl", "KV", 4, [KC, 2 * P], F32R)
        xnTh = sb("xnTh", "KV", 8, [KC, P], F32R)
        xnTl = sb("xnTl", "KV", 10, [KC, P], F32R)
        KVst = sb("KVst", "O", 0, [XKV, 1024], F32R)
        Kbdh = sb("Kbdh", "WQ", 0, [KC, D], F32R)
        QTh = sb("QTh", "WQ", 8, [KC, P], F32R)
        KTh = sb("KTh", "WQ", 10, [KC, P], F32R)
        HTh = sb("HTh", "WQ", 12, [KC, KEYS], F32R)
        Kbdl = sb("Kbdl", "WQ", 16, [KC, D], F32R)
        QTl = sb("QTl", "WQ", 24, [KC, P], F32R)
        KTl = sb("KTl", "WQ", 26, [KC, P], F32R)
        HTl = sb("HTl", "WQ", 28, [KC, KEYS], F32R)
        Pa = sb("Pa", "P", 0, [3, D])
        cx = sb("cx", "P", 6, [D])
        PTah = sb("PTah", "PT", 0, [2, D], F32R)
        PTal = sb("PTal", "PT", 4, [2, D], F32R)
        xn = sb("xn", "ST", 0, [D])
        xn2 = sb("xn2", "ST", 2, [D])
        kr = sb("kr", "ST", 4, [D])
        mask_r = sb("mask_r", "ST", 6.5, [P], F32R)
        a_max = sb("a_max", "ST", 7, [SH])
        a_nb = sb("a_nb", "ST", 7.125, [SH])
        a_sum = sb("a_sum", "ST", 7.25, [SH])
        a_rec = sb("a_rec", "ST", 7.375, [SH])
        mask_f = sb("mask_f", "ST", 7.5, [P])
        VBW = P + SD
        Vbdh = sb("Vbdh", "F", 0, [SKV * VBW], F32R)
        Vbdl = sb("Vbdl", "F", 4.5, [SKV * VBW], F32R)
        OTh, OTl = PTah[:, 0, :], PTal[:, 0, :]

        temp_h = sb("temp_h", "XT", 0, [KC, NB * P])
        temp_l = sb("temp_l", "XT", 16, [KC, NB * P])
        last2, last1 = slice((NB - 2) * P, (NB - 1) * P), slice((NB - 1) * P, NB * P)
        rope_q1, rope_q2, q_rot = temp_h[:, :, last1], temp_l[:, :, last1], temp_l[:, :, last2]
        rope_k1, rope_k2 = temp_h[:, 0, last2], temp_h[:, 1, last2]
        q_first = sb("q_first", "PT", 0, [KC, P])
        rawQ = sb("rawQ", "O", 0, [KC, D])
        rawO = sb("rawO", "O", 8, [KC, D])
        rawOg = sb("rawOg", "XT", 0, [KC, D])
        rawKV = sb("rawKV", "P", 0, [2, D])
        rawXK = sb("rawXK", "XT", 8, [KC, D])
        rawXV = sb("rawXV", "XT", 16, [KC, D])

        WQh = sb("WQh", "WQ", 0, [XG, KC, P], F32R)
        WQl = sb("WQl", "WQ", 16, [XG, KC, P], F32R)
        WOh = sb("WOh", "WO", 0, [XG, D], F32R)
        WOl = sb("WOl", "WO", 16, [XG, D], F32R)
        Qh = sb("Qh", "Q", 0, [2, XG, KEYS], F32R)
        Ql = sb("Ql", "Q", 16, [2, XG, KEYS], F32R)
        Oh = sb("Oh", "O", 0, [2, XG, P], F32R)
        Ol = sb("Ol", "O", 8, [2, XG, P], F32R)
        KV = sb("KV", "KV", 0, [3, 1024], F32R)
        Pb = sb("Pb", "P", 0, [4, 2, KEYS])
        PTh = sb("PTh", "PT", 0, [2, D], F32R)
        PTl = sb("PTl", "PT", 4, [2, D], F32R)
        raw = sb("raw", "ST", 0, [4, D])
        raw_first = sb("raw_first", "WO", 0, [XG, D])
        b_max = sb("b_max", "F", 8, [4, 2])
        b_nb = sb("b_nb", "F", 8.0625, [4, 2])
        b_sum = sb("b_sum", "F", 8.125, [4, 2])
        b_rec = sb("b_rec", "F", 8.1875, [4, 2])

        UPh = sb("UPh", "WQ", 0, [KC, INT], F32R)
        UPl = sb("UPl", "WQ", 16, [KC, INT], F32R)
        DNh = sb("DNh", "XT", 0, [IC, D], F32R)
        DNl = sb("DNl", "XT", 16, [IC, D], F32R)
        F1h = sb("F1h", "Q", 0, [KC, LAT], F32R)
        F2h = sb("F2h", "Q", 4, [LC, D], F32R)
        HBh = sb("HBh", "Q", 8, [IC, KEYS], F32R)
        F1l = sb("F1l", "Q", 16, [KC, LAT], F32R)
        F2l = sb("F2l", "Q", 20, [LC, D], F32R)
        HBl = sb("HBl", "Q", 24, [IC, KEYS], F32R)
        EXh = sb("EXh", "KV", 8, [LC, LAT], F32R)
        EXl = sb("EXl", "KV", 10, [LC, LAT], F32R)
        xn3 = sb("xn3", "F", 0, [2, D])
        GTh = sb("GTh", "F", 4, [KC, P], F32R)
        GTl = sb("GTl", "F", 6, [KC, P], F32R)
        gate_raw = sb("gate_raw", "F", 8.5, [KC, NE])
        X3h = sb("X3h", "KV", 0, [KC, KEYS], F32R)
        X3l = sb("X3l", "KV", 4, [KC, KEYS], F32R)
        gam = sb("gam", "WO", 0, [D])
        bet = sb("bet", "WO", 2, [D])
        yr = sb("yr", "WO", 12, [2, D])
        yy = sb("yy", "WO", 16, [2, D])
        yo = sb("yo", "WO", 20, [2, D])
        xb = sb("xb", "WO", 24, [2, D])
        lgT = sb("lgT", "WO", 28, [KEYS])
        logits = sb("logits", "WO", 29.25, [2, NE])
        hr = sb("hr", "O", 0, [2, D])
        hq = sb("hq", "O", 4, [2, D])
        LTh = sb("LTh", "O", 8, [LC, KEYS], F32R)
        LTl = sb("LTl", "O", 10, [LC, KEYS], F32R)
        ETh = sb("ETh", "O", 12, [LC, KEYS], F32R)
        ETl = sb("ETl", "O", 14, [LC, KEYS], F32R)

        kv_scratch = nc.dram_tensor("kv_scratch", (XKV, NB, P, 1024), F32, kind="Internal").ap()

        bank = [stack.enter_context(nc.psum_tensor(f"bank{i}", [P, 512], F32)) for i in range(8)]

        def split3(pe, dst, lh, ll, rh, rl, start, stop):
            pe.matmul(dst, lh, rh, start=start, stop=False)
            pe.matmul(dst, lh, rl, start=False, stop=False)
            return pe.matmul(dst, ll, rh, start=False, stop=stop)

        ld_x0, ld_x, ld_q, ld_kv, ld_o, ld_xk, ld_xv, ld_rope, ld_cx, st_kv, st_xt = (sem(n) for n in (
            "ld_x0", "ld_x", "ld_q", "ld_kv", "ld_o", "ld_xk", "ld_xv", "ld_rope", "ld_cx", "st_kv", "st_xt"))
        g_const, g_rstd1, g_rstd, g_kbd, g_norm, g_xw = (sem(n) for n in (
            "g_const", "g_rstd1", "g_rstd", "g_kbd", "g_norm", "g_xw"))
        pe_w, pe_xn, pe_ht, pe_qkv, pe_kvp, pe_qk, pe_s, pe_pt, pe_pv, pe_wo = (sem(n) for n in (
            "pe_w", "pe_xn", "pe_ht", "pe_qkv", "pe_kvp", "pe_qk", "pe_s", "pe_pt", "pe_pv", "pe_wo"))
        a_w, a_xn, a_ht, a_v, a_kvp, a_qk, a_exp, a_pt, a_o = (sem(n) for n in (
            "a_w", "a_xn", "a_ht", "a_v", "a_kvp", "a_qk", "a_exp", "a_pt", "a_o"))
        a_wog, a_xw = sem("a_wog"), sem("a_xw")
        v_ptl_half, v_ol_half, v_htl_half = sem("v_ptl_half"), sem("v_ol_half"), sem("v_htl_half")
        v_c, v_w, v_st, v_xn, v_xnl, v_htl, v_rt, v_qr, v_vl, v_kvl, v_qkl, v_kbd, v_mx, v_nb, \
            v_rec, v_ptl, v_ol, v_x2, v_st2, v_xn2 = (sem(n) for n in (
                "v_c", "v_w", "v_st", "v_xn", "v_xnl", "v_htl", "v_rt", "v_qr", "v_vl", "v_kvl",
                "v_qkl", "v_kbd", "v_mx", "v_nb", "v_rec", "v_ptl", "v_ol", "v_x2", "v_st2", "v_xn2"))
        b_ld_first = sem("b_ld_first")
        b_ld = [sem(f"b_ld{i}") for i in range(4)]
        b_kv = [sem(f"b_kv{i}") for i in range(3)]
        b_pe_q, b_pe_s, b_pe_pt, b_pe_pv, b_pe_wo = (sem(n) for n in (
            "b_pe_q", "b_pe_s", "b_pe_pt", "b_pe_pv", "b_pe_wo"))
        b_a_w, b_a_q, b_a_exp, b_a_pt, b_a_o = (sem(n) for n in (
            "b_a_w", "b_a_q", "b_a_exp", "b_a_pt", "b_a_o"))
        b_v_mx, b_v_nb, b_v_rec, b_v_pt, b_v_q, b_v_o, b_v_x = (sem(n) for n in (
            "b_v_mx", "b_v_nb", "b_v_rec", "b_v_pt", "b_v_q", "b_v_o", "b_v_x"))
        b_g_w, b_g_norm = sem("b_g_w"), sem("b_g_norm")
        ld_gate, c_ld, c_out = sem("ld_gate"), sem("c_ld"), [sem("c_out0"), sem("c_out1")]
        c_pe_x, c_pe_g, c_pe_gt, c_pe_h, c_pe_l, c_pe_e, c_pe_y = (sem(n) for n in (
            "c_pe_x", "c_pe_g", "c_pe_gt", "c_pe_h", "c_pe_l", "c_pe_e", "c_pe_y"))
        c_a_x, c_a_g, c_a_hr, c_a_h, c_a_l = (sem(n) for n in (
            "c_a_x", "c_a_g", "c_a_hr", "c_a_h", "c_a_l"))
        c_v_g0, c_v_st, c_v_xn, c_v_x, c_v_h2, c_v_h, c_v_l, c_v_r, c_v_y, c_v_n = (
            sem(n) for n in ("c_v_g0", "c_v_st", "c_v_xn", "c_v_x", "c_v_h2", "c_v_h", "c_v_l",
                             "c_v_r", "c_v_y", "c_v_n"))
        c_g_r, c_g_xb = sem("c_g_r"), sem("c_g_xb")

        W0 = XG
        WPG = 2 * XG
        ffn_chunks = (
            [(up_w[kc * P:(kc + 1) * P, n * D:(n + 1) * D], UPh[:, kc, n * D:(n + 1) * D],
              UPl[:, kc, n * D:(n + 1) * D]) for kc in range(KC) for n in range(INT // D)]
            + [(fc1_w[c * 2 * P:(c + 1) * 2 * P, :].rearrange("(k p) n -> p k n", p=P),
                F1h[:, 2 * c:2 * c + 2, :], F1l[:, 2 * c:2 * c + 2, :]) for c in range(KC // 2)]
            + [(fc2_w[c * P:(c + 1) * P, :], F2h[:, c, :], F2l[:, c, :]) for c in range(LC)]
            + [(expert_w.rearrange("(k p) n -> p k n", p=P), EXh[:, :, :], EXl[:, :, :])]
            + [(down_w[c * P:(c + 1) * P, :], DNh[:, c, :], DNl[:, c, :]) for c in range(IC)])
        NUP = KC * INT // D
        NFC = KC // 2 + LC
        NF = len(ffn_chunks)

        def wq_src(g, h):
            return x_wq.rearrange("(k p) (h n) -> h p k n", p=P, n=XD)[XG * g + h]

        def wo_src(g, h):
            return x_wo.rearrange("(h p) n -> h p n", p=XD)[XG * g + h]

        def chunk_steps(last):
            steps = [((0, 0, 1, 2, 3, 4, 5, 5)[h], "wo", h) for h in range(XG)]
            if not last:
                steps += [(17 + h, "wq", h) for h in range(XG)]
            else:
                steps += [(17 + i, "ffn", i) for i in range(NUP)]
                steps += [(22 + i - NUP, "ffn", i) for i in range(NUP, NUP + NFC)]
                steps += [(min(26 + i - NUP - NFC, DUOS), "ffn", i) for i in range(NUP + NFC, NF)]
            return sorted(steps, key=lambda step: step[0])

        def raw_view(slot, dst):
            v = raw[:, slot, :]
            if len(dst.shape) == 3:
                v = v.rearrange("p (k n) -> p k n", k=dst.shape[1])
            return v

        def targets(kind, i):
            if kind == "wo":
                return WOh[:, i, :], WOl[:, i, :]
            if kind == "wq":
                return WQh[:, i, :, :], WQl[:, i, :, :]
            return ffn_chunks[i][1:]

        WBANK = (2, 3, 4, 5, 6, 7, 4, 5, 6, 7)

        QBANK = (2, 3, 5, 4)
        LN3_STEPS = (14, 16)
        VBANK = (4, 1)

        block = stack.enter_context(nc.Block())

        @block.sync
        def _(sp):
            sp.dma_start(x_res[:, 0, :], x[0]).then_inc(ld_x0, 16)
            sp.dma_start(rope_t[:], rope).then_inc(ld_rope, 16)
            sp.dma_start(rawQ[:], s_wq.rearrange("(m p) n -> p m n", p=P)).then_inc(ld_q, 16)
            sp.dma_start(rawKV[:, 0, :], s_wk).then_inc(ld_kv, 16)
            sp.dma_start(rawKV[:, 1, :], s_wv).then_inc(ld_kv, 16)
            sp.dma_start(rawO[:], s_wo.rearrange("(m p) n -> p m n", p=P)).then_inc(ld_o, 16)
            sp.dma_start(rawXK[:], x_wk.rearrange("(k p) n -> p k n", p=P)).then_inc(ld_xk, 16)
            sp.dma_start(rawXV[:], x_wv.rearrange("(k p) n -> p k n", p=P)).then_inc(ld_xv, 16)
            sp.dma_start(x_res[:, 1:, :], x[1:].rearrange("b t d -> t b d")).then_inc(ld_x, 16)
            sp.dma_start(cx[:], ctx[0]).then_inc(ld_cx, 16)
            sp.sem_inc(st_xt, 32)
            sp.sem_inc(st_kv, 16)

            def keep(b):
                sp.wait_ge(v_htl, 2 * b + 2)
                for src, dst in ((HTh, XTh), (HTl, XTl)):
                    sp.dma_start(f32(dst[:].rearrange("p k (b n) -> p b k n", b=NB)[:, b]),
                                 f32(src[:, :, P:KEYS])).then_inc(st_xt, 16)

            def store_kv(b):
                sp.wait_ge(v_kvl, 4 * b + 8)
                sp.dma_start(kv_scratch[:, b].rearrange("g p n -> p g n"), f32(KVst[:])).then_inc(st_kv, 16)

            with sp.Fori(0, NB - 1) as b:
                next_ctx = sp.snap(b + 1)
                sp.wait_ge(pe_ht, 2 * b + 1)
                sp.dma_start(cx[:], ctx[next_ctx]).then_inc(ld_cx, 16)
                keep(b)
                store_kv(b)
            sp.wait_ge(pe_qkv, 2 * NB)
            for h in range(XG):
                sp.dma_start(raw_first[:, h, :].rearrange("p (k n) -> p k n", k=KC), wq_src(0, h)).then_inc(b_ld_first, 16)
            sp.wait_ge(st_kv, 16 * NB)
            for b in range(3):
                sp.dma_start(f32(KV[:, b, :]), kv_scratch[0, b]).then_inc(b_kv[b], 16)
            keep(NB - 1)
            sp.wait_ge(pe_pv, NB)
            sp.dma_start(gate_raw[:], gate_w.rearrange("(k p) n -> p k n", p=P)).then_inc(ld_gate, 16)
            store_kv(NB - 1)
            sp.wait_ge(st_kv, 16 * NB + 16)
            sp.wait_ge(pe_ht, 2 * NB)

            def first_loads(g):
                for n in range(4):
                    src = wo_src(g, n)
                    sp.wait_ge(b_g_w, W0 + WPG * g + n - 3)
                    sp.dma_start(raw[:, n, :], src).then_inc(b_ld[n], 16)

            first_loads(0)

            def group(g, last):
                kv_loads = [(4 * (b - 3) + 4, g, b) for b in range(3, NB)]
                if not last:
                    kv_loads += [(24, g + 1, 2), (28, g + 1, 0), (32, g + 1, 1)]
                w_loads = [(max(step - 2, 0), kind, i) for step, kind, i in chunk_steps(last)]
                for k in range(DUOS):
                    for n, (step, kind, i) in enumerate(w_loads):
                        if step == k and n >= 4:
                            sp.wait_ge(b_g_w, W0 + WPG * g + n - 3)
                            dst = targets(kind, i)[0]
                            src = (wo_src(g, i) if kind == "wo" else wq_src(g + 1, i) if kind == "wq"
                                   else ffn_chunks[i][0])
                            sp.dma_start(raw_view(n % 4, dst), src).then_inc(b_ld[n % 4], 16)
                    if k == 26 and not last:
                        first_loads(sp.snap(g + 1))
                    for done, gg, b in kv_loads:
                        if done == k + 1:
                            n = NB * gg + b if last else sp.snap(NB * gg + b)
                            sp.wait_ge(b_pe_pv, DUOS * g + done)
                            sp.dma_start(f32(KV[:, b % 3, :]), kv_scratch.rearrange("g b p n -> (g b) p n")[n]
                                         ).then_inc(b_kv[b % 3], 16)

            with sp.Fori(0, XKV - 1) as g:
                group(g, False)
            group(XKV - 1, True)
            sp.wait_ge(b_pe_wo, PB * NB * XKV + 1)
            sp.dma_start(gam[:], gamma.partition_broadcast(P)).then_inc(c_ld, 16)
            sp.dma_start(bet[:], beta.partition_broadcast(P)).then_inc(c_ld, 16)
            sp.sem_inc(c_out[0], 16)
            sp.sem_inc(c_out[1], 16)
            with sp.Fori(0, NB // 2) as c:
                for t in range(2):
                    tile = sp.snap(2 * c + t)
                    sp.wait_ge(c_v_n, 6 * c + 3 * t + 9)
                    sp.dma_start(out[tile], yo[:, t, :]).then_inc(c_out[t], 16)
            sp.wait_ge(c_out[0], 16 * (NB // 2) + 16)
            sp.wait_ge(c_out[1], 16 * (NB // 2) + 16)

        @block.gpsimd
        def _(gp):
            gp.memset(ident[:], 0.0).then_inc(g_const, 1)
            gp.memset(mask_f[:], 0.0).then_inc(g_const, 1)
            gp.memset(bd_mask[:], 0.0).then_inc(g_const, 1)
            gp.memset(half[:], -0.5).then_inc(g_const, 1)
            gp.wait_ge(g_const, 4)
            gp.affine_select(out=ident[:], in_=ident[:], compare_op=ALU.not_equal, fill=1.0, base=0,
                             pattern=[[-1, P]], channel_multiplier=1).then_inc(g_const, 1)
            gp.affine_select(out=mask_f[:], in_=mask_f[:], compare_op=ALU.is_ge, fill=MASKED, base=0,
                             pattern=[[-1, P]], channel_multiplier=1).then_inc(g_const, 1)
            def inv_std1(b):
                gp.wait_ge(v_st, b + 1)
                gp.tensor_tensor(rstd1[:], var1[:], half[:], ALU.pow).then_inc(g_rstd1, 1)

            inv_std1(0)
            n = 6
            for base in range(2):
                for r in range(SD):
                    gp.wait_ge(g_const, n)
                    gp.affine_select(out=bd_mask[:], in_=bd_mask[:], compare_op=ALU.not_equal, fill=1.0,
                                     base=-(64 * base + r), pattern=[[-SD, SG]],
                                     channel_multiplier=1).then_inc(g_const, 1)
                    n += 1

            def diagonal_keys(b, ms):
                for m in ms:
                    gp.wait_ge(a_qk, 2 * b + 2)
                    src = f32(KTh[:, m, :]).unsqueeze(1).to_broadcast([P, SG, P])
                    gp.tensor_tensor(Kbdh[:, m, :].rearrange("p (c k) -> p c k", c=SG), src,
                                     bd_mask[:].unsqueeze(2).to_broadcast([P, SG, P]), ALU.mult).then_inc(g_kbd, 1)

            def lo_part(src, count, dst, hi):
                gp.wait_ge(b_a_w, count)
                gp.tensor_tensor(dst, src, f32(hi), ALU.subtract).then_inc(b_g_w, 1)

            def first_wq_lo(h):
                lo_part(raw_first[:, h, :].rearrange("p (k n) -> p k n", k=KC), h + 1, WQl[:, h, :, :], WQh[:, h, :, :])

            def normalise(b, j):
                gp.wait_ge(v_rec, SKV * b + j + 1)
                pj = Pa[:, j % 3, :].rearrange("p (c k) -> p c k", c=SG)
                gp.tensor_tensor(pj, pj, a_rec[:, SG * j:SG * j + SG].unsqueeze(2).to_broadcast([P, SG, P]),
                                 ALU.mult).then_inc(g_norm, 1)

            def batch(b, last):
                if not last:
                    inv_std1(b + 1)
                for j in range(2, SKV):
                    normalise(b, j)
                if not last:
                    diagonal_keys(b + 1, (0, 1))
                else:
                    first_wq_lo(0)
                    first_wq_lo(1)
                gp.wait_ge(v_st2, b + 1)
                gp.tensor_tensor(rstd[:], var_eps[:], half[:], ALU.pow).then_inc(g_rstd, 1)
                if not last:
                    diagonal_keys(b + 1, (2, 3))
                    normalise(b + 1, 0)
                    normalise(b + 1, 1)

            gp.wait_ge(a_xw, 1)
            gp.tensor_tensor(XKl[:], rawXK[:], f32(XKh[:]), ALU.subtract).then_inc(g_xw, 1)
            gp.wait_ge(g_const, 6 + 2 * SD)
            diagonal_keys(0, range(KC))
            normalise(0, 0)
            normalise(0, 1)
            gp.wait_ge(a_xw, 2)
            gp.tensor_tensor(XVl[:], rawXV[:], f32(XVh[:]), ALU.subtract).then_inc(g_xw, 1)
            with gp.Fori(0, NB - 1) as b:
                batch(b, False)
            batch(NB - 1, True)

            def norm(g, k):
                gp.wait_ge(b_v_rec, DUOS * g + k + 1)
                pk = Pb[:, k % 4, :, :]
                gp.tensor_tensor(pk, pk, b_rec[:, k % 4, :].unsqueeze(2).to_broadcast([P, 2, KEYS]),
                                 ALU.mult).then_inc(b_g_norm, 1)

            def inv_std(n):
                gp.wait_ge(c_v_st, n)
                gp.tensor_tensor(rstd[:], var_eps[:], half[:], ALU.pow).then_inc(c_g_r, 1)

            for h in range(2, XG):
                first_wq_lo(h)
            norm(0, 0)
            norm(0, 1)

            def group(g, last):
                chunks = chunk_steps(last)

                def split_weights(k):
                    for n, (step, kind, i) in enumerate(chunks):
                        if step == k:
                            hi, lo = targets(kind, i)
                            lo_part(raw_view(n % 4, lo), W0 + WPG * g + n + 1, lo, hi)

                for k in range(DUOS):
                    if k + 2 < DUOS:
                        norm(g, k + 2)
                    elif not last:
                        norm(g + 1, k + 2 - DUOS)
                    if last and k - 1 in LN3_STEPS:
                        inv_std(LN3_STEPS.index(k - 1) + 1)
                    split_weights(k)
                split_weights(DUOS)

            with gp.Fori(0, XKV - 1) as g:
                group(g, False)
            group(XKV - 1, True)

            def pair(c, last):
                for t in range(2):
                    gp.wait_ge(c_ld, 32)
                    gp.wait_ge(c_v_n, 6 * c + 6)
                    gp.tensor_tensor(xb[:, t, :], x_res[:, 2 * c + t, :], bet[:], ALU.add).then_inc(c_g_xb, 1)
                for t in range(2 if last else 4):
                    inv_std(4 * c + t + 3)

            with gp.Fori(0, NB // 2 - 1) as c:
                pair(c, False)
            pair(NB // 2 - 1, True)

        @block.tensor
        def _(pe):
            def turn_weights(n):
                for m in range(KC):
                    if n < 4:
                        src = rawQ[:, m, n * P:(n + 1) * P]
                    elif n < 6:
                        kc = 2 * (n - 4) + m // 2
                        src = rawKV[:, m % 2, kc * P:(kc + 1) * P]
                    else:
                        src = rawOg[:, m, (n - 6) * P:(n - 5) * P]
                    op = pe.transpose(bank[WBANK[n]][:, m * P:(m + 1) * P], src, ident[:])
                op.then_inc(pe_w, 1)

            def turn_xn(b):
                pe.wait_ge(v_xn, b + 1)
                for kc in range(KC):
                    op = pe.transpose(bank[0][:, kc * P:(kc + 1) * P], xn[:, kc * P:(kc + 1) * P], ident[:])
                op.then_inc(pe_xn, 1)

            def q_product(kcs):
                for kc in kcs:
                    op = split3(pe, bank[1][:], xnTh[:, kc, :], xnTl[:, kc, :], SQh[:, kc, :], SQl[:, kc, :],
                                kc == 0, kc == KC - 1)
                if KC - 1 in kcs:
                    op.then_inc(pe_qkv, 1)

            def kv_product(kcs):
                for kc in kcs:
                    op = split3(pe, bank[0][:, 0:2 * P], xnTh[:, kc, :], xnTl[:, kc, :], SKVh[:, kc, :],
                                SKVl[:, kc, :], kc == 0, kc == KC - 1)
                if KC - 1 in kcs:
                    op.then_inc(pe_qkv, 1)

            def turn_qk(b, q):
                pe.wait_ge(v_qr, 2 * b + 2)
                for m in range(KC):
                    op = pe.transpose(bank[2][:, m * P:(m + 1) * P], q[:, m, :], ident[:])
                op.then_inc(pe_qk, 1)
                for m in range(KC):
                    op = pe.transpose(bank[3][:, m * P:(m + 1) * P], kr[:, m * P:(m + 1) * P], ident[:])
                op.then_inc(pe_qk, 1)

            def turn_context(b):
                pe.wait_ge(ld_cx, 16 * b + 16)
                for kc in range(KC):
                    op = pe.transpose(bank[1][:, kc * P:(kc + 1) * P], cx[:, kc * P:(kc + 1) * P], ident[:])
                op.then_inc(pe_ht, 1)

            def cross_values(t, kcs):
                for kc in kcs:
                    op = split3(pe, bank[VBANK[t]][:], HTh[:, kc, t * P:(t + 1) * P], HTl[:, kc, t * P:(t + 1) * P],
                                XVh[:, kc, :], XVl[:, kc, :], kc == 0, kc == KC - 1)
                if KC - 1 in kcs:
                    op.then_inc(pe_kvp, 1)

            def cross_keys(n, b):
                for gg in range(2):
                    g = 2 * n + gg
                    dst = bank[6 + n][:, gg * KEYS:(gg + 1) * KEYS]
                    for kc in range(KC):
                        if g == 0 and kc % 2 == 0:
                            pe.wait_ge(v_htl if kc else v_htl_half, 2 * b + 2 if kc else b + 1)
                        op = split3(pe, dst, XKh[:, kc, g * XD:(g + 1) * XD], XKl[:, kc, g * XD:(g + 1) * XD],
                                    HTh[:, kc, :], HTl[:, kc, :], kc == 0, kc == KC - 1)
                op.then_inc(pe_kvp, 1)

            def scores(b, j):
                bk = bank[2 + j % 3]
                m, r = j // 2, 64 * (j % 2)
                if j >= 3:
                    pe.wait_ge(a_exp, SKV * b + j - 2)
                elif j < 2:
                    pe.wait_ge(v_qkl, 2 * b + 2)
                pe.wait_ge(g_kbd, KC * b + m + 1)
                pe.wait_ge(v_kbd, KC * b + m + 1)
                pe.matmul(bk[:].rearrange("p (c k) -> p c k", c=SG), ident_r[:],
                          mask_r[:].unsqueeze(1).to_broadcast([P, SG, P]), start=True, stop=False)
                rows = slice(r, r + 64)
                split3(pe, bk[:], QTh[rows, m, :], QTl[rows, m, :], Kbdh[rows, m, :], Kbdl[rows, m, :],
                       False, True).then_inc(pe_s, 1)

            def queries(g_count, head, pair, bk):
                pe.wait_ge(b_g_w, g_count)
                for kc in range(KC):
                    op = split3(pe, bank[bk][:, (head % 2) * KEYS:(head % 2 + 1) * KEYS],
                                WQh[:, head, kc, :], WQl[:, head, kc, :],
                                XTh[:, kc, pair * KEYS:(pair + 1) * KEYS], XTl[:, kc, pair * KEYS:(pair + 1) * KEYS],
                                kc == 0, kc == KC - 1)
                op.then_inc(b_pe_q, 1)

            def batch(b, last):
                def turn(j):
                    pe.wait_ge(g_norm, SKV * b + j + 1)
                    if j >= 2:
                        pe.wait_ge(v_ptl, SKV * b + j - 1)
                    elif j == 0:
                        pe.wait_ge(v_kvl, 4 * b + 3)
                    for c in range(SG):
                        op = pe.transpose(bank[5 + j % 2][:, c * P:(c + 1) * P],
                                          Pa[:, j % 3, c * P:(c + 1) * P], ident[:])
                    op.then_inc(pe_pt, 1)

                def values(j):
                    if j == SKV - 1:
                        for n, split in enumerate((v_ptl_half, v_ptl)):
                            pe.wait_ge(split, SKV * b + SKV if n else b + 1)
                            cols = slice(n * KEYS, (n + 1) * KEYS)
                            op = split3(pe, bank[7][:, cols], Vbdh[:, j * P:(j + 1) * P], Vbdl[:, j * P:(j + 1) * P],
                                        PTah[:, j % 2, cols], PTal[:, j % 2, cols], False, n == 1)
                        op.then_inc(pe_pv, 1)
                        return
                    pe.wait_ge(v_ptl, SKV * b + j + 1)
                    if j == 0:
                        pe.wait_ge(v_vl, b + 1)
                        pe.wait_ge(a_v, b + 1)
                    op = split3(pe, bank[7][:], Vbdh[:, j * P:(j + 1) * P], Vbdl[:, j * P:(j + 1) * P],
                                PTah[:, j % 2, :], PTal[:, j % 2, :], j == 0, False)

                for j in range(SKV):
                    turn(j)
                    if j + 3 < SKV:
                        scores(b, j + 3)
                    if j == 5 and not last:
                        kv_product((0, 1))
                    if j == 6 and not last:
                        kv_product((2, 3))
                    if j == 7:
                        pe.wait_ge(v_htl, 2 * b + 1)
                        pe.wait_ge(g_xw, 2)
                        cross_values(0, (0,))
                    if j == 1:
                        pe.wait_ge(v_kvl, 4 * b + 4)
                        turn_context(b)
                    if j >= 1:
                        values(j - 1)
                    if j == 1 and not last:
                        turn_xn(b + 1)
                    if j == 3 and not last:
                        pe.wait_ge(v_xnl, b + 2)
                        pe.wait_ge(v_htl, 2 * b + 1)
                        q_product((0, 1))
                    if j == 4 and not last:
                        q_product((2, 3))
                values(SKV - 1)
                if not last:
                    pe.wait_ge(a_exp, SKV * b + SKV)
                    turn_qk(b + 1, q_rot)
                for g in range(SG):
                    if g % 2 == 0:
                        pe.wait_ge(v_ol if g else v_ol_half, b + 1)
                    op = split3(pe, bank[6][:], OTh[:, g * P:(g + 1) * P], OTl[:, g * P:(g + 1) * P], SOh[:, g, :],
                                SOl[:, g, :], g == 0, g == SG - 1)
                op.then_inc(pe_wo, 1)
                cross_values(0, (1, 2, 3))
                if last:
                    pe.wait_ge(st_xt, 32 * NB)
                    queries(1, 0, 0, QBANK[0])
                    queries(2, 1, 0, QBANK[0])
                else:
                    scores(b + 1, 0)
                    scores(b + 1, 1)
                    pe.wait_ge(v_vl, b + 2)
                pe.wait_ge(v_xn2, b + 1)
                for kc in range(KC):
                    op = pe.transpose(bank[0][:, kc * P:(kc + 1) * P], xn2[:, kc * P:(kc + 1) * P], ident[:])
                op.then_inc(pe_ht, 1)
                pe.wait_ge(v_kvl, 4 * b + 5)
                if last:
                    queries(3, 2, 0, QBANK[1])
                    queries(4, 3, 0, QBANK[1])
                else:
                    scores(b + 1, 2)
                cross_keys(0, b)
                cross_keys(1, b)
                cross_values(1, range(KC))

            pe.wait_ge(g_const, 6)
            pe.wait_ge(ld_q, 16)
            for n in range(4):
                turn_weights(n)
            turn_xn(0)
            pe.wait_ge(ld_kv, 32)
            for n in range(4, 6):
                turn_weights(n)
            pe.wait_ge(v_w, 4)
            pe.wait_ge(v_xnl, 1)
            q_product(range(KC))
            pe.wait_ge(v_w, 6)
            kv_product(range(KC))
            pe.wait_ge(a_wog, KC)
            for n in range(6, 10):
                turn_weights(n)
            turn_qk(0, q_first)
            pe.wait_ge(v_c, 4)
            scores(0, 0)
            scores(0, 1)
            pe.wait_ge(v_w, 7)
            scores(0, 2)
            pe.wait_ge(v_w, 10)
            with pe.Fori(0, NB - 1) as b:
                batch(b, False)
            batch(NB - 1, True)

            def scores_b(g, k):
                b, i = k // PB, k % PB
                slot = b % 3
                if i == 0:
                    pe.wait_ge(b_kv[slot], 16 * ((3 if slot < 2 else 2) * g + b // 3 + 1))
                if b % 2 == 0:
                    pe.wait_ge(b_v_q, 4 + 16 * g + 4 * (b // 2) - 4 + i + 1)
                for h in range(2):
                    head = 2 * i + h
                    op = split3(pe, bank[k % 3][:, h * KEYS:(h + 1) * KEYS],
                                Qh[:, (b // 2) % 2, head, (b % 2) * P:(b % 2 + 1) * P],
                                Ql[:, (b // 2) % 2, head, (b % 2) * P:(b % 2 + 1) * P],
                                KV[:, slot, 0:KEYS], KV[:, slot, KEYS:2 * KEYS], True, True)
                op.then_inc(b_pe_s, 1)

            def out_piece(g, b, i):
                pe.wait_ge(b_v_o, DUOS * g + PB * b + i + 2)
                pe.wait_ge(b_g_w, W0 + WPG * g + 2 * i + 2)
                if i == 0:
                    pe.wait_ge(b_v_x, NB * g + b + 1)
                for h in range(2):
                    head = 2 * i + h
                    op = split3(pe, bank[7][:], Oh[:, b % 2, head, :], Ol[:, b % 2, head, :], WOh[:, head, :],
                                WOl[:, head, :], head == 0, head == XG - 1)
                op.then_inc(b_pe_wo, 1)

            def turn_x3(c):
                for t in range(2):
                    pe.wait_ge(c_v_xn, 2 * c + t + 1)
                    for kc in range(KC):
                        op = pe.transpose(bank[2 + t][:, kc * P:(kc + 1) * P], xn3[:, t, kc * P:(kc + 1) * P],
                                          ident[:])
                    op.then_inc(c_pe_x, 1)

            pe.sem_inc(b_pe_wo, 1)
            for h in range(4, XG):
                queries(h + 1, h, 0, QBANK[h // 2])
            pe.wait_ge(st_xt, 32 * NB + 32)
            pe.wait_ge(v_kvl, 4 * NB + 4)
            scores_b(0, 0)
            scores_b(0, 1)

            def outputs(g, k):
                pe.wait_ge(b_v_pt, DUOS * g + k + 3)
                pe.wait_ge(b_v_o, DUOS * g + k + 1)
                slot = (k // PB) % 3
                for c in range(2):
                    vh = KV[:, slot, 2 * KEYS + c * P:2 * KEYS + (c + 1) * P]
                    vl = KV[:, slot, 3 * KEYS + c * P:3 * KEYS + (c + 1) * P]
                    op = split3(pe, bank[5][:, 0:KEYS], vh, vl, PTh[:, k % 2, c * KEYS:(c + 1) * KEYS],
                                PTl[:, k % 2, c * KEYS:(c + 1) * KEYS], c == 0, c == 1)
                op.then_inc(b_pe_pv, 1)

            def group(g, last):
                for k in range(DUOS):
                    if k + 2 < DUOS or not last:
                        if k + 2 < DUOS:
                            pe.wait_ge(b_a_exp, DUOS * g + max(k, 1))
                            scores_b(g, k + 2)
                        else:
                            pe.wait_ge(b_a_exp, DUOS * g + k + 1)
                            scores_b(g + 1, k + 2 - DUOS)
                    pe.wait_ge(b_g_norm, DUOS * g + k + 1)
                    pe.wait_ge(b_v_pt, DUOS * g + k + 1)
                    for c in range(2):
                        for h in range(2):
                            op = pe.transpose(bank[3 + k % 2][:, c * KEYS + h * P:c * KEYS + (h + 1) * P],
                                              Pb[:, k % 4, h, c * P:(c + 1) * P], ident[:])
                    op.then_inc(b_pe_pt, 1)
                    if k >= PB:
                        out_piece(g, k // PB - 1, k % PB)
                    if k < DUOS - XG or not last:
                        if k % 2 == 0:
                            pe.wait_ge(b_v_q, 4 + 16 * g + k // 2)
                        if k < DUOS - XG:
                            queries(W0 + WPG * g, k % XG, k // XG + 1, 6)
                        else:
                            queries(W0 + WPG * g + XG + k % XG + 1, k % XG, 0, 6)
                    if k:
                        outputs(g, k - 1)
                out_piece(g, NB - 1, 0)
                outputs(g, DUOS - 1)
                if last:
                    turn_x3(0)
                for i in range(1, PB):
                    out_piece(g, NB - 1, i)

            with pe.Fori(0, XKV - 1) as g:
                group(g, False)
            group(XKV - 1, True)

            pe.wait_ge(b_g_w, W0 + WPG * (XKV - 1) + XG + NUP + NFC)
            pe.wait_ge(c_v_g0, 3)

            def pair(c, last):
                pe.wait_ge(c_v_x, 2 * c + 2)
                pe.wait_ge(c_v_y, 2 * c + 1)
                for kc in range(KC):
                    op = split3(pe, bank[0][:, 0:KEYS], GTh[:, kc, :], GTl[:, kc, :], X3h[:, kc, :], X3l[:, kc, :],
                                kc == 0, kc == KC - 1)
                op.then_inc(c_pe_g, 1)
                pe.wait_ge(c_v_y, 2 * c + 2)
                for m in range(LC):
                    for kc in range(KC):
                        op = split3(pe, bank[1][:, m * KEYS:(m + 1) * KEYS], F1h[:, kc, m * P:(m + 1) * P],
                                    F1l[:, kc, m * P:(m + 1) * P], X3h[:, kc, :], X3l[:, kc, :], kc == 0, kc == KC - 1)
                op.then_inc(c_pe_l, 1)
                for n in range(IC // 2):
                    for mm in range(2):
                        m = 2 * n + mm
                        for kc in range(KC):
                            op = split3(pe, bank[2 + n][:, mm * KEYS:(mm + 1) * KEYS], UPh[:, kc, m * P:(m + 1) * P],
                                        UPl[:, kc, m * P:(m + 1) * P], X3h[:, kc, :], X3l[:, kc, :],
                                        kc == 0, kc == KC - 1)
                    op.then_inc(c_pe_h, 1)
                    if n == 0:
                        pe.wait_ge(c_a_g, c + 2)
                        for t in range(2):
                            op = pe.transpose(bank[0][:, KEYS + t * P:KEYS + (t + 1) * P],
                                              lgT[:, t * P:(t + 1) * P], ident[:])
                        op.then_inc(c_pe_gt, 1)
                    if n == 1:
                        pe.wait_ge(b_g_w, W0 + WPG * (XKV - 1) + XG + NUP + NFC + 1)
                        pe.wait_ge(c_v_l, 2 * c + 1)
                        for m in range(LC):
                            for kc in range(LC):
                                op = split3(pe, bank[1][:, m * KEYS:(m + 1) * KEYS], EXh[:, kc, m * P:(m + 1) * P],
                                            EXl[:, kc, m * P:(m + 1) * P], LTh[:, kc, :], LTl[:, kc, :],
                                            kc == 0, kc == LC - 1)
                        op.then_inc(c_pe_e, 1)
                pe.wait_ge(c_v_l, 2 * c + 2)
                pe.wait_ge(c_v_r, c + 1)
                for t in range(2):
                    for kc in range(LC):
                        op = split3(pe, bank[t][:], ETh[:, kc, t * P:(t + 1) * P], ETl[:, kc, t * P:(t + 1) * P],
                                    F2h[:, kc, :], F2l[:, kc, :], kc == 0, kc == LC - 1)
                    op.then_inc(c_pe_y, 1)
                if not last:
                    pe.wait_ge(c_v_h, 4 * c + 2)
                    turn_x3(c + 1)
                pe.wait_ge(b_g_w, W0 + WPG * (XKV - 1) + XG + NF)
                pe.wait_ge(b_v_x, NB * XKV + 1)
                for t in range(2):
                    for m in range(IC):
                        if t == 0 and m % 2 == 0:
                            pe.wait_ge(c_v_h, 4 * c + m // 2 + 1)
                        op = split3(pe, bank[6 + t][:], HBh[:, m, t * P:(t + 1) * P], HBl[:, m, t * P:(t + 1) * P],
                                    DNh[:, m, :], DNl[:, m, :], m == 0, m == IC - 1)
                    op.then_inc(c_pe_y, 1)

            with pe.Fori(0, NB // 2 - 1) as c:
                pair(c, False)
            pair(NB // 2 - 1, True)

        @block.scalar
        def _(act):
            def hi(dst, src):
                return act.activation(dst, src, ACT.Copy)

            def weight_a(n):
                act.wait_ge(pe_w, n + 1)
                if n < 4:
                    dst = SQh[:, n, :]
                elif n < 6:
                    dst = SKVh[:, 2 * (n - 4):2 * (n - 4) + 2, :].rearrange("p k n -> p (k n)")
                else:
                    dst = SOh[:, n - 6, :]
                hi(dst, bank[WBANK[n]][:]).then_inc(a_w, 1)

            def xn_hi(b):
                act.wait_ge(pe_xn, b + 1)
                hi(xnTh[:], bank[0][:].rearrange("p (k n) -> p k n", k=KC)).then_inc(a_xn, 1)

            def values_hi(b):
                act.wait_ge(pe_qkv, 2 * b + 2)
                hi(Vbdh[:].rearrange("p (j c) -> p j c", c=VBW)[:, :, 0:SD],
                   bank[0][:, P:2 * P].rearrange("p (j d) -> p j d", j=SKV)).then_inc(a_v, 1)

            def qk_hi(b):
                act.wait_ge(pe_qk, 2 * b + 1)
                hi(QTh[:], bank[2][:].rearrange("p (k n) -> p k n", k=KC)).then_inc(a_qk, 1)
                act.wait_ge(pe_qk, 2 * b + 2)
                hi(KTh[:], bank[3][:].rearrange("p (k n) -> p k n", k=KC)).then_inc(a_qk, 1)

            def context_hi(b):
                act.wait_ge(pe_ht, 2 * b + 1)
                hi(HTh[:, :, 0:P], bank[1][:].rearrange("p (k n) -> p k n", k=KC)).then_inc(a_ht, 1)

            def latents_hi(b):
                act.wait_ge(pe_ht, 2 * b + 2)
                act.wait_ge(st_xt, 32 * b + 32)
                hi(HTh[:, :, P:KEYS], bank[0][:].rearrange("p (k n) -> p k n", k=KC)).then_inc(a_ht, 1)

            def cross_values_hi(b, t):
                act.wait_ge(pe_kvp, 4 * b + 3 * t + 1)
                hi(KVst[:, :, 2 * KEYS + t * P:2 * KEYS + (t + 1) * P],
                   bank[VBANK[t]][:].rearrange("p (g n) -> p g n", g=XKV)).then_inc(a_kvp, 1)

            def cross_keys_hi(b, n):
                act.wait_ge(pe_kvp, 4 * b + n + 2)
                hi(KVst[:, 2 * n:2 * n + 2, 0:KEYS],
                   bank[6 + n][:].rearrange("p (g n) -> p g n", g=2)).then_inc(a_kvp, 1)

            def probs(b, j):
                act.wait_ge(v_nb, SKV * b + j + 1)
                if j >= 3:
                    act.wait_ge(pe_pt, SKV * b + j - 2)
                for c in range(SG):
                    h = SG * j + c
                    op = act.activation(Pa[:, j % 3, c * P:(c + 1) * P], bank[2 + j % 3][:, c * P:(c + 1) * P],
                                        ACT.Exp, bias=a_nb[:, h:h + 1], scale=S_SCALE, accum_out=a_sum[:, h:h + 1])
                op.then_inc(a_exp, 1)

            def first_wq(h):
                act.wait_ge(b_ld_first, 16 * XG)
                hi(WQh[:, h, :, :], raw_first[:, h, :].rearrange("p (k n) -> p k n", k=KC)).then_inc(b_a_w, 1)

            def batch(b, last):
                for j in range(SKV):
                    if 3 <= j + 2 < SKV:
                        probs(b, j + 2)
                    act.wait_ge(pe_pt, SKV * b + j + 1)
                    hi(PTah[:, j % 2, :], bank[5 + j % 2][:]).then_inc(a_pt, 1)
                    if j == 1:
                        context_hi(b)
                    if j == 2 and not last:
                        xn_hi(b + 1)
                act.wait_ge(pe_pv, b + 1)
                hi(OTh, bank[7][:]).then_inc(a_o, 1)
                if not last:
                    qk_hi(b + 1)
                    values_hi(b + 1)
                else:
                    for h in range(6):
                        first_wq(h)
                act.wait_ge(st_kv, 16 * b + 16)
                cross_values_hi(b, 0)
                latents_hi(b)
                if not last:
                    probs(b + 1, 0)
                    probs(b + 1, 1)
                cross_keys_hi(b, 0)
                if not last:
                    probs(b + 1, 2)
                cross_keys_hi(b, 1)
                cross_values_hi(b, 1)

            for n in range(4):
                weight_a(n)
            xn_hi(0)
            for n in range(4, 6):
                weight_a(n)
            act.wait_ge(ld_o, 16)
            for m in range(KC):
                act.activation(rawOg[:, m, :].rearrange("p (g j d) -> p g j d", g=SG, j=SKV),
                               rawO[:, m, :].rearrange("p (j g d) -> p g j d", j=SKV, g=SG),
                               ACT.Copy).then_inc(a_wog, 1)
            act.wait_ge(ld_xk, 16)
            hi(XKh[:], rawXK[:]).then_inc(a_xw, 1)
            qk_hi(0)
            for n in range(6, 10):
                weight_a(n)
            act.wait_ge(v_c, 2)
            values_hi(0)
            act.wait_ge(ld_xv, 16)
            hi(XVh[:], rawXV[:]).then_inc(a_xw, 1)
            for j in range(3):
                probs(0, j)
            with act.Fori(0, NB - 1) as b:
                batch(b, False)
            batch(NB - 1, True)

            def weight(slot, loads, hi_dst):
                act.wait_ge(b_ld[slot], 16 * loads)
                hi(hi_dst, raw_view(slot, hi_dst)).then_inc(b_a_w, 1)

            def probs_b(g, k):
                act.wait_ge(b_v_nb, DUOS * g + k + 1)
                for h in range(2):
                    op = act.activation(Pb[:, k % 4, h, :], bank[k % 3][:, h * KEYS:(h + 1) * KEYS], ACT.Exp,
                                        bias=b_nb[:, k % 4, h:h + 1], scale=X_SCALE,
                                        accum_out=b_sum[:, k % 4, h:h + 1])
                op.then_inc(b_a_exp, 1)

            def queries(count, fill, parity, bk=6):
                act.wait_ge(b_pe_q, 2 * count)
                hi(Qh[:, parity, 2 * fill:2 * fill + 2, :],
                   bank[bk][:].rearrange("p (h n) -> p h n", h=2)).then_inc(b_a_q, 1)

            act.wait_ge(pe_kvp, 4 * NB)
            act.wait_ge(st_xt, 32 * NB + 32)
            for h in range(6, XG):
                first_wq(h)
            for f in range(4):
                queries(f + 1, f, 0, QBANK[f])
            probs_b(0, 0)
            probs_b(0, 1)
            act.wait_ge(b_g_w, W0)
            act.wait_ge(ld_gate, 16)
            act.wait_ge(c_v_g0, 2)
            hi(GTh[:, :, 0:NE], gate_raw[:]).then_inc(c_a_g, 1)

            def outputs(g, k):
                act.wait_ge(b_pe_pv, DUOS * g + k + 1)
                b, i = k // PB, k % PB
                hi(Oh[:, b % 2, 2 * i:2 * i + 2, :],
                   bank[5][:, 0:KEYS].rearrange("p (h n) -> p h n", h=2)).then_inc(b_a_o, 1)

            def group(g, last):
                chunks = chunk_steps(last)

                def split_weights(k):
                    for n, (step, kind, i) in enumerate(chunks):
                        if step == k:
                            if kind == "wo":
                                act.wait_ge(b_pe_wo, PB * NB * g + 1)
                            elif kind == "wq" or i < NUP:
                                act.wait_ge(b_pe_q, XG + DUOS * g + 17 + i)
                            elif i < NUP + NFC:
                                act.wait_ge(b_pe_s, DUOS * g + 24)
                            elif i == NUP + NFC:
                                act.wait_ge(b_pe_pv, DUOS * g + 24)
                            else:
                                act.wait_ge(b_pe_q, XG + DUOS * g + 24)
                            weight(n % 4, 4 * g + n // 4 + 1, targets(kind, i)[0])

                for k in range(DUOS):
                    act.wait_ge(b_pe_pt, DUOS * g + k + 1)
                    hi(PTh[:, k % 2, :], bank[3 + k % 2][:]).then_inc(b_a_pt, 1)
                    if k + 2 < DUOS:
                        probs_b(g, k + 2)
                    elif not last:
                        probs_b(g + 1, k + 2 - DUOS)
                    split_weights(k)
                    if k % 2 == 1 and (k < DUOS - XG or not last):
                        queries(4 + 16 * g + k // 2 + 1, (k % XG) // 2, (k // XG + 1) % 2)
                    if k:
                        outputs(g, k - 1)
                outputs(g, DUOS - 1)
                split_weights(DUOS)

            with act.Fori(0, XKV - 1) as g:
                group(g, False)
            group(XKV - 1, True)

            def x3_hi(c):
                for t in range(2):
                    act.wait_ge(c_pe_x, 2 * c + t + 1)
                    hi(X3h[:, :, t * P:(t + 1) * P],
                       bank[2 + t][:].rearrange("p (k n) -> p k n", k=KC)).then_inc(c_a_x, 1)

            def pair(c, last):
                act.wait_ge(c_pe_g, c + 1)
                hi(lgT[:], bank[0][:, 0:KEYS]).then_inc(c_a_g, 1)
                act.wait_ge(c_pe_l, c + 1)
                hi(LTh[:].rearrange("p m n -> p (m n)"), bank[1][:]).then_inc(c_a_l, 1)
                for n in range(IC // 2):
                    act.wait_ge(c_pe_h, 4 * c + n + 1)
                    act.activation(hr[:, n % 2, :], bank[2 + n][:], ACT.Relu).then_inc(c_a_hr, 1)
                    if n == 2:
                        act.wait_ge(c_pe_e, c + 1)
                        hi(ETh[:].rearrange("p m n -> p (m n)"), bank[1][:]).then_inc(c_a_l, 1)
                    act.wait_ge(c_v_h2, 4 * c + n + 1)
                    hi(HBh[:, 2 * n:2 * n + 2, :].rearrange("p m n -> p (m n)"), hq[:, n % 2, :]).then_inc(c_a_h, 1)
                if not last:
                    x3_hi(c + 1)

            x3_hi(0)
            with act.Fori(0, NB // 2 - 1) as c:
                pair(c, False)
            pair(NB // 2 - 1, True)

        @block.vector
        def _(dve):
            def lo(dst, src, hi_part):
                return dve.tensor_tensor(dst, src, f32(hi_part), ALU.subtract)

            dve.memset(f32(Vbdh[:]), 0.0).then_inc(v_c, 1)
            dve.memset(f32(Vbdl[:]), 0.0).then_inc(v_c, 1)
            dve.wait_ge(g_const, 6)
            dve.tensor_copy(ident_r[:], ident[:]).then_inc(v_c, 1)
            dve.tensor_copy(mask_r[:], mask_f[:]).then_inc(v_c, 1)

            def ln1_stats(b):
                dve.drain()
                dve.bn_stats(stats1[:], x_res[:, b, :])
                dve.drain()
                dve.bn_aggr(mv1[:], stats1[:])
                dve.drain()
                dve.tensor_scalar(var1[:], mv1[:, 1:2], EPS, None, ALU.add).then_inc(v_st, 1)

            def weight_a(n):
                dve.wait_ge(a_w, n + 1)
                if n < 4:
                    dst, h = SQl[:, n, :], SQh[:, n, :]
                elif n < 6:
                    dst = SKVl[:, 2 * (n - 4):2 * (n - 4) + 2, :].rearrange("p k n -> p (k n)")
                    h = SKVh[:, 2 * (n - 4):2 * (n - 4) + 2, :].rearrange("p k n -> p (k n)")
                else:
                    dst, h = SOl[:, n - 6, :], SOh[:, n - 6, :]
                lo(dst, bank[WBANK[n]][:], h).then_inc(v_w, 1)

            def norm_stats(src, sem_st):
                dve.drain()
                dve.bn_stats(stats[:], src)
                dve.drain()
                dve.bn_aggr(mv[:], stats[:])
                dve.drain()
                dve.tensor_scalar(var_eps[:], mv[:, 1:2], EPS, None, ALU.add).then_inc(sem_st, 1)

            cosf, sinf = rope_t[:, 0:SD], rope_t[:, SD:2 * SD]
            HD = SD // 2

            def ln1(b):
                dve.wait_ge(g_rstd1, b + 1)
                dve.tensor_scalar(xn[:], x_res[:, b, :], mv1[:, 0:1], rstd1[:], ALU.subtract,
                                  ALU.mult).then_inc(v_xn, 1)

            def ln1_lo(b):
                dve.wait_ge(a_xn, b + 1)
                lo(xnTl[:], bank[0][:].rearrange("p (k n) -> p k n", k=KC), xnTh[:]).then_inc(v_xnl, 1)

            def rotate(src, t1, t2, m, nh):
                s4, a4, b4 = (t.rearrange("p (m h d) -> p m h d", m=m, d=SD) if len(t.shape) == 2 else
                              t.rearrange("p m (h d) -> p m h d", d=SD) for t in (src, t1, t2))
                cos4 = cosf.unsqueeze(1).unsqueeze(1).to_broadcast([P, m, nh, SD])
                sin4 = [sinf[:, n * HD:(n + 1) * HD].unsqueeze(1).unsqueeze(1).to_broadcast([P, m, nh, HD])
                        for n in range(2)]
                dve.tensor_tensor(a4, s4, cos4, ALU.mult).then_inc(v_rt, 1)
                dve.tensor_tensor(b4[:, :, :, 0:HD], s4[:, :, :, HD:SD], sin4[0], ALU.mult).then_inc(v_rt, 1)
                dve.tensor_tensor(b4[:, :, :, HD:SD], s4[:, :, :, 0:HD], sin4[1], ALU.mult).then_inc(v_rt, 1)

            def rope_q(b, t1, t2, q):
                dve.wait_ge(pe_qkv, 2 * b + 1)
                rotate(bank[1][:], t1, t2, KC, SH // KC)
                dve.wait_ge(v_rt, 6 * b + 3)
                dve.tensor_tensor(q, t1, t2, ALU.add).then_inc(v_qr, 1)

            def rope_k(b, t1, t2):
                dve.wait_ge(pe_qkv, 2 * b + 2)
                rotate(bank[0][:, 0:P], t1, t2, 1, SKV)
                dve.wait_ge(v_rt, 6 * b + 6)
                k1, k2 = (t.rearrange("p (j d) -> p j d", d=SD).unsqueeze(2).to_broadcast([P, SKV, SG, SD])
                          for t in (t1, t2))
                dve.tensor_tensor(kr[:].rearrange("p (j g d) -> p j g d", j=SKV, g=SG), k1, k2,
                                  ALU.add).then_inc(v_qr, 1)

            def values_lo(b):
                dve.wait_ge(a_v, b + 1)
                vv = [t[:].rearrange("p (j c) -> p j c", c=VBW)[:, :, 0:SD] for t in (Vbdl, Vbdh)]
                lo(vv[0], bank[0][:, P:2 * P].rearrange("p (j d) -> p j d", j=SKV), vv[1]).then_inc(v_vl, 1)

            def qk_lo(b):
                dve.wait_ge(a_qk, 2 * b + 1)
                lo(QTl[:], bank[2][:].rearrange("p (k n) -> p k n", k=KC), QTh[:]).then_inc(v_qkl, 1)
                dve.wait_ge(a_qk, 2 * b + 2)
                lo(KTl[:], bank[3][:].rearrange("p (k n) -> p k n", k=KC), KTh[:]).then_inc(v_qkl, 1)

            def diagonal_keys(b, ms):
                dve.wait_ge(v_qkl, 2 * b + 2)
                for m in ms:
                    dve.tensor_tensor(Kbdl[:, m, :].rearrange("p (c k) -> p c k", c=SG),
                                      f32(KTl[:, m, :]).unsqueeze(1).to_broadcast([P, SG, P]),
                                      bd_mask[:].unsqueeze(2).to_broadcast([P, SG, P]), ALU.mult).then_inc(v_kbd, 1)

            def latents(b, t):
                dve.wait_ge(a_ht, 2 * b + t + 1)
                src = bank[1 - t][:].rearrange("p (k n) -> p k n", k=KC)
                cols = slice(t * P, (t + 1) * P)
                if t == 0:
                    lo(HTl[:, :, cols], src, HTh[:, :, cols]).then_inc(v_htl, 1)
                else:
                    lo(HTl[:, 0:2, cols], src[:, 0:2, :], HTh[:, 0:2, cols]).then_inc(v_htl_half, 1)
                    lo(HTl[:, 2:4, cols], src[:, 2:4, :], HTh[:, 2:4, cols]).then_inc(v_htl, 1)

            def cross_values_lo(b, t):
                dve.wait_ge(a_kvp, 4 * b + 3 * t + 1)
                lo(KVst[:, :, 3 * KEYS + t * P:3 * KEYS + (t + 1) * P],
                   bank[VBANK[t]][:].rearrange("p (g n) -> p g n", g=XKV),
                   KVst[:, :, 2 * KEYS + t * P:2 * KEYS + (t + 1) * P]).then_inc(v_kvl, 1)

            def cross_keys_lo(b, n):
                dve.wait_ge(a_kvp, 4 * b + n + 2)
                lo(KVst[:, 2 * n:2 * n + 2, KEYS:2 * KEYS], bank[6 + n][:].rearrange("p (g n) -> p g n", g=2),
                   KVst[:, 2 * n:2 * n + 2, 0:KEYS]).then_inc(v_kvl, 1)

            def maxima(b, j):
                dve.wait_ge(pe_s, SKV * b + j + 1)
                hs = slice(SG * j, SG * j + SG)
                dve.tensor_reduce(a_max[:, hs], bank[2 + j % 3][:].rearrange("p (c k) -> p c k", c=SG), AX.X,
                                  ALU.max).then_inc(v_mx, 1)
                dve.wait_ge(v_mx, SKV * b + j + 1)
                dve.tensor_scalar(a_nb[:, hs], a_max[:, hs], -S_SCALE, None, ALU.mult).then_inc(v_nb, 1)

            def reciprocals_a(b, j):
                dve.wait_ge(a_exp, SKV * b + j + 1)
                hs = slice(SG * j, SG * j + SG)
                dve.reciprocal(a_rec[:, hs], a_sum[:, hs]).then_inc(v_rec, 1)

            def batch(b, last, stats_ahead):
                for j in range(SKV):
                    if j + 3 < SKV:
                        maxima(b, j + 3)
                    dve.wait_ge(a_pt, SKV * b + j + 1)
                    if j < SKV - 1:
                        lo(PTal[:, j % 2, :], bank[5 + j % 2][:], PTah[:, j % 2, :]).then_inc(v_ptl, 1)
                    else:
                        for n, done in enumerate((v_ptl_half, v_ptl)):
                            cols = slice(n * KEYS, (n + 1) * KEYS)
                            lo(PTal[:, j % 2, cols], bank[5 + j % 2][:, cols], PTah[:, j % 2, cols]).then_inc(done, 1)
                    if j == 0 and not last:
                        ln1(b + 1)
                    if 3 <= j + 2 < SKV:
                        reciprocals_a(b, j + 2)
                    if j == 1:
                        latents(b, 0)
                    if last:
                        continue
                    if j == 2:
                        ln1_lo(b + 1)
                    if j == 5:
                        rope_q(b + 1, rope_q1, rope_q2, q_rot)
                    if j == 6:
                        rope_k(b + 1, rope_k1, rope_k2)
                dve.wait_ge(a_o, b + 1)
                for n, done in enumerate((v_ol_half, v_ol)):
                    cols = slice(n * KEYS, (n + 1) * KEYS)
                    lo(OTl[:, cols], bank[7][:, cols], OTh[:, cols]).then_inc(done, 1)
                if not last:
                    qk_lo(b + 1)
                    diagonal_keys(b + 1, (0, 1))
                    values_lo(b + 1)
                dve.wait_ge(pe_wo, b + 1)
                dve.tensor_tensor(x_res[:, b, :], x_res[:, b, :], bank[6][:], ALU.add).then_inc(v_x2, 1)
                norm_stats(x_res[:, b, :], v_st2)
                dve.wait_ge(g_rstd, b + 1)
                dve.tensor_scalar(xn2[:], x_res[:, b, :], mv[:, 0:1], rstd[:], ALU.subtract,
                                  ALU.mult).then_inc(v_xn2, 1)
                cross_values_lo(b, 0)
                latents(b, 1)
                if not last:
                    maxima(b + 1, 0)
                    maxima(b + 1, 1)
                    maxima(b + 1, 2)
                    diagonal_keys(b + 1, (2, 3))
                    reciprocals_a(b + 1, 0)
                    reciprocals_a(b + 1, 1)
                cross_keys_lo(b, 0)
                if stats_ahead:
                    ln1_stats(b + 2)
                cross_keys_lo(b, 1)
                if not last:
                    reciprocals_a(b + 1, 2)
                cross_values_lo(b, 1)

            dve.sem_inc(v_kvl, 4)
            dve.wait_ge(ld_x0, 16)
            ln1_stats(0)
            ln1(0)
            for n in range(4):
                weight_a(n)
            ln1_lo(0)
            for n in range(4, 6):
                weight_a(n)
            dve.wait_ge(ld_rope, 16)
            rope_q(0, Pa[:, 0, :], Pa[:, 1, :], q_first[:].rearrange("p m n -> p (m n)"))
            rope_k(0, Pa[:, 2, 0:P], Pa[:, 2, P:2 * P])
            qk_lo(0)
            dve.wait_ge(g_const, 6 + 2 * SD)
            diagonal_keys(0, (0, 1))
            weight_a(6)
            maxima(0, 0)
            weight_a(7)
            maxima(0, 1)
            weight_a(8)
            reciprocals_a(0, 0)
            maxima(0, 2)
            weight_a(9)
            reciprocals_a(0, 1)
            values_lo(0)
            reciprocals_a(0, 2)
            diagonal_keys(0, (2, 3))
            dve.wait_ge(ld_x, 16)
            ln1_stats(1)
            with dve.Fori(0, NB - 2) as b:
                batch(b, False, True)
            batch(NB - 2, False, False)
            batch(NB - 1, True, False)

            def maxima_b(g, k):
                dve.wait_ge(b_pe_s, DUOS * g + k + 1)
                dve.tensor_reduce(b_max[:, k % 4, :], bank[k % 3][:].rearrange("p (h k) -> p h k", h=2), AX.X,
                                  ALU.max).then_inc(b_v_mx, 1)
                dve.wait_ge(b_v_mx, DUOS * g + k + 1)
                dve.tensor_scalar(b_nb[:, k % 4, :], b_max[:, k % 4, :], -X_SCALE, None, ALU.mult).then_inc(b_v_nb, 1)

            def reciprocals(g, k):
                dve.wait_ge(b_a_exp, DUOS * g + k + 1)
                dve.reciprocal(b_rec[:, k % 4, :], b_sum[:, k % 4, :]).then_inc(b_v_rec, 1)

            def queries(count, fill, parity, bk=6):
                dve.wait_ge(b_a_q, count)
                lo(Ql[:, parity, 2 * fill:2 * fill + 2, :], bank[bk][:].rearrange("p (h n) -> p h n", h=2),
                   Qh[:, parity, 2 * fill:2 * fill + 2, :]).then_inc(b_v_q, 1)

            def residual(g, b):
                dve.wait_ge(b_pe_wo, PB * NB * g + PB * b + PB + 1)
                dve.tensor_tensor(x_res[:, b, :], x_res[:, b, :], bank[7][:], ALU.add).then_inc(b_v_x, 1)

            dve.memset(f32(GTh[:]), 0.0).then_inc(c_v_g0, 1)
            dve.memset(f32(GTl[:]), 0.0).then_inc(c_v_g0, 1)
            dve.wait_ge(c_v_g0, 2)
            dve.sem_inc(b_v_pt, 2)
            dve.sem_inc(b_v_o, 1)
            dve.sem_inc(b_v_x, 1)

            def ln3(c, t, n):
                dve.wait_ge(c_g_r, n)
                dve.tensor_scalar(xn3[:, t, :], x_res[:, 2 * c + t, :], mv[:, 0:1], rstd[:], ALU.subtract,
                                  ALU.mult).then_inc(c_v_xn, 1)

            def x3_lo(c):
                for t in range(2):
                    dve.wait_ge(c_a_x, 2 * c + t + 1)
                    lo(X3l[:, :, t * P:(t + 1) * P], bank[2 + t][:].rearrange("p (k n) -> p k n", k=KC),
                       X3h[:, :, t * P:(t + 1) * P]).then_inc(c_v_x, 1)

            for f in range(4):
                queries(f + 1, f, 0, QBANK[f])
            for k in range(2):
                maxima_b(0, k)
            for k in range(2):
                reciprocals(0, k)
            dve.wait_ge(c_a_g, 1)
            lo(GTl[:, :, 0:NE], gate_raw[:], GTh[:, :, 0:NE]).then_inc(c_v_g0, 1)

            def outputs(g, k):
                dve.wait_ge(b_a_o, DUOS * g + k + 1)
                b, i = k // PB, k % PB
                lo(Ol[:, b % 2, 2 * i:2 * i + 2, :], bank[5][:, 0:KEYS].rearrange("p (h n) -> p h n", h=2),
                   Oh[:, b % 2, 2 * i:2 * i + 2, :]).then_inc(b_v_o, 1)

            def group(g, last):
                for k in range(DUOS):
                    gg, kk = (g, k + 2) if k + 2 < DUOS else (g + 1, k + 2 - DUOS)
                    ahead = k + 2 < DUOS or not last
                    if ahead:
                        maxima_b(gg, kk)
                    dve.wait_ge(b_a_pt, DUOS * g + k + 1)
                    lo(PTl[:, k % 2, :], bank[3 + k % 2][:], PTh[:, k % 2, :]).then_inc(b_v_pt, 1)
                    if ahead:
                        reciprocals(gg, kk)
                    if k >= PB and k % PB == PB - 1:
                        residual(g, k // PB - 1)
                    if k % 2 == 1 and (k < DUOS - XG or not last):
                        queries(4 + 16 * g + k // 2 + 1, (k % XG) // 2, (k // XG + 1) % 2)
                    if k:
                        outputs(g, k - 1)
                    if last:
                        if k - 2 in LN3_STEPS:
                            ln3(0, LN3_STEPS.index(k - 2), LN3_STEPS.index(k - 2) + 1)
                        if k in LN3_STEPS:
                            norm_stats(x_res[:, LN3_STEPS.index(k), :], c_v_st)
                outputs(g, DUOS - 1)
                if last:
                    x3_lo(0)
                residual(g, NB - 1)

            with dve.Fori(0, XKV - 1) as g:
                group(g, False)
            group(XKV - 1, True)

            def pair(c, last):
                dve.wait_ge(c_a_l, 2 * c + 1)
                lo(LTl[:].rearrange("p m n -> p (m n)"), bank[1][:],
                   LTh[:].rearrange("p m n -> p (m n)")).then_inc(c_v_l, 1)
                for n in range(IC // 2):
                    dve.wait_ge(c_a_hr, 4 * c + n + 1)
                    dve.scalar_tensor_tensor(out=hq[:, n % 2, :], in0=bank[2 + n][:], scalar=0.0, in1=hr[:, n % 2, :],
                                             op0=ALU.max, op1=ALU.mult).then_inc(c_v_h2, 1)
                    if n == 2:
                        dve.wait_ge(c_a_l, 2 * c + 2)
                        lo(ETl[:].rearrange("p m n -> p (m n)"), bank[1][:],
                           ETh[:].rearrange("p m n -> p (m n)")).then_inc(c_v_l, 1)
                    dve.wait_ge(c_a_h, 4 * c + n + 1)
                    lo(HBl[:, 2 * n:2 * n + 2, :].rearrange("p m n -> p (m n)"), hq[:, n % 2, :],
                       HBh[:, 2 * n:2 * n + 2, :].rearrange("p m n -> p (m n)")).then_inc(c_v_h, 1)
                    if n == 1:
                        dve.wait_ge(c_pe_gt, c + 1)
                        dve.tensor_copy(logits[:], bank[0][:, KEYS:2 * KEYS].rearrange(
                            "p (t n) -> p t n", t=2)[:, :, 0:NE])
                        dve.drain()
                        for t in range(2):
                            dve.max(top8[:, t, :], logits[:, t, :])
                        dve.drain()
                        dve.tensor_tensor(route[:], top8[:, :, 0], top8[:, :, 1], ALU.add).then_inc(c_v_r, 1)
                    if not last and n in (0, 2):
                        norm_stats(x_res[:, 2 * c + 2 + n // 2, :], c_v_st)
                        ln3(c + 1, n // 2, 4 * c + 3 + n // 2)
                for t in range(2):
                    dve.wait_ge(c_pe_y, 4 * c + 1 + t)
                    dve.tensor_scalar(yr[:, t, :], bank[t][:], route[:, t:t + 1], None, ALU.mult).then_inc(c_v_y, 1)
                if not last:
                    x3_lo(c + 1)
                for t in range(2):
                    dve.wait_ge(c_pe_y, 4 * c + 3 + t)
                    dve.wait_ge(c_v_y, 2 * c + 3 + t)
                    dve.tensor_tensor(yy[:, t, :], yr[:, t, :], bank[6 + t][:], ALU.add)
                    norm_stats(yy[:, t, :], c_v_st)
                    dve.wait_ge(c_g_r, 4 * c + t + (3 if last else 5))
                    dve.scalar_tensor_tensor(out=yy[:, t, :], in0=yy[:, t, :], scalar=mv[:, 0:1], in1=gam[:],
                                             op0=ALU.subtract, op1=ALU.mult).then_inc(c_v_n, 1)
                    dve.wait_ge(c_v_n, 6 * c + 3 * t + 7)
                    dve.wait_ge(c_g_xb, 2 * c + t + 1)
                    dve.wait_ge(c_out[t], 16 * c + 16)
                    dve.scalar_tensor_tensor(out=yo[:, t, :], in0=yy[:, t, :], scalar=rstd[:], in1=xb[:, t, :],
                                             op0=ALU.mult, op1=ALU.add).then_inc(c_v_n, 2)

            dve.sem_inc(c_v_y, 2)
            dve.sem_inc(c_v_n, 6)
            with dve.Fori(0, NB // 2 - 1) as c:
                pair(c, False)
            pair(NB // 2 - 1, True)


def rope_tables():
    f = np.float32
    inv = (f(1.0) / np.power(f(500000.0), np.arange(0, SD, 2, dtype=np.float32) / f(SD))).astype(f)
    wavelen = (f(2.0 * np.pi) / inv).astype(f)
    lo, hi, factor, ctx = f(1.0), f(4.0), f(32.0), f(1024)
    freq = np.where(wavelen > ctx / lo, inv / factor, inv).astype(f)
    smooth = ((ctx / wavelen - lo) / (hi - lo)).astype(f)
    smoothed = ((f(1.0) - smooth) * freq / factor + smooth * freq).astype(f)
    medium = ~(wavelen < ctx / lo) & ~(wavelen > ctx / hi)
    freq = np.where(medium, smoothed, freq).astype(f)
    ang = (np.arange(P, dtype=np.float32)[:, None] * freq[None, :]).astype(f)
    cos, sin = np.cos(ang), np.sin(ang)
    return np.concatenate([cos, cos, -sin, sin], axis=1).astype(f)


_INS = ["x", "ctx_4096", "L0_attn_Wq", "L0_attn_Wk", "L0_attn_Wv", "L0_attn_Wo", "L0_xattn_Wq", "L0_xattn_Wk",
        "L0_xattn_Wv", "L0_xattn_Wo", "L0_ffn_gate_w", "L0_ffn_up_w", "L0_ffn_down_w", "L0_ffn_fc1_w",
        "L0_ffn_fc2_w", "L0_ffn_expert_w", "L0_ffn_ln_gamma", "L0_ffn_ln_beta"]


def kernel(**inputs):
    import numpy as _np
    import concourse.bacc as _bacc
    from concourse import mybir as _mybir
    from concourse.bass_utils import run_bass_kernel_spmd as _run

    nc = _bacc.Bacc("TRN2", target_bir_lowering=False, num_devices=1)
    arrays, args = {}, []
    for name in _INS:
        a = _np.ascontiguousarray(inputs[name])
        arrays[f"in_{name}_dram"] = a
        args.append(nc.dram_tensor(f"in_{name}_dram", a.shape, _mybir.dt.from_np(a.dtype), kind="ExternalInput").ap())
    table = rope_tables()
    arrays["rope_dram"] = table
    args.append(nc.dram_tensor("rope_dram", table.shape, _mybir.dt.from_np(table.dtype), kind="ExternalInput").ap())
    args.append(nc.dram_tensor("out_0_dram", (NB, P, D), F32, kind="ExternalOutput").ap())
    decoder_layer(nc, *args)
    r = _run(nc, [arrays], core_ids=[0])
    return r.results[0]["out_0_dram"]
```
